# Optimizing a Trainium2 kernel written in Bass

```python
import numpy as np
import jax
import jax.numpy as jnp

def _softmax(x, axis=-1):
    return jax.nn.softmax(x, axis=axis)

def _gelu(x):
    return jax.nn.gelu(x, approximate=True)

def _silu(x):
    return jax.nn.silu(x)

def _sigmoid(x):
    return jax.nn.sigmoid(x)

def _layernorm(x, axis=-1, eps=1e-05):
    m = jnp.mean(x, axis=axis, keepdims=True)
    v = jnp.var(x, axis=axis, keepdims=True)
    return (x - m) / jnp.sqrt(v + eps)

def _scatter_add(tgt, idx, src, axis=0):
    return tgt.at[idx].add(src)

def _segment_sum(src, seg, n):
    return jax.ops.segment_sum(src, seg, n)
kernel_name = 'mk_gnn_preln_d4_gnn_r32_f91dd7'

def setup_inputs(seed: int=0):
    np.random.seed(seed)
    _w = jnp.asarray

    def _rec_inputs():
        import jax
        import jax.numpy as jnp
        _gk = jax.random.key(seed)
        x = -6.415e-05 + 1 * jax.random.normal(jax.random.fold_in(_gk, 1), (10000, 512), jnp.float32)
        _s = jax.random.randint(jax.random.fold_in(_gk, 2), (5000,), 0, 10000, jnp.int32)
        _d = jax.random.randint(jax.random.fold_in(_gk, 3), (5000,), 0, 10000, jnp.int32)
        _loop = jnp.arange(10000, dtype=jnp.int32)
        src = jnp.concatenate([_s, _d, _loop])
        dst = jnp.concatenate([_d, _s, _loop])
        _o = jnp.argsort(dst, stable=True)
        src = src[_o]
        dst = dst[_o]
        return (x, src, dst)
    x, src, dst = _rec_inputs()

    def _L0_gnn_setup():
        import jax, jax.numpy as jnp
        import numpy as np
        N_NODES = 625
        N_EDGES = 10000
        D = 512
        L = 3
        key = jax.random.key(seed)
        ks = jax.random.split(key, 6)
        x = jax.random.normal(ks[0], (N_NODES, D), dtype=jnp.float32)
        Ws_self = jax.random.normal(ks[1], (L, D, D), dtype=jnp.float32) * 0.05
        Ws_neigh = jax.random.normal(ks[2], (L, D, D), dtype=jnp.float32) * 0.05
        bs = jax.random.normal(ks[3], (L, D), dtype=jnp.float32) * 0.05
        src = jax.random.randint(ks[4], (N_EDGES,), 0, N_NODES, dtype=jnp.int64)
        dst = jax.random.randint(ks[5], (N_EDGES,), 0, N_NODES, dtype=jnp.int64)
        return {'x': x, 'Ws_self': Ws_self, 'Ws_neigh': Ws_neigh, 'bs': bs, 'src': src, 'dst': dst}
    _L0_gnn_all = _L0_gnn_setup()
    _L0_gnn_in = {k: v for k, v in _L0_gnn_all.items() if k in ('Ws_self', 'Ws_neigh', 'bs')}
    del _L0_gnn_all

    def _L1_gnn_setup():
        import jax, jax.numpy as jnp
        import numpy as np
        EPS = 1e-07

        def _logmap0(x):
            n = jnp.linalg.norm(x, axis=-1, keepdims=True)
            n = jnp.clip(n, EPS, 1.0 - EPS)
            return jnp.arctanh(n) * x / n

        def _expmap0(v):
            n = jnp.maximum(jnp.linalg.norm(v, axis=-1, keepdims=True), EPS)
            return jnp.tanh(n) * v / n
        N, E, DIN, DOUT = (3125, 31250, 512, 512)
        key = jax.random.key(seed)
        k1, k2, k3, k4, k5, k6 = jax.random.split(key, 6)
        g = jax.random.normal(k1, (N, DIN), jnp.float32)
        r = 0.9 * jax.random.uniform(k2, (N, 1), jnp.float32)
        x = g / jnp.maximum(jnp.linalg.norm(g, axis=-1, keepdims=True), 1e-06) * r
        src = jax.random.randint(k3, (E,), 0, N)
        dst = jax.random.randint(k4, (E,), 0, N)
        W = jax.random.normal(k5, (DOUT, DIN), jnp.float32) / np.sqrt(DIN).astype(np.float32)
        b = jax.random.normal(k6, (DOUT,), jnp.float32) * 0.01
        return {'x': x, 'src': src, 'dst': dst, 'W': W, 'b': b}
    _L1_gnn_all = _L1_gnn_setup()
    _L1_gnn_in = {k: v for k, v in _L1_gnn_all.items() if k in ('W', 'b')}
    del _L1_gnn_all

    def _L2_gnn_setup():
        import jax, jax.numpy as jnp
        import numpy as np
        N = 50000
        IN_CH = 512
        OUT_CH = 512
        DEG = 32
        E = N * DEG
        key = jax.random.key(seed)
        kx, kwc, kwn, kb, ke = jax.random.split(key, 5)
        x = jax.random.normal(kx, (N, IN_CH), dtype=jnp.float32)
        bound = 1.0 / np.sqrt(IN_CH)
        wc = jax.random.uniform(kwc, (IN_CH, OUT_CH), minval=-bound, maxval=bound, dtype=jnp.float32)
        wn = jax.random.uniform(kwn, (IN_CH, OUT_CH), minval=-bound, maxval=bound, dtype=jnp.float32)
        bias = jax.random.uniform(kb, (OUT_CH,), minval=-bound, maxval=bound, dtype=jnp.float32)
        src = jnp.repeat(jnp.arange(N, dtype=jnp.int64), DEG)
        dst = jax.random.randint(ke, (E,), 0, N, dtype=jnp.int64)
        edge_index = jnp.stack([src, dst], axis=0)
        return {'x': x, 'wc': wc, 'wn': wn, 'bias': bias, 'edge_index': edge_index}
    _L2_gnn_all = _L2_gnn_setup()
    _L2_gnn_in = {k: v for k, v in _L2_gnn_all.items() if k in ('wc', 'wn', 'bias')}
    del _L2_gnn_all

    def _L3_gnn_setup():
        import jax, jax.numpy as jnp
        import numpy as np
        N, E, D, H = (10000, 5000, 512, 8)
        C = D // H
        key = jax.random.key(seed)
        ks = jax.random.split(key, 5)
        x = jax.random.normal(ks[0], (N, D), dtype=jnp.float32)
        edge_index = jax.random.randint(ks[1], (2, E), 0, N, dtype=jnp.int64 if jax.config.jax_enable_x64 else jnp.int32)
        scale = 1.0 / np.sqrt(D).astype(np.float32)
        W_l = jax.random.normal(ks[2], (D, D), dtype=jnp.float32) * scale
        W_r = jax.random.normal(ks[3], (D, D), dtype=jnp.float32) * scale
        att = jax.random.normal(ks[4], (H, C), dtype=jnp.float32) * np.float32(1.0 / np.sqrt(C))
        bias = jnp.zeros((D,), dtype=jnp.float32)
        return {'x': x, 'edge_index': edge_index, 'W_l': W_l, 'W_r': W_r, 'att': att, 'bias': bias}
    _L3_gnn_all = _L3_gnn_setup()
    _L3_gnn_in = {k: v for k, v in _L3_gnn_all.items() if k in ('W_l', 'W_r', 'att', 'bias')}
    del _L3_gnn_all
    return {'x': x, 'src': src, 'dst': dst, 'L0_gnn_Ws_self': _L0_gnn_in['Ws_self'], 'L0_gnn_Ws_neigh': _L0_gnn_in['Ws_neigh'], 'L0_gnn_bs': _L0_gnn_in['bs'], 'L1_gnn_W': _L1_gnn_in['W'], 'L1_gnn_b': _L1_gnn_in['b'], 'L2_gnn_wc': _L2_gnn_in['wc'], 'L2_gnn_wn': _L2_gnn_in['wn'], 'L2_gnn_bias': _L2_gnn_in['bias'], 'L3_gnn_W_l': _L3_gnn_in['W_l'], 'L3_gnn_W_r': _L3_gnn_in['W_r'], 'L3_gnn_att': _L3_gnn_in['att'], 'L3_gnn_bias': _L3_gnn_in['bias']}

def reference(x, src, dst, L0_gnn_Ws_self, L0_gnn_Ws_neigh, L0_gnn_bs, L1_gnn_W, L1_gnn_b, L2_gnn_wc, L2_gnn_wn, L2_gnn_bias, L3_gnn_W_l, L3_gnn_W_r, L3_gnn_att, L3_gnn_bias):
    import jax
    import jax.numpy as jnp

    def _L0_gnn_ref(x, Ws_self, Ws_neigh, bs, src, dst):
        import jax, jax.numpy as jnp
        import numpy as np
        N_NODES = 625
        N_EDGES = 10000
        D = 512
        L = 3
        n = x.shape[0]
        deg = jax.ops.segment_sum(jnp.ones_like(dst, dtype=x.dtype), dst, num_segments=n)
        inv_deg = (1.0 / jnp.clip(deg, 1.0))[:, None]
        h = x
        n_layers = Ws_self.shape[0]
        for l in range(n_layers):
            neigh = jax.ops.segment_sum(h[src], dst, num_segments=n) * inv_deg
            h = h @ Ws_self[l] + neigh @ Ws_neigh[l] + bs[l]
            if l != n_layers - 1:
                h = jax.nn.relu(h)
        return h

    def _L1_gnn_ref(x, src, dst, W, b):
        import jax, jax.numpy as jnp
        import numpy as np
        EPS = 1e-07

        def _logmap0(x):
            n = jnp.linalg.norm(x, axis=-1, keepdims=True)
            n = jnp.clip(n, EPS, 1.0 - EPS)
            return jnp.arctanh(n) * x / n

        def _expmap0(v):
            n = jnp.maximum(jnp.linalg.norm(v, axis=-1, keepdims=True), EPS)
            return jnp.tanh(n) * v / n
        N = x.shape[0]
        tangent = _logmap0(x)
        h = tangent @ W.T + b
        sums = jax.ops.segment_sum(h[src], dst, num_segments=N)
        deg = jax.ops.segment_sum(jnp.ones_like(dst, dtype=h.dtype), dst, num_segments=N)
        neigh = sums / jnp.maximum(deg, 1.0)[:, None]
        return _expmap0(neigh)

    def _L2_gnn_ref(x, wc, wn, bias, edge_index):
        import jax, jax.numpy as jnp
        import numpy as np
        N = 50000
        IN_CH = 512
        OUT_CH = 512
        DEG = 32
        E = N * DEG
        alpha = x @ wc
        beta = x @ wn
        src, dst = (edge_index[0], edge_index[1])
        sums = jax.ops.segment_sum(beta[dst], src, num_segments=x.shape[0])
        counts = jax.ops.segment_sum(jnp.ones_like(src, dtype=beta.dtype), src, num_segments=x.shape[0])
        gamma = sums / counts[:, None]
        return alpha + gamma + bias

    def _L3_gnn_ref(x, edge_index, W_l, W_r, att, bias):
        import jax, jax.numpy as jnp
        import numpy as np
        N, E, D, H = (10000, 5000, 512, 8)
        C = D // H
        n = x.shape[0]
        self_idx = jnp.arange(n, dtype=edge_index.dtype)
        src = jnp.concatenate([edge_index[0], self_idx])
        dst = jnp.concatenate([edge_index[1], self_idx])
        x_l = (x @ W_l).reshape(n, H, C)
        x_r = (x @ W_r).reshape(n, H, C)
        m = jax.nn.leaky_relu(x_l[src] + x_r[dst], negative_slope=0.2)
        alpha = jnp.einsum('ehc,hc->eh', m, att)
        amax = jax.lax.stop_gradient(jax.ops.segment_max(alpha, dst, num_segments=n))
        ea = jnp.exp(alpha - amax[dst])
        denom = jax.ops.segment_sum(ea, dst, num_segments=n)
        w = ea / jnp.maximum(denom[dst], 1e-16)
        out = jax.ops.segment_sum(w[:, :, None] * x_l[src], dst, num_segments=n)
        out = out.reshape(n, H * C) + bias
        return jax.nn.elu(out) + x
    edge_index = jnp.stack([src, dst])
    h = jnp.maximum(_layernorm(x, axis=-1), 0.0)
    x = x + _L0_gnn_ref(h, L0_gnn_Ws_self, L0_gnn_Ws_neigh, L0_gnn_bs, src, dst)
    h = jnp.maximum(_layernorm(x, axis=-1), 0.0)
    x = x + _L1_gnn_ref(h, src, dst, L1_gnn_W, L1_gnn_b)
    h = jnp.maximum(_layernorm(x, axis=-1), 0.0)
    x = x + _L2_gnn_ref(h, L2_gnn_wc, L2_gnn_wn, L2_gnn_bias, edge_index)
    h = jnp.maximum(_layernorm(x, axis=-1), 0.0)
    x = x + _L3_gnn_ref(h, edge_index, L3_gnn_W_l, L3_gnn_W_r, L3_gnn_att, L3_gnn_bias)
    return x

_drawn_inputs = setup_inputs


def setup_inputs(seed=0):
    import zlib

    import numpy as np

    out = dict(_drawn_inputs(seed))
    spreads = {'L3_gnn_bias': (0.0, 0.1)}
    factors = {'L1_gnn_b': 8.0, 'L2_gnn_bias': 4.157, 'L3_gnn_W_r': 8.0, 'L3_gnn_att': 3.736}
    for name, (base, spread) in spreads.items():
        noise = np.random.default_rng([zlib.crc32(name.encode()), seed]).standard_normal(out[name].shape)
        drawn = base * np.exp(spread * noise) if base else spread * noise
        out[name] = jnp.asarray(drawn.astype(out[name].dtype))
    for name, factor in factors.items():
        out[name] = (out[name] * factor).astype(out[name].dtype)
    return out
```

```python
import concourse.bass as bass
from concourse import mybir
from contextlib import ExitStack

P = 128
D = 512
N_NODES = 10000
N_EDGES = 20000
HEADS = 8
HEAD_DIM = D // HEADS
UNROLL = 4
N_TILES = -(-N_NODES // (P * UNROLL)) * UNROLL
N_PAD = N_TILES * P
EDGES = P - 1
N_CHUNKS = -(-(N_EDGES + N_PAD - N_NODES) // (EDGES * UNROLL)) * UNROLL
E_PAD = N_CHUNKS * EDGES
HALF = N_CHUNKS // 2
BANK = 512
KT = D // P
SKIP = float(1 << 20)
W_SCALE = 256.0
EPS_LN = 1e-5
EPS_HYP = 1e-7
CLIP_HYP = 1.0 - 1e-7
LOW = -1e30


class Signal:

    def __init__(self, handle):
        self.handle = handle
        self.base = 0

    def after(self, n):
        return self.base + n

    def passed(self, n):
        self.base += n


def pipelined(eng, n, steps, unroll=UNROLL, end=0):
    rounds = n // unroll

    def body(i, j):
        for lag, step in steps:
            s, back = (j - lag) % unroll, (j - lag) // unroll
            if type(i) is int and not 0 <= i + back < rounds:
                continue
            step((i + back) * unroll + s, s, i + back)

    for i in (0, 1):
        for j in range(unroll):
            body(i, j)
    with eng.Fori(2, rounds - end) as i:
        for j in range(unroll):
            body(i, j)
    for i in range(rounds - end, rounds + 1 + (max(lag for lag, _ in steps) - 1) // unroll):
        for j in range(unroll):
            body(i, j)


def wait_apart(eng, step_sem, *waits):
    for sem, value in waits:
        eng.wait_ge(sem, value)
    eng.sem_inc(step_sem, 1)


def gnn_program(nc, x, src_list, dst_list, Ws_self, Ws_neigh, bs, W1, b1, wc, wn, b2, W_l, W_r, att, b3,
                out, dram):
    f32, f16, i32 = mybir.dt.float32, mybir.dt.float16, mybir.dt.int32
    ACT, ALU, AX = mybir.ActivationFunctionType, mybir.AluOpType, mybir.AxisListType

    def later(t, depth):
        return type(t) is not int or t >= depth

    Z = dram("Z", (N_PAD, 2 * D), f16)
    U = dram("U", (N_PAD, D), f32)
    HT = dram("HT", (N_TILES, P, 2 * D), f16)
    X1 = dram("X1", (N_PAD, D), f32)
    X2 = dram("X2", (N_PAD, D), f32)
    AGG_D = dram("AGG_D", (N_PAD, D), f32)
    AGG_S = dram("AGG_S", (N_PAD, D), f32)
    AGG_A = dram("AGG_A", (N_PAD, D + 2 * HEADS), f32)
    XL = dram("XL", (N_PAD, D), f32)
    XR = dram("XR", (N_PAD, D), f32)
    XH = dram("XH", (N_PAD, D), f32)
    SORTED = dram("SORTED", (E_PAD + 2, 2), i32)
    IDX_D = dram("IDX_D", (P, N_CHUNKS * 3), i32)
    IDX_S = dram("IDX_S", (P, N_CHUNKS * 3), i32)

    ctx = ExitStack()
    with ctx:
        made = {}

        def sb(name, shape, dt, where=ctx):
            made[name] = made.get(name, 0) + 1
            if made[name] > 1:
                name = f"{name}_{made[name]}"
            return where.enter_context(nc.sbuf_tensor(name, shape, dt))

        def signal(name):
            return Signal(ctx.enter_context(nc.semaphore(name)))

        ident = sb("ident", [P, P], f32)
        ident16 = sb("ident16", [P, P], f16)
        pick = sb("pick", [P, P], f32)
        ones = sb("ones", [P, P], f32)
        below = sb("below", [P, P], f32)
        earlier = sb("earlier", [P, P], f32)
        lane_row = sb("lane_row", [P, P], f32)
        tile_row = sb("tile_row", [P, N_TILES], f32)
        skip0 = sb("skip0", [P, 1], f32)
        neg_half = sb("neg_half", [P, 1], f32)
        half = sb("half", [P, 1], f32)
        SEL = sb("SEL", [P, N_CHUNKS, P], f16)
        key_col = sb("key_col", [P, N_CHUNKS], f32)
        next_col = sb("next_col", [P, N_CHUNKS], f32)
        val_col = sb("val_col", [P, N_CHUNKS], f32)
        inv_d = sb("inv_d", [P, N_TILES], f32)
        inv_s = sb("inv_s", [P, N_TILES], f32)
        w_own = sb("w_own", [P, 2, KT, D], f16)
        w_out = sb("w_out", [P, 2, KT, D], f16)
        w_out2 = sb("w_out2", [P, 2, KT, D], f16)
        bias_own = sb("bias_own", [P, D], f32)
        bias_out = sb("bias_out", [P, D], f32)
        att_row = sb("att_row", [P, D], f32)
        psum = ctx.enter_context(nc.psum_tensor("psum", [P, 8 * BANK], f32))
        banks = [psum[:, i * BANK:(i + 1) * BANK] for i in range(8)]

        load = [signal(f"load{s}") for s in range(UNROLL)]
        store = [signal(f"store{s}") for s in range(UNROLL)]
        gather = [signal(f"gather{s}") for s in range(UNROLL)]
        gather2 = [signal(f"gather2{s}") for s in range(UNROLL)]
        scatter = [signal(f"scatter{s}") for s in range(UNROLL)]
        index = [signal(f"index{s}") for s in range(2)]
        once = signal("once")
        apart_sp, apart_dve, apart_pool, apart_act = (signal(f"apart{n}").handle for n in range(4))
        names = ("combined", "stats", "aggr", "rstd", "bias_ln", "eps_added", "h_done", "transposed", "hi_done",
                 "lo_done", "product", "out_hi", "out_lo", "out_sum", "squares", "norm", "summed", "carry_hi", "carry_lo",
                 "sums_out", "own_product", "own_out", "v_step", "a_step", "p_step", "t_step",
                 "onehot", "counted", "ranked", "placed", "weighed", "w_hi", "w_lo", "den_out",
                 "diag_done", "keys_row", "sel_done", "based", "looked", "pow_step", "x_step", "y_step")
        sig = {n: signal(n) for n in names}

        def chain(eng, ins, s):
            ins.then_inc(s.handle, 1)
            s.base += 1
            eng.wait_ge(s.handle, s.base)

        def constants():
            with nc.Block() as block:
                @block.gpsimd
                def _(pool):
                    p = sig["p_step"]
                    chain(pool, pool.memset(ones[:], 1.0), p)
                    chain(pool, pool.memset(neg_half[:], -0.5), p)
                    chain(pool, pool.memset(half[:], 0.5), p)
                    chain(pool, pool.affine_select(out=ident[:], in_=ones[:], compare_op=ALU.is_equal, fill=0.0,
                                                   base=0, pattern=[[-1, P]], channel_multiplier=1), p)
                    chain(pool, pool.affine_select(out=below[:], in_=ones[:], compare_op=ALU.is_gt, fill=0.0,
                                                   base=0, pattern=[[1, P]], channel_multiplier=-1), p)
                    chain(pool, pool.affine_select(out=earlier[:], in_=ones[:], compare_op=ALU.is_gt, fill=0.0,
                                                   base=0, pattern=[[-1, P]], channel_multiplier=1), p)
                    chain(pool, pool.memset(earlier[:, 0:1], 0.0), p)
                    chain(pool, pool.tensor_copy(pick[:, 1:P], ident[:, 1:P]), p)
                    chain(pool, pool.tensor_copy(pick[:, 0:1], ident[:, P - 1:P]), p)
                    chain(pool, pool.tensor_copy(ident16[:], ident[:]), p)
                    chain(pool, pool.tensor_scalar(skip0[:], ident[:, 0:1], SKIP, None, ALU.mult), p)
                    chain(pool, pool.iota(lane_row[:], pattern=[[1, P]], base=0, channel_multiplier=0,
                                          allow_small_or_imprecise_dtypes=True), p)
                    chain(pool, pool.iota(tile_row[:], pattern=[[1, N_TILES]], base=0, channel_multiplier=0,
                                          allow_small_or_imprecise_dtypes=True), p)

        def edge_columns(keys_dram, vals_dram, idx_dram):
            with ExitStack() as local:
                rows = sb("edge_rows", [HALF, 2, 2, P + 2], i32, local)
                rowsf = sb("edge_rowsf", [HALF, 2, 2, P + 2], f32, local)
                idx = sb("edge_idx", [P, N_CHUNKS, 3], i32, local)
                same = sb("edge_same", [P, N_CHUNKS], f32, local)
                block = local.enter_context(nc.Block())
                n_loads = 2 if vals_dram is None else 4
                parts = rows.rearrange("p h k e -> p h (k e)").rearrange("p h (e k) -> p h k e", k=2) \
                    if vals_dram is None else rows

                @block.sync
                def _(sp):
                    for h in range(2):
                        if vals_dram is None:
                            sp.dma_start(rows[:, h].rearrange("p k e -> p (k e)")[:, 0:2 * (P + 1)], keys_dram[h])\
                              .then_inc(once.handle, 16)
                        else:
                            sp.dma_start(rows[:, h, 0, 0:P + 1], keys_dram[h]).then_inc(once.handle, 16)
                            sp.dma_start(rows[:, h, 1, 0:P + 1], vals_dram[h]).then_inc(once.handle, 16)
                    wait_apart(sp, apart_sp, (sig["v_step"].handle, sig["v_step"].after(9)))
                    sp.dma_start(idx_dram, idx[:].rearrange("p c k -> p (c k)")).then_inc(once.handle, 16)
                    wait_apart(sp, apart_sp, (once.handle, once.after(16 * (n_loads + 1))))

                @block.tensor
                def _(pe):
                    pe.wait_ge(sig["v_step"].handle, sig["v_step"].after(1))
                    for h in range(2):
                        for k, (which, first) in enumerate(((0, 0), (0, 1), (1, 0))):
                            last = nc.tensor.transpose(banks[k][:, h * HALF:(h + 1) * HALF],
                                                       rowsf[:, h, which, first:first + P], ident[0:HALF, 0:HALF])
                    last.then_inc(sig["t_step"].handle, 1)

                @block.vector
                def _(dve):
                    v = Signal(sig["v_step"].handle)
                    v.base = sig["v_step"].base
                    dve.wait_ge(once.handle, once.after(16 * n_loads))
                    chain(dve, dve.tensor_copy(rowsf[:, :, :, 0:P + 1], parts[:, :, :, 0:P + 1]), v)
                    dve.wait_ge(sig["t_step"].handle, sig["t_step"].after(1))
                    chain(dve, dve.tensor_copy(key_col[:], banks[0][:, 0:N_CHUNKS]), v)
                    chain(dve, dve.tensor_copy(next_col[:], banks[1][:, 0:N_CHUNKS]), v)
                    chain(dve, dve.tensor_copy(val_col[:], banks[2][:, 0:N_CHUNKS]), v)
                    chain(dve, dve.tensor_scalar(idx[:, :, 0], val_col[:], skip0[:, 0:1], None, ALU.add), v)
                    chain(dve, dve.tensor_tensor(same[:], key_col[:], next_col[:], ALU.is_equal), v)
                    chain(dve, dve.scalar_tensor_tensor(same[:], same[:], SKIP, key_col[:], ALU.mult, ALU.add), v)
                    chain(dve, dve.tensor_scalar(idx[:, :, 1], same[:], skip0[:, 0:1], None, ALU.add), v)
                    chain(dve, dve.tensor_scalar(idx[:, :, 2], key_col[:], skip0[:, 0:1], None, ALU.add), v)
            once.passed(16 * (n_loads + 1))
            sig["v_step"].passed(9)
            sig["t_step"].passed(1)

        def select_matrices():
            with ExitStack() as local:
                diag = sb("diag", [P, 2, UNROLL, P], f32, local)
                rounds = N_CHUNKS // UNROLL
                block = local.enter_context(nc.Block())
                dg, kr, sd = sig["diag_done"], sig["keys_row"], sig["sel_done"]

                def body_v(dve, q, half_, b):
                    if later(q, 2):
                        dve.wait_ge(kr.handle, kr.after(q - 1))
                    for j in range(UNROLL):
                        ins = dve.tensor_scalar(diag[:, b, j, :], pick[:], key_col[:, bass.ds(q * UNROLL + j, 1)],
                                                None, ALU.mult)
                    ins.then_inc(dg.handle, 1)

                def body_s(dve, q, half_, b):
                    dve.wait_ge(kr.handle, kr.after(q + 1))
                    for j in range(UNROLL):
                        c = bass.ds(q * UNROLL + j, 1)
                        ins = dve.tensor_scalar(SEL[:, c, :].rearrange("p o m -> p (o m)"), banks[b][:, j * P:(j + 1) * P],
                                                key_col[:, c], None, ALU.is_equal)
                    ins.then_inc(sd.handle, 1)

                @block.vector
                def _(dve):
                    body_v(dve, 0, 0, 0)
                    body_v(dve, 1, 0, 1)
                    body_s(dve, 0, 0, 0)
                    body_v(dve, 2, 0, 0)
                    body_s(dve, 1, 0, 1)
                    with dve.Fori(1, rounds // 2 - 1) as i:
                        body_v(dve, 2 * i + 1, 0, 1)
                        body_s(dve, 2 * i, 0, 0)
                        body_v(dve, 2 * i + 2, 0, 0)
                        body_s(dve, 2 * i + 1, 0, 1)
                    body_v(dve, rounds - 1, 0, 1)
                    body_s(dve, rounds - 2, 0, 0)
                    body_s(dve, rounds - 1, 0, 1)

                @block.tensor
                def _(pe):
                    def body(q, b):
                        pe.wait_ge(dg.handle, dg.after(q + 1))
                        if later(q, 2):
                            pe.wait_ge(sd.handle, sd.after(q - 1))
                        nc.tensor.matmul(banks[b][:], ones[:], diag[:, b].rearrange("p j m -> p (j m)"),
                                         start=True, stop=True).then_inc(kr.handle, 1)
                    body(0, 0)
                    body(1, 1)
                    with pe.Fori(1, rounds // 2) as i:
                        body(2 * i, 0)
                        body(2 * i + 1, 1)
            for s in (dg, kr, sd):
                s.passed(rounds)

        def count_keys(inverse, clamp, lane_col, tile_col, total):
            with ExitStack() as local:
                key_i = sb("key_i", [P, 2, N_CHUNKS], i32, local)
                lane_hot = sb("lane_hot", [P, UNROLL, P], f16, local)
                tile_hot = sb("tile_hot", [P, UNROLL, N_TILES], f16, local)
                block = local.enter_context(nc.Block())
                hot, cnt, v0 = sig["onehot"], sig["counted"], sig["v_step"]

                @block.vector
                def _(dve):
                    v = Signal(v0.handle)
                    v.base = v0.base
                    chain(dve, dve.tensor_copy(key_i[:, 0, :], key_col[:]), v)
                    chain(dve, dve.tensor_scalar(key_i[:, 1, :], key_i[:, 0, :], P - 1, None, ALU.bitwise_and), v)
                    chain(dve, dve.tensor_copy(lane_col[:], key_i[:, 1, :]), v)
                    chain(dve, dve.tensor_scalar(key_i[:, 1, :], key_i[:, 0, :], 7, None, ALU.arith_shift_right), v)
                    chain(dve, dve.tensor_copy(tile_col[:], key_i[:, 1, :]), v)
                    chain(dve, dve.tensor_scalar(lane_col[:], lane_col[:], skip0[:, 0:1], None, ALU.add), v)

                    def step(c, s, r):
                        if later(c, UNROLL):
                            dve.wait_ge(cnt.handle, cnt.after(c - UNROLL + 1))
                        dve.tensor_scalar(lane_hot[:, s, :], lane_row[:], lane_col[:, bass.ds(c, 1)], None, ALU.is_equal)
                        dve.tensor_scalar(tile_hot[:, s, :], tile_row[:], tile_col[:, bass.ds(c, 1)], None,
                                          ALU.is_equal).then_inc(hot.handle, 1)
                    pipelined(dve, N_CHUNKS, [(0, step)])
                    dve.wait_ge(cnt.handle, cnt.after(N_CHUNKS))
                    chain(dve, dve.tensor_copy(total[:], banks[0][:, 0:N_TILES]), v)
                    if clamp:
                        chain(dve, dve.tensor_scalar(inverse[:], total[:], 1.0, None, ALU.max), v)
                    else:
                        chain(dve, dve.tensor_copy(inverse[:], total[:]), v)
                    chain(dve, dve.reciprocal(inverse[:], inverse[:]), v)

                @block.tensor
                def _(pe):
                    for c in range(N_CHUNKS):
                        s = c % UNROLL
                        pe.wait_ge(hot.handle, hot.after(c + 1))
                        nc.tensor.matmul(banks[0][:, 0:N_TILES], lane_hot[:, s, :], tile_hot[:, s, :],
                                         start=c == 0, stop=c == N_CHUNKS - 1).then_inc(cnt.handle, 1)
            v0.passed(9)
            hot.passed(N_CHUNKS)
            cnt.passed(N_CHUNKS)

        def split_weights(jobs, rows):
            with ExitStack() as local:
                raw = sb("w_raw", [P, len(jobs), KT, D], f32, local)
                block = local.enter_context(nc.Block())
                hi, lo, t = sig["w_hi"], sig["w_lo"], sig["t_step"]
                turned = any(j[2] for j in jobs)
                n_once = len(jobs) + len(rows)

                @block.sync
                def _(sp):
                    for n, (w, _, _) in enumerate(jobs):
                        sp.dma_start(raw[:, n], w.rearrange("(t p) n -> p t n", p=P)).then_inc(once.handle, 16)
                    for row, tile in rows:
                        sp.dma_start(tile[:], row.to_broadcast([P, D])).then_inc(once.handle, 16)
                    wait_apart(sp, apart_sp, (once.handle, once.after(16 * n_once)))

                @block.tensor
                def _(pe):
                    if turned:
                        pe.wait_ge(once.handle, once.after(16 * n_once))
                        for k in range(KT):
                            for m in range(KT):
                                last = nc.tensor.transpose(banks[k][:, m * P:(m + 1) * P],
                                                           raw[:, 0, m, k * P:(k + 1) * P], ident[:])
                        last.then_inc(t.handle, 1)

                @block.scalar
                def _(act):
                    act.wait_ge(once.handle, once.after(16 * n_once))
                    if turned:
                        act.wait_ge(t.handle, t.after(1))
                    for n, (_, w, turn) in enumerate(jobs):
                        for k in range(KT):
                            of = banks[k][:] if turn else raw[:, n, k, :]
                            act.activation(w[:, 0, k, :], of, ACT.Copy, scale=W_SCALE).then_inc(hi.handle, 1)

                @block.vector
                def _(dve):
                    for n, (_, w, turn) in enumerate(jobs):
                        for k in range(KT):
                            of = banks[k][:] if turn else raw[:, n, k, :]
                            dve.wait_ge(hi.handle, hi.after(n * KT + k + 1))
                            dve.scalar_tensor_tensor(w[:, 1, k, :], of, W_SCALE, w[:, 0, k, :], ALU.mult,
                                                     ALU.subtract).then_inc(lo.handle, 1)
            once.passed(16 * n_once)
            hi.passed(KT * len(jobs))
            lo.passed(KT * len(jobs))
            t.passed(1 if turned else 0)

        def products(bank_, left, w, ks, first, last):
            for k in ks:
                for a, b in ((0, 0), (1, 0), (0, 1)):
                    ins = nc.tensor.matmul(bank_[:], left[:, a, k, :], w[:, b, k, :],
                                           start=first and k == ks[0] and (a, b) == (0, 0),
                                           stop=last and k == ks[-1] and (a, b) == (0, 1))
            return ins

        def dense(x_in=None, own=None, agg=None, inverse=None, exp_map=False, norm=True, log_map=False,
                  x_out=None, ht=False, attention=False):
            ins_of = [a for a in (x_in, own, agg) if a is not None]
            nl = len(ins_of)
            z_out = not attention
            ns = (x_out is not None) + ht + (1 if z_out else 3)
            combine = agg is not None
            F = 3 if exp_map else 1 if combine else 0
            L = F + 1
            with ExitStack() as local:
                inX = sb("inX", [P, UNROLL, D], f32, local) if x_in is not None else None
                inU = sb("inU", [P, UNROLL, D], f32, local) if own is not None else None
                inG = sb("inG", [P, UNROLL, D], f32, local) if combine else None
                y = sb("y", [P, UNROLL, D], f32, local) if combine else inX
                part = sb("part", [P, 2, D], f32, local)
                scrap = sb("scrap", [P, 2, D], f32, local)
                h = sb("h", [P, 2, D], f32, local)
                hT = sb("hT", [P, UNROLL, 2, KT, P], f16, local)
                zout = sb("zout", [P, UNROLL, 2, D], f16, local) if z_out else None
                zsum = sb("zsum", [P, 2, D], f32, local) if log_map else None
                xl = sb("xl", [P, UNROLL, D], f32, local) if attention else None
                xr = sb("xr", [P, UNROLL, D], f32, local) if attention else None
                xh = sb("xh", [P, UNROLL, D], f32, local) if attention else None
                six = sb("six", [P, UNROLL, 6], f32, local)
                mv = sb("mv", [P, UNROLL, 2], f32, local)
                small = sb("small", [P, UNROLL, 24], f32, local)
                VAR, RSTD, LNB, SS, NORM, NC_, REC, TANH, FAC = 0, 1, 2, 3, 4, 6, 8, 10, 11
                Q, LNQ, N2, SER, MASK, DIF, ONEP = 12, 13, 14, 15, 16, 17, 18

                def sm(s, k, n=1):
                    return small[:, s, k:k + n]
                block = local.enter_context(nc.Block())
                g = sig
                rows = lambda t: bass.ds(t * P, P)

                @block.sync
                def _(sp):
                    def loads(t, s, r):
                        if later(t, UNROLL):
                            wait_apart(sp, apart_sp, (g["h_done"].handle, g["h_done"].after(t - UNROLL + 1)))
                            if combine:
                                wait_apart(sp, apart_sp, (g["combined"].handle, g["combined"].after(t - UNROLL + 1)))
                            if attention:
                                wait_apart(sp, apart_sp, (g["x_step"].handle, g["x_step"].after(t - UNROLL + 1)))
                        if x_in is not None:
                            sp.dma_start(inX[:, s], x_in[rows(t), :]).then_inc(load[s].handle, 16)
                        if own is not None:
                            sp.dma_start(inU[:, s], own[rows(t), :]).then_inc(load[s].handle, 16)
                        if combine:
                            sp.dma_start(inG[:, s], agg[rows(t), :]).then_inc(load[s].handle, 16)

                    def stores(t, s, r):
                        wait_apart(sp, apart_sp, (g["out_lo"].handle, g["out_lo"].after(t + 1)))
                        if z_out:
                            sp.dma_start(Z[rows(t), :], zout[:, s].rearrange("p a n -> p (a n)")).then_inc(store[s].handle, 16)
                        else:
                            wait_apart(sp, apart_sp, (g["out_hi"].handle, g["out_hi"].after(t + 1)))
                            sp.dma_start(XL[rows(t), :], xl[:, s]).then_inc(store[s].handle, 16)
                            sp.dma_start(XR[rows(t), :], xr[:, s]).then_inc(store[s].handle, 16)
                            wait_apart(sp, apart_sp, (g["x_step"].handle, g["x_step"].after(t + 1)))
                            sp.dma_start(XH[rows(t), :], xh[:, s]).then_inc(store[s].handle, 16)
                        if ht:
                            sp.dma_start(HT[bass.ds(t, 1)].rearrange("o p n -> (o p) n"),
                                         hT[:, s].rearrange("p a k n -> p (a k n)")).then_inc(store[s].handle, 16)
                        if x_out is not None:
                            sp.dma_start(x_out[rows(t), :], y[:, s]).then_inc(store[s].handle, 16)
                    pipelined(sp, N_TILES, [(0, loads), (L + 3, stores)])
                    for s in range(UNROLL):
                        wait_apart(sp, apart_sp, (store[s].handle, store[s].after(16 * ns * N_TILES // UNROLL)))

                @block.vector
                def _(dve):
                    def combination(t, s, r):
                        wait_apart(dve, apart_dve, (load[s].handle, load[s].after((r + 1) * (16 * nl))))
                        if combine and later(t, UNROLL):
                            dve.wait_ge(g["h_done"].handle, g["h_done"].after(t - UNROLL + 1))
                            if x_out is not None:
                                dve.wait_ge(store[s].handle, store[s].after(r * (16 * ns)))
                            if attention:
                                dve.wait_ge(g["x_step"].handle, g["x_step"].after(t - UNROLL + 1))
                        if exp_map:
                            f = g["v_step"]
                            dve.wait_ge(g["norm"].handle, g["norm"].after(t + 1))
                            dve.reciprocal(sm(s, REC), sm(s, NC_)).then_inc(g["y_step"].handle, 1)
                            dve.wait_ge(g["a_step"].handle, g["a_step"].after(t + 1))
                            wait_apart(dve, apart_dve, (g["y_step"].handle, g["y_step"].after(2 * t + 1)))
                            dve.scalar_tensor_tensor(sm(s, FAC), sm(s, TANH), sm(s, REC), inverse[:, bass.ds(t, 1)],
                                                     ALU.mult, ALU.mult).then_inc(g["y_step"].handle, 1)
                            wait_apart(dve, apart_dve, (g["y_step"].handle, g["y_step"].after(2 * t + 2)))
                            dve.scalar_tensor_tensor(y[:, s], inG[:, s], sm(s, FAC), inX[:, s], ALU.mult,
                                                     ALU.add).then_inc(g["combined"].handle, 1)
                        elif combine and x_in is None:
                            wait_apart(dve, apart_dve)
                            dve.scalar_tensor_tensor(y[:, s], inG[:, s], inverse[:, bass.ds(t, 1)], inU[:, s],
                                                     ALU.mult, ALU.add).then_inc(g["combined"].handle, 1)
                        elif combine:
                            wait_apart(dve, apart_dve)
                            dve.scalar_tensor_tensor(part[:, s % 2], inG[:, s], inverse[:, bass.ds(t, 1)], inU[:, s],
                                                     ALU.mult, ALU.add).then_inc(g["y_step"].handle, 1)
                            dve.wait_ge(g["y_step"].handle, g["y_step"].after(t + 1))
                            dve.tensor_tensor(y[:, s], part[:, s % 2], inX[:, s], ALU.add)\
                               .then_inc(g["combined"].handle, 1)
                        if norm:
                            if combine:
                                dve.wait_ge(g["combined"].handle, g["combined"].after(t + 1))
                            dve.bn_stats(six[:, s], y[:, s]).then_inc(g["stats"].handle, 1)
                            wait_apart(dve, apart_dve, (g["stats"].handle, g["stats"].after(t + 1)))
                            dve.bn_aggr(mv[:, s], six[:, s]).then_inc(g["aggr"].handle, 1)

                    def log_factor(t, s, r):
                        v = g["ranked"]
                        dve.wait_ge(g["norm"].handle, g["norm"].after(t + 1))
                        dve.reciprocal(sm(s, REC, 2), sm(s, NC_, 2)).then_inc(v.handle, 1)
                        wait_apart(dve, apart_dve, (v.handle, v.after(4 * t + 1)))
                        dve.tensor_tensor(sm(s, Q), sm(s, REC + 1), sm(s, ONEP), ALU.mult).then_inc(v.handle, 1)

                    def log_factor_end(t, s, r):
                        v = g["ranked"]
                        wait_apart(dve, apart_dve, (g["a_step"].handle, g["a_step"].after(t + 1)))
                        dve.tensor_scalar(sm(s, LNQ), sm(s, LNQ), sm(s, REC), 0.5 / W_SCALE, ALU.mult, ALU.mult).then_inc(v.handle, 1)
                        wait_apart(dve, apart_dve, (v.handle, v.after(4 * t + 3)), (g["placed"].handle, g["placed"].after(t + 1)))
                        dve.scalar_tensor_tensor(sm(s, DIF), sm(s, SER), 1.0 / W_SCALE, sm(s, LNQ), ALU.mult, ALU.subtract).then_inc(v.handle, 1)
                        wait_apart(dve, apart_dve, (v.handle, v.after(4 * t + 4)))
                        dve.scalar_tensor_tensor(sm(s, FAC), sm(s, DIF), sm(s, MASK), sm(s, LNQ), ALU.mult,
                                                 ALU.add).then_inc(g["weighed"].handle, 1)

                    def low(t, s, r):
                        dve.wait_ge(g["hi_done"].handle, g["hi_done"].after(t + 1))
                        dve.tensor_tensor(hT[:, s, 1].rearrange("p k n -> p (k n)"), banks[s % 2][:],
                                          hT[:, s, 0].rearrange("p k n -> p (k n)"), ALU.subtract)\
                           .then_inc(g["lo_done"].handle, 1)

                    def results_sum(t, s, r):
                        dve.wait_ge(g["weighed"].handle, g["weighed"].after(t + 1))
                        dve.wait_ge(g["product"].handle, g["product"].after(t + 1))
                        if later(t, 2):
                            dve.wait_ge(g["out_lo"].handle, g["out_lo"].after(t - 1))
                        dve.scalar_tensor_tensor(zsum[:, s % 2], banks[2 + s % 2][:], sm(s, FAC), bias_out[:], ALU.mult,
                                                 ALU.add).then_inc(g["out_sum"].handle, 1)

                    def results(t, s, r):
                        if log_map:
                            dve.wait_ge(g["out_hi"].handle, g["out_hi"].after(t + 1))
                            dve.tensor_tensor(zout[:, s, 1], zsum[:, s % 2], zout[:, s, 0], ALU.subtract)\
                               .then_inc(g["out_lo"].handle, 1)
                        elif z_out:
                            dve.wait_ge(g["out_hi"].handle, g["out_hi"].after(t + 1))
                            dve.scalar_tensor_tensor(zout[:, s, 1], banks[2 + s % 2][:], 1.0 / W_SCALE, zout[:, s, 0],
                                                     ALU.mult, ALU.subtract).then_inc(g["out_lo"].handle, 1)
                        else:
                            dve.wait_ge(g["product"].handle, g["product"].after(t + 1))
                            if later(t, UNROLL):
                                dve.wait_ge(store[s].handle, store[s].after(r * (16 * ns)))
                            dve.tensor_scalar(xr[:, s], banks[4 + s % 2][:], 1.0 / W_SCALE, None, ALU.mult)\
                               .then_inc(g["out_lo"].handle, 1)
                    steps = [(F, combination), (L + 2, results), (L, low)]
                    if log_map:
                        steps = [(F, combination), (L + 1, log_factor_end), (L + 2, results_sum), (L, low), (L, log_factor),
                                 (L + 2, results)]
                    pipelined(dve, N_TILES, steps)

                @block.gpsimd
                def _(pool):
                    def mean_norm(t, s, r):
                        n = g["pow_step"]
                        wait_apart(pool, apart_pool, (g["squares"].handle, g["squares"].after(t + 1)))
                        pool.tensor_tensor(out=sm(s, NORM), in0=sm(s, SS), in1=half[:], op=ALU.pow).then_inc(n.handle, 1)
                        wait_apart(pool, apart_pool, (n.handle, n.after(t + 1)))
                        pool.tensor_scalar(sm(s, NC_), sm(s, NORM), EPS_HYP, None, ALU.max).then_inc(g["norm"].handle, 1)

                    def ln_scale(t, s, r):
                        wait_apart(pool, apart_pool, (g["aggr"].handle, g["aggr"].after(t + 1)))
                        pool.tensor_scalar(sm(s, VAR), mv[:, s, 1:2], EPS_LN, None, ALU.add)\
                            .then_inc(g["eps_added"].handle, 1)
                        wait_apart(pool, apart_pool, (g["eps_added"].handle, g["eps_added"].after(t + 1)))
                        pool.tensor_tensor(out=sm(s, RSTD), in0=sm(s, VAR), in1=neg_half[:], op=ALU.pow)\
                            .then_inc(g["rstd"].handle, 1)
                        wait_apart(pool, apart_pool, (g["rstd"].handle, g["rstd"].after(t + 1)))
                        pool.tensor_scalar(sm(s, LNB), mv[:, s, 0:1], sm(s, RSTD), -1.0, ALU.mult, ALU.mult)\
                            .then_inc(g["bias_ln"].handle, 1)

                    def clipped_norm(t, s, r):
                        n, m = g["pow_step"], g["p_step"]
                        wait_apart(pool, apart_pool, (g["squares"].handle, g["squares"].after(t + 1)))
                        pool.tensor_tensor(out=sm(s, NORM), in0=sm(s, SS), in1=half[:], op=ALU.pow).then_inc(n.handle, 1)
                        wait_apart(pool, apart_pool, (n.handle, n.after(t + 1)))
                        pool.tensor_scalar(sm(s, NC_), sm(s, NORM), EPS_HYP, CLIP_HYP, ALU.max, ALU.min)\
                            .then_inc(m.handle, 1)
                        wait_apart(pool, apart_pool, (m.handle, m.after(4 * t + 1)))
                        pool.tensor_scalar(sm(s, ONEP), sm(s, NC_), 1.0, None, ALU.add)
                        pool.tensor_scalar(sm(s, NC_ + 1), sm(s, NC_), -1.0, 1.0, ALU.mult, ALU.add)\
                            .then_inc(g["norm"].handle, 1)
                        pool.tensor_scalar(sm(s, MASK), sm(s, NC_), 0.1, None, ALU.is_lt)
                        pool.tensor_tensor(out=sm(s, N2), in0=sm(s, NC_), in1=sm(s, NC_), op=ALU.mult).then_inc(m.handle, 1)
                        wait_apart(pool, apart_pool, (m.handle, m.after(4 * t + 2)))
                        pool.tensor_scalar(sm(s, SER), sm(s, N2), 1.0 / 7, 1.0 / 5, ALU.mult, ALU.add).then_inc(m.handle, 1)
                        wait_apart(pool, apart_pool, (m.handle, m.after(4 * t + 3)))
                        pool.tensor_scalar(sm(s, Q + 8), sm(s, SER), sm(s, N2), 1.0 / 3, ALU.mult, ALU.add).then_inc(m.handle, 1)
                        wait_apart(pool, apart_pool, (m.handle, m.after(4 * t + 4)))
                        pool.tensor_scalar(sm(s, SER), sm(s, Q + 8), sm(s, N2), 1.0, ALU.mult, ALU.add)\
                            .then_inc(g["placed"].handle, 1)

                    def residual(t, s, r):
                        wait_apart(pool, apart_pool, (g["h_done"].handle, g["h_done"].after(t + 1)))
                        if later(t, UNROLL):
                            wait_apart(pool, apart_pool, (store[s].handle, store[s].after(r * (16 * ns))))
                        pool.tensor_tensor(out=xh[:, s], in0=y[:, s], in1=h[:, s % 2], op=ALU.add)\
                            .then_inc(g["x_step"].handle, 1)
                    steps = []
                    if exp_map:
                        steps.append((1, mean_norm))
                    if norm:
                        steps.append((F, ln_scale))
                    if log_map:
                        steps.append((L, clipped_norm))
                    if attention:
                        steps.append((L, residual))
                    if steps:
                        pipelined(pool, N_TILES, steps)

                @block.scalar
                def _(act):
                    def mean_squares(t, s, r):
                        wait_apart(act, apart_act, (load[s].handle, load[s].after((r + 1) * (16 * nl))))
                        if later(t, 2):
                            wait_apart(act, apart_act, (g["squares"].handle, g["squares"].after(t - 1)))
                        act.activation(scrap[:, s % 2], inG[:, s], ACT.Square, scale=inverse[:, bass.ds(t, 1)],
                                       accum_out=sm(s, SS)).then_inc(g["squares"].handle, 1)

                    def tanh_norm(t, s, r):
                        act.wait_ge(g["norm"].handle, g["norm"].after(t + 1))
                        act.activation(sm(s, TANH), sm(s, NC_), ACT.Tanh).then_inc(g["a_step"].handle, 1)

                    def hidden(t, s, r):
                        if later(t, 2):
                            act.wait_ge(g["transposed"].handle, g["transposed"].after(t - 1))
                            if attention:
                                act.wait_ge(g["x_step"].handle, g["x_step"].after(t - 1))
                        if norm:
                            act.wait_ge(g["bias_ln"].handle, g["bias_ln"].after(t + 1))
                            act.activation(h[:, s % 2], y[:, s], ACT.Relu, bias=sm(s, LNB), scale=sm(s, RSTD))\
                               .then_inc(g["h_done"].handle, 1)
                        else:
                            act.wait_ge(g["combined"].handle, g["combined"].after(t + 1))
                            act.activation(h[:, s % 2], y[:, s], ACT.Relu).then_inc(g["h_done"].handle, 1)
                        if log_map:
                            wait_apart(act, apart_act, (g["h_done"].handle, g["h_done"].after(t + 1)))
                            act.activation(scrap[:, s % 2], h[:, s % 2], ACT.Square, accum_out=sm(s, SS))\
                               .then_inc(g["squares"].handle, 1)

                    def high(t, s, r):
                        act.wait_ge(g["transposed"].handle, g["transposed"].after(t + 1))
                        if later(t, UNROLL):
                            act.wait_ge(g["product"].handle, g["product"].after(t - UNROLL + 1))
                            if ht:
                                act.wait_ge(store[s].handle, store[s].after(r * (16 * ns)))
                        act.activation(hT[:, s, 0].rearrange("p k n -> p (k n)"), banks[s % 2][:], ACT.Copy)\
                           .then_inc(g["hi_done"].handle, 1)

                    def results(t, s, r):
                        if later(t, UNROLL):
                            act.wait_ge(store[s].handle, store[s].after(r * (16 * ns)))
                        if log_map:
                            act.wait_ge(g["out_sum"].handle, g["out_sum"].after(t + 1))
                            act.activation(zout[:, s, 0], zsum[:, s % 2], ACT.Copy).then_inc(g["out_hi"].handle, 1)
                        else:
                            act.wait_ge(g["product"].handle, g["product"].after(t + 1))
                            act.activation(zout[:, s, 0] if z_out else xl[:, s], banks[2 + s % 2][:], ACT.Copy,
                                           scale=1.0 / W_SCALE).then_inc(g["out_hi"].handle, 1)

                    def log_norm(t, s, r):
                        act.wait_ge(g["ranked"].handle, g["ranked"].after(4 * t + 2))
                        act.activation(sm(s, LNQ), sm(s, Q), ACT.Ln).then_inc(g["a_step"].handle, 1)
                    steps = [(L, hidden), (L + 2, results), (L, high)]
                    if exp_map:
                        steps = [(1, mean_squares), (2, tanh_norm)] + steps
                    if log_map:
                        steps = [(L + 1, log_norm), (L, hidden), (L, high), (L + 2, results)]
                    pipelined(act, N_TILES, steps)

                @block.tensor
                def _(pe):
                    def turn(t, s, r):
                        pe.wait_ge(g["h_done"].handle, g["h_done"].after(t + 1))
                        if later(t, 2):
                            pe.wait_ge(g["lo_done"].handle, g["lo_done"].after(t - 1))
                        for k in range(KT):
                            last = nc.tensor.transpose(banks[s % 2][:, k * P:(k + 1) * P], h[:, s % 2, k * P:(k + 1) * P],
                                                       ident[:])
                        last.then_inc(g["transposed"].handle, 1)

                    def multiply(t, s, r):
                        pe.wait_ge(g["lo_done"].handle, g["lo_done"].after(t + 1))
                        if later(t, 2):
                            b = g["out_sum"] if log_map else g["out_lo"]
                            pe.wait_ge(b.handle, b.after(t - 1))
                            if attention:
                                pe.wait_ge(g["out_hi"].handle, g["out_hi"].after(t - 1))
                        last = products(banks[2 + s % 2], hT[:, s], w_out, range(KT), True, True)
                        if attention:
                            last = products(banks[4 + s % 2], hT[:, s], w_out2, range(KT), True, True)
                        last.then_inc(g["product"].handle, 1)
                    pipelined(pe, N_TILES, [(0, turn), (1, multiply)])
            for s in range(UNROLL):
                load[s].passed(16 * nl * N_TILES // UNROLL)
                store[s].passed(16 * ns * N_TILES // UNROLL)
            done = {"h_done": 1, "transposed": 1, "hi_done": 1, "lo_done": 1, "product": 1, "out_hi": 1, "out_lo": 1,
                    "combined": combine, "stats": norm, "aggr": norm, "rstd": norm, "bias_ln": norm, "eps_added": norm,
                    "squares": exp_map or log_map, "norm": exp_map or log_map, "pow_step": exp_map or log_map,
                    "a_step": exp_map or log_map, "x_step": attention, "out_sum": log_map, "weighed": log_map,
                    "placed": log_map, "ranked": 4 * log_map, "p_step": 4 * log_map,
                    "y_step": 2 * exp_map + (combine and x_in is not None and not exp_map)}
            for name, n in done.items():
                g[name].passed(int(n) * N_TILES)

        def aggregate(idx_dram, agg, own_row=None):
            A = 2 * UNROLL
            own = own_row
            with ExitStack() as local:
                rows_in = sb("rows_in", [P, A, 2, D], f16, local)
                sums = sb("sums", [P, A, D], f32, local)
                idx = sb("idx", [P, A, 3], i32, local)
                hT = sb("hT_in", [P, UNROLL, 2, KT, P], f16, local) if own else None
                u = sb("u_out", [P, UNROLL, D], f32, local) if own else None
                block = local.enter_context(nc.Block())
                g = sig
                ind = [load[s] for s in range(UNROLL)] + [gather2[s] for s in range(UNROLL)]
                got = [gather[s] for s in range(UNROLL)] + [scatter[s] for s in range(UNROLL)]
                put = put_sems
                bound = N_PAD - 1

                @block.sync
                def _(sp):
                    def indices(c, s, r):
                        if later(c, A):
                            wait_apart(sp, apart_sp, (put[s].handle, put[s].after(16 * r)))
                        sp.dma_start(idx[:, s], idx_dram[:, bass.ds(3 * c, 3)]).then_inc(ind[s].handle, 16)

                    def own_load(c, s, r):
                        if s % 2:
                            return
                        t = r * UNROLL + s // 2
                        if later(t, UNROLL):
                            wait_apart(sp, apart_sp, (g["own_product"].handle, g["own_product"].after(t - UNROLL + 1)))
                        sp.dma_start(hT[:, s // 2].rearrange("p a k n -> p (a k n)"),
                                     HT[bass.ds(t, 1)].rearrange("o p n -> (o p) n")).then_inc(own_in[s // 2].handle, 16)

                    def own_store(c, s, r):
                        if s % 2:
                            return
                        t = r * UNROLL + s // 2
                        wait_apart(sp, apart_sp, (g["own_out"].handle, g["own_out"].after(t + 1)))
                        sp.dma_start(U[bass.ds(t * P, P), :], u[:, s // 2]).then_inc(store[s // 2].handle, 16)
                    pipelined(sp, N_CHUNKS, [(0, indices)] + ([(0, own_load), (5, own_store)] if own else []), A)
                    if own:
                        for s in range(UNROLL):
                            wait_apart(sp, apart_sp, (store[s].handle, store[s].after(16 * N_TILES // UNROLL)))
                    for s in range(A):
                        wait_apart(sp, apart_sp, (put[s].handle, put[s].after(16 * N_CHUNKS // A)))

                @block.gpsimd
                def _(pool):
                    def gathers(c, s, r):
                        wait_apart(pool, apart_pool, (ind[s].handle, ind[s].after(16 * (r + 1))))
                        if later(c, A):
                            wait_apart(pool, apart_pool, (g["summed"].handle, g["summed"].after(c - A + 1)))
                        pool.indirect_dma_start(out=rows_in[:, s].rearrange("p a n -> p (a n)"), out_offset=None, in_=Z,
                                                in_offset=bass.IndirectOffsetOnAxis(ap=idx[:, s, 0:1], axis=0),
                                                bounds_check=bound, oob_is_err=False).then_inc(got[s].handle, 16)

                    def scatters(c, s, r):
                        wait_apart(pool, apart_pool, (g["sums_out"].handle, g["sums_out"].after(c + 1)))
                        pool.indirect_dma_start(out=agg, out_offset=bass.IndirectOffsetOnAxis(ap=idx[:, s, 1:2], axis=0),
                                                in_=sums[:, s], in_offset=None,
                                                bounds_check=bound, oob_is_err=False).then_inc(put[s].handle, 16)
                    pool.wait_ge(g["carry_lo"].handle, g["carry_lo"].after(1))
                    pipelined(pool, N_CHUNKS, [(0, gathers), (5, scatters)], A)

                @block.tensor
                def _(pe):
                    def sum_up(c, s, r):
                        pe.wait_ge(got[s].handle, got[s].after(16 * (r + 1)))
                        pe.wait_ge(g["carry_lo"].handle, g["carry_lo"].after(c + 1))
                        if later(c, 2):
                            pe.wait_ge(g["sums_out"].handle, g["sums_out"].after(c - 1))
                        sel = SEL[:, bass.ds(c, 1), :].rearrange("p o m -> p (o m)")
                        nc.tensor.matmul(banks[s % 2][:], sel, rows_in[:, s, 0], start=True, stop=False)
                        nc.tensor.matmul(banks[s % 2][:], sel, rows_in[:, s, 1], start=False, stop=True)\
                          .then_inc(g["summed"].handle, 1)

                    def own_part(c, s, r):
                        t = r * UNROLL + s // 2
                        b = 2 + s // 2 % 2
                        if s % 2 == 0:
                            pe.wait_ge(own_in[s // 2].handle, own_in[s // 2].after(16 * (r + 1)))
                            if later(t, 2):
                                pe.wait_ge(g["own_out"].handle, g["own_out"].after(t - 1))
                            products(banks[b], hT[:, s // 2], w_own, range(0, KT // 2), True, False)
                        else:
                            products(banks[b], hT[:, s // 2], w_own, range(KT // 2, KT), False, True)\
                                .then_inc(g["own_product"].handle, 1)
                    pipelined(pe, N_CHUNKS, [(0, sum_up)] + ([(0, own_part)] if own else []), A)

                @block.scalar
                def _(act):
                    def carry_high(c, s, r):
                        act.wait_ge(g["summed"].handle, g["summed"].after(c + 1))
                        if type(c) is not int or c + 1 < N_CHUNKS:
                            act.wait_ge(got[(s + 1) % A].handle, got[(s + 1) % A].after(16 * (r + 1 + (s + 1) // A)))
                        act.activation(rows_in[0:1, (s + 1) % A, 0], banks[s % 2][0:1, :], ACT.Copy)\
                           .then_inc(g["carry_hi"].handle, 1)

                    def evict(c, s, r):
                        act.wait_ge(g["carry_lo"].handle, g["carry_lo"].after(c + 2))
                        if later(c, A):
                            act.wait_ge(put[s].handle, put[s].after(16 * r))
                        act.activation(sums[:, s], banks[s % 2][:], ACT.Copy).then_inc(g["sums_out"].handle, 1)
                    pipelined(act, N_CHUNKS, [(0, carry_high), (0, evict)], A, end=1)

                @block.vector
                def _(dve):
                    dve.memset(rows_in[0:1, 0], 0.0).then_inc(g["carry_lo"].handle, 1)

                    def carry_low(c, s, r):
                        dve.wait_ge(g["carry_hi"].handle, g["carry_hi"].after(c + 1))
                        dve.tensor_tensor(rows_in[0:1, (s + 1) % A, 1], banks[s % 2][0:1, :],
                                          rows_in[0:1, (s + 1) % A, 0], ALU.subtract).then_inc(g["carry_lo"].handle, 1)

                    def own_evict(c, s, r):
                        if s % 2 == 0:
                            return
                        t = r * UNROLL + s // 2
                        dve.wait_ge(g["own_product"].handle, g["own_product"].after(t + 1))
                        if later(t, UNROLL):
                            dve.wait_ge(store[s // 2].handle, store[s // 2].after(16 * r))
                        dve.scalar_tensor_tensor(u[:, s // 2], banks[2 + s // 2 % 2][:], 1.0 / W_SCALE, bias_own[:],
                                                 ALU.mult, ALU.add).then_inc(g["own_out"].handle, 1)
                    pipelined(dve, N_CHUNKS, [(0, carry_low)] + ([(0, own_evict)] if own else []), A)
            for s in range(UNROLL):
                for d_ in (load, gather2, gather, scatter):
                    d_[s].passed(16 * N_CHUNKS // A)
                if own:
                    own_in[s].passed(16 * N_TILES // UNROLL)
                    store[s].passed(16 * N_TILES // UNROLL)
            for s in range(A):
                put[s].passed(16 * N_CHUNKS // A)
            for name, n in {"summed": 0, "carry_hi": 0, "carry_lo": 1, "sums_out": 0}.items():
                g[name].passed(N_CHUNKS + n)
            if own:
                g["own_product"].passed(N_TILES)
                g["own_out"].passed(N_TILES)

        def order_edges(lane_col, tile_col, total):
            with ExitStack() as local:
                S = UNROLL
                pairs = sb("pairs", [P, N_CHUNKS, 2], i32, local)
                lane_hot = sb("lane_hot", [P, S, P], f16, local)
                tile_hot = sb("tile_hot", [P, S, N_TILES], f32, local)
                tile_hot16 = sb("tile_hot16", [P, S, N_TILES], f16, local)
                lane_turned = sb("lane_turned", [P, S, P], f32, local)
                diag = sb("diag", [P, S, P], f32, local)
                scrap = sb("scrap", [P, S, P], f32, local)
                scrap2 = sb("scrap2", [P, S, N_TILES], f32, local)
                base = sb("base", [P, S, N_TILES], f32, local)
                col_sum = sb("col_sum", [P, N_TILES], f32, local)
                scan = sb("scan", [P, N_TILES], f32, local)
                rank = sb("rank", [P, S], f32, local)
                ahead = sb("ahead", [P, S], f32, local)
                place_i = sb("place_i", [P, S], i32, local)
                pair = sb("pair", [P, S, 2], i32, local)
                ends = sb("ends", [1, 2], i32, local)
                block = local.enter_context(nc.Block())
                g = sig
                v0, t0 = g["v_step"], g["t_step"]

                @block.sync
                def _(sp):
                    wait_apart(sp, apart_sp, (v0.handle, v0.after(1)))
                    sp.dma_start(SORTED[0:1, :], ends[:]).then_inc(once.handle, 16)
                    sp.dma_start(SORTED[E_PAD + 1:E_PAD + 2, :], ends[:]).then_inc(once.handle, 16)
                    wait_apart(sp, apart_sp, (once.handle, once.after(32)))
                    for s in range(S):
                        wait_apart(sp, apart_sp, (scatter[s].handle, scatter[s].after(16 * N_CHUNKS // S)))

                @block.gpsimd
                def _(pool):
                    def put(c, s, r):
                        wait_apart(pool, apart_pool, (g["placed"].handle, g["placed"].after(c + 1)))
                        pool.indirect_dma_start(out=SORTED,
                                                out_offset=bass.IndirectOffsetOnAxis(ap=place_i[:, s:s + 1], axis=0),
                                                in_=pair[:, s], in_offset=None, bounds_check=E_PAD,
                                                oob_is_err=False).then_inc(scatter[s].handle, 16)
                    pipelined(pool, N_CHUNKS, [(0, put)])

                @block.tensor
                def _(pe):
                    pe.wait_ge(v0.handle, v0.after(1))
                    nc.tensor.matmul(banks[0][:, 0:N_TILES], ones[:], total[:], start=True, stop=True)
                    nc.tensor.matmul(banks[1][:, 0:N_TILES], below[:], total[:], start=True, stop=True)\
                      .then_inc(t0.handle, 1)

                    def spread(c, s, r):
                        b = s % 2
                        pe.wait_ge(g["onehot"].handle, g["onehot"].after(c + 1))
                        if type(c) is int and c < 2:
                            pe.wait_ge(v0.handle, v0.after(8))
                        else:
                            pe.wait_ge(g["a_step"].handle, g["a_step"].after(c - 1))
                            pe.wait_ge(g["ranked"].handle, g["ranked"].after(c - 1))
                            pe.wait_ge(g["based"].handle, g["based"].after(c - 1))
                        nc.tensor.transpose(banks[b].bitcast(f16)[:, 0:P], lane_hot[:, s], ident16[:])
                        nc.tensor.matmul(banks[2 + b][:, 0:P], ones[:], diag[:, s], start=True, stop=True)
                        nc.tensor.matmul(banks[4 + b][:, 0:N_TILES], lane_hot[:, s], tile_hot16[:, s], start=True,
                                         stop=True).then_inc(g["counted"].handle, 1)

                    def look_up(c, s, r):
                        pe.wait_ge(g["a_step"].handle, g["a_step"].after(c + 1))
                        pe.wait_ge(g["based"].handle, g["based"].after(c + 1))
                        if later(c, 2):
                            pe.wait_ge(g["placed"].handle, g["placed"].after(c - 1))
                        nc.tensor.matmul(banks[6 + s % 2][:, 0:N_TILES], lane_turned[:, s], base[:, s], start=True,
                                         stop=True).then_inc(g["looked"].handle, 1)
                    pipelined(pe, N_CHUNKS, [(0, spread), (1, look_up)])

                @block.scalar
                def _(act):
                    def turned(c, s, r):
                        act.wait_ge(g["counted"].handle, g["counted"].after(c + 1))
                        if later(c, S):
                            act.wait_ge(g["looked"].handle, g["looked"].after(c - S + 1))
                        act.activation(lane_turned[:, s], banks[s % 2].bitcast(f16)[:, 0:P], ACT.Copy)\
                           .then_inc(g["a_step"].handle, 1)
                    pipelined(act, N_CHUNKS, [(0, turned)])

                @block.vector
                def _(dve):
                    v = Signal(v0.handle)
                    v.base = v0.base
                    chain(dve, dve.memset(ends[:], -1), v)
                    chain(dve, dve.tensor_copy(pairs[:, :, 0], key_col[:]), v)
                    chain(dve, dve.tensor_copy(pairs[:, :, 1], val_col[:]), v)
                    dve.wait_ge(t0.handle, t0.after(1))
                    chain(dve, dve.tensor_copy(col_sum[:], banks[0][:, 0:N_TILES]), v)
                    chain(dve, dve.tensor_tensor_scan(scan[:], ones[:, 0:N_TILES], col_sum[:], 0.0, ALU.mult, ALU.add), v)
                    chain(dve, dve.tensor_tensor(scan[:], scan[:], col_sum[:], ALU.subtract), v)
                    chain(dve, dve.scalar_tensor_tensor(base[:, 0], banks[1][:, 0:N_TILES], 1.0, scan[:], ALU.add,
                                                        ALU.add), v)
                    dve.sem_inc(g["based"].handle, 1)
                    chain(dve, dve.tensor_copy(scrap[:, 0], ones[:]), v)

                    def hot(c, s, r):
                        if later(c, S):
                            dve.wait_ge(g["counted"].handle, g["counted"].after(c - S + 1))
                        one = bass.ds(c, 1)
                        dve.tensor_scalar(lane_hot[:, s], lane_row[:], lane_col[:, one], None, ALU.is_equal)
                        dve.tensor_scalar(tile_hot[:, s], tile_row[:], tile_col[:, one], None, ALU.is_equal)
                        dve.tensor_scalar(tile_hot16[:, s], tile_row[:], tile_col[:, one], None, ALU.is_equal)
                        dve.tensor_scalar(diag[:, s], ident[:], key_col[:, one], None, ALU.mult)\
                           .then_inc(g["onehot"].handle, 1)

                    def rest(c, s, r):
                        one = bass.ds(c, 1)
                        dve.wait_ge(g["counted"].handle, g["counted"].after(c + 1))
                        wait_apart(dve, apart_dve, (g["based"].handle, g["based"].after(c + 1)))
                        dve.tensor_tensor(base[:, (s + 1) % S], base[:, s], banks[4 + s % 2][:, 0:N_TILES], ALU.add)\
                           .then_inc(g["based"].handle, 1)
                        dve.scalar_tensor_tensor(scrap[:, s], banks[2 + s % 2][:, 0:P], key_col[:, one], earlier[:],
                                                 ALU.is_equal, ALU.mult, accum_out=rank[:, s:s + 1])\
                           .then_inc(g["ranked"].handle, 1)

                    def place(c, s, r):
                        one = bass.ds(c, 1)
                        wait_apart(dve, apart_dve, (g["looked"].handle, g["looked"].after(c + 1)))
                        dve.scalar_tensor_tensor(scrap2[:, s], banks[6 + s % 2][:, 0:N_TILES], 1.0, tile_hot[:, s],
                                                 ALU.mult, ALU.mult, accum_out=ahead[:, s:s + 1])\
                           .then_inc(g["sel_done"].handle, 1)
                        if later(c, S):
                            wait_apart(dve, apart_dve, (scatter[s].handle, scatter[s].after(16 * r)))
                        dve.tensor_copy(pair[:, s], pairs[:, one, :].rearrange("p o k -> p (o k)"))
                        wait_apart(dve, apart_dve, (g["sel_done"].handle, g["sel_done"].after(c + 1)))
                        dve.scalar_tensor_tensor(place_i[:, s:s + 1], rank[:, s:s + 1], ahead[:, s:s + 1], skip0[:, 0:1],
                                                 ALU.add, ALU.add).then_inc(g["placed"].handle, 1)
                    pipelined(dve, N_CHUNKS, [(0, hot), (1, rest), (2, place)])
            v0.passed(8)
            t0.passed(1)
            once.passed(32)
            for s in range(S):
                scatter[s].passed(16 * N_CHUNKS // S)
            for name in ("onehot", "counted", "a_step", "looked", "ranked", "sel_done", "placed"):
                g[name].passed(N_CHUNKS)
            g["based"].passed(N_CHUNKS + 1)

        def attention_scores(score):
            A = 2 * UNROLL
            with ExitStack() as local:
                left = sb("left", [P, A, D], f32, local)
                right = sb("right", [P, A, D], f32, local)
                t1 = sb("t1", [P, 2, D], f32, local)
                t2 = sb("t2", [P, 2, D], f32, local)
                idx = sb("idx", [P, A, 3], i32, local)
                block = local.enter_context(nc.Block())
                g = sig
                ind = load + gather2
                got = gather + scatter

                @block.sync
                def _(sp):
                    def indices(c, s, r):
                        if later(c, A):
                            wait_apart(sp, apart_sp, (got[s].handle, got[s].after(32 * r)))
                        sp.dma_start(idx[:, s], IDX_D[:, bass.ds(3 * c, 3)]).then_inc(ind[s].handle, 16)
                    pipelined(sp, N_CHUNKS, [(0, indices)], A)

                @block.gpsimd
                def _(pool):
                    pool.wait_ge(g["v_step"].handle, g["v_step"].after(2))

                    def gathers(c, s, r):
                        wait_apart(pool, apart_pool, (ind[s].handle, ind[s].after(16 * (r + 1))))
                        if later(c, A):
                            wait_apart(pool, apart_pool, (g["summed"].handle, g["summed"].after(c - A + 1)))
                        for rows, table, k in ((left, XL, 0), (right, XR, 2)):
                            pool.indirect_dma_start(out=rows[:, s], out_offset=None, in_=table,
                                                    in_offset=bass.IndirectOffsetOnAxis(ap=idx[:, s, k:k + 1], axis=0),
                                                    bounds_check=N_PAD - 1, oob_is_err=False).then_inc(got[s].handle, 16)
                    pipelined(pool, N_CHUNKS, [(0, gathers)], A)

                @block.vector
                def _(dve):
                    dve.memset(left[0:1], 0.0).then_inc(g["v_step"].handle, 1)
                    dve.memset(right[0:1], 0.0).then_inc(g["v_step"].handle, 1)

                    def scores(c, s, r):
                        b = s % 2
                        q = g["y_step"]
                        dve.wait_ge(got[s].handle, got[s].after(32 * (r + 1)))
                        dve.tensor_tensor(t1[:, b], left[:, s], right[:, s], ALU.add).then_inc(g["summed"].handle, 1)
                        wait_apart(dve, apart_dve, (g["summed"].handle, g["summed"].after(c + 1)))
                        dve.scalar_tensor_tensor(t2[:, b], t1[:, b], 0.2, t1[:, b], ALU.mult, ALU.max).then_inc(q.handle, 1)
                        wait_apart(dve, apart_dve, (q.handle, q.after(2 * c + 1)))
                        dve.tensor_tensor(t1[:, b], t2[:, b], att_row[:], ALU.mult).then_inc(q.handle, 1)
                        wait_apart(dve, apart_dve, (q.handle, q.after(2 * c + 2)))
                        dve.tensor_reduce(score[:, bass.ds(c, 1), :].rearrange("p o h -> p (o h)"),
                                          t1[:, b].rearrange("p (h k) -> p h k", h=HEADS), AX.X, ALU.add)
                    pipelined(dve, N_CHUNKS, [(0, scores)], A)
            for s in range(UNROLL):
                load[s].passed(16 * N_CHUNKS // A)
                gather2[s].passed(16 * N_CHUNKS // A)
                gather[s].passed(32 * N_CHUNKS // A)
                scatter[s].passed(32 * N_CHUNKS // A)
            g["v_step"].passed(2)
            g["summed"].passed(N_CHUNKS)
            g["y_step"].passed(2 * N_CHUNKS)

        def attention_maxima(score, top, weight):
            Q = 4
            J = N_CHUNKS // Q
            W = J * EDGES
            LANES = P // Q
            with ExitStack() as local:
                turned = sb("turned", [P, 1 + W], f32, local)
                keys = sb("keys", [P, W + 2], i32, local)
                gap = sb("gap", [P, W], f32, local)
                start = sb("start", [P, 1], f32, local)
                spread = sb("spread", [P, J, Q, LANES], f32, local)
                block = local.enter_context(nc.Block())
                g = sig
                v0, t0, a0 = g["v_step"], g["t_step"], g["a_step"]
                B = J // UNROLL
                N_SCAN = 3 + 2 * (2 + 2 * Q)

                @block.sync
                def _(sp):
                    for q in range(Q):
                        sp.dma_start(keys[q * LANES:(q + 1) * LANES, :],
                                     bass.AP(dst_list.tensor, q * W, [[0, LANES], [1, W + 2]])).then_inc(once.handle, 16)

                @block.tensor
                def _(pe):
                    pe.wait_ge(v0.handle, v0.after(2))
                    for b in range(B):
                        if b >= 2:
                            pe.wait_ge(a0.handle, a0.after(b - 1))
                        for n in range(UNROLL):
                            j = b * UNROLL + n
                            last = nc.tensor.transpose(banks[b % 2][:, n * P:(n + 1) * P],
                                                       spread[:, j].rearrange("p q l -> p (q l)"), ident[:])
                        last.then_inc(t0.handle, 1)
                    pe.wait_ge(v0.handle, v0.after(N_SCAN))
                    for b in range(B):
                        pe.wait_ge(a0.handle, a0.after(max(B, B + b - 1)))
                        for n in range(UNROLL):
                            j = b * UNROLL + n
                            last = nc.tensor.transpose(banks[b % 2][:, n * P:(n + 1) * P],
                                                       turned[:, j * EDGES:j * EDGES + P], ident[:])
                        last.then_inc(t0.handle, 1)

                @block.scalar
                def _(act):
                    for b in range(B):
                        act.wait_ge(t0.handle, t0.after(b + 1))
                        act.activation(turned[:, 1 + b * UNROLL * EDGES:1 + (b + 1) * UNROLL * EDGES]
                                       .rearrange("p (n e) -> p n e", n=UNROLL),
                                       banks[b % 2].rearrange("p (n e) -> p n e", n=UNROLL)[:, :, 1:], ACT.Copy)\
                           .then_inc(a0.handle, 1)
                    for b in range(B):
                        act.wait_ge(t0.handle, t0.after(B + b + 1))
                        for n in range(UNROLL):
                            j = b * UNROLL + n
                            last = act.activation(top[:].rearrange("p (q j) h -> p j q h", q=Q)[:, j],
                                                  banks[b % 2][:, n * P:(n + 1) * P]
                                                  .rearrange("p (q l) -> p q l", q=Q)[:, :, 0:HEADS], ACT.Copy)
                        last.then_inc(a0.handle, 1)
                    act.wait_ge(v0.handle, v0.after(N_SCAN + 1))
                    act.activation(weight[:], weight[:], ACT.Exp).then_inc(a0.handle, 1)

                @block.vector
                def _(dve):
                    v = Signal(v0.handle)
                    v.base = v0.base
                    lanes = lambda q: slice(q * LANES, (q + 1) * LANES)
                    chain(dve, dve.memset(spread[:], 0.0), v)
                    chain(dve, dve.tensor_copy(spread[:, :, :, 0:HEADS],
                                               score[:].rearrange("p (q j) h -> p j q h", q=Q)), v)
                    dve.wait_ge(once.handle, once.after(16 * Q))
                    chain(dve, dve.memset(turned[:, 0:1], 0.0), v)
                    for back in (False, True):
                        other = keys[:, 2:W + 2] if back else keys[:, 0:W]
                        chain(dve, dve.tensor_tensor(gap[:], keys[:, 1:W + 1], other, ALU.is_equal), v)
                        chain(dve, dve.tensor_scalar(gap[:], gap[:], -1.0, -LOW, ALU.add, ALU.mult), v)
                        if not back:
                            dve.wait_ge(a0.handle, a0.after(B))
                        for n in range(Q):
                            q = Q - 1 - n if back else n
                            prior = q + 1 if back else q - 1
                            if n == 0:
                                chain(dve, dve.memset(start[lanes(q), :], LOW), v)
                            else:
                                end = turned[lanes(prior), 1:2] if back else turned[lanes(prior), W:W + 1]
                                chain(dve, dve.tensor_copy(start[lanes(q), :], end), v)
                            line = turned[lanes(q), 1:W + 1]
                            flags = gap[lanes(q), :]
                            if back:
                                line, flags = turned[lanes(q), W:0:-1], gap[lanes(q), ::-1]
                            chain(dve, dve.tensor_tensor_scan(line, flags, line, start[lanes(q), 0:1], ALU.add, ALU.max), v)
                    dve.wait_ge(a0.handle, a0.after(2 * B))
                    dve.tensor_tensor(weight[:], score[:], top[:], ALU.subtract).then_inc(v.handle, 1)
                    dve.wait_ge(a0.handle, a0.after(2 * B + 1))
                    dve.memset(weight[0:1], 0.0)
            once.passed(16 * Q)
            v0.passed(N_SCAN + 1)
            t0.passed(2 * B)
            a0.passed(2 * B + 1)

        def attention_sums(top, weight):
            A = 2 * UNROLL
            WIDE = D + HEADS
            with ExitStack() as local:
                raw = sb("raw", [P, A, D], f32, local)
                rows_in = sb("rows_in", [P, UNROLL, 2, WIDE], f16, local)
                scaled = sb("scaled", [P, 2, WIDE], f32, local)
                sums = sb("sums", [P, A, WIDE + HEADS], f32, local)
                idx = sb("idx", [P, A, 3], i32, local)
                block = local.enter_context(nc.Block())
                g = sig
                ind = load + gather2
                got = gather + scatter
                put = put_sems
                pair = lambda s: psum[:, (s % 2) * 2 * BANK:(s % 2) * 2 * BANK + WIDE]

                @block.sync
                def _(sp):
                    def indices(c, s, r):
                        if later(c, A):
                            wait_apart(sp, apart_sp, (put[s].handle, put[s].after(16 * r)))
                        sp.dma_start(idx[:, s], IDX_D[:, bass.ds(3 * c, 3)]).then_inc(ind[s].handle, 16)
                    pipelined(sp, N_CHUNKS, [(0, indices)], A)
                    for s in range(A):
                        wait_apart(sp, apart_sp, (put[s].handle, put[s].after(16 * N_CHUNKS // A)))

                @block.gpsimd
                def _(pool):
                    pool.wait_ge(g["v_step"].handle, g["v_step"].after(1))

                    def gathers(c, s, r):
                        wait_apart(pool, apart_pool, (ind[s].handle, ind[s].after(16 * (r + 1))))
                        if later(c, A):
                            wait_apart(pool, apart_pool, (g["weighed"].handle, g["weighed"].after(c - A + 1)))
                        pool.indirect_dma_start(out=raw[:, s], out_offset=None, in_=XL,
                                                in_offset=bass.IndirectOffsetOnAxis(ap=idx[:, s, 0:1], axis=0),
                                                bounds_check=N_PAD - 1, oob_is_err=False).then_inc(got[s].handle, 16)

                    def scatters(c, s, r):
                        wait_apart(pool, apart_pool, (g["sums_out"].handle, g["sums_out"].after(c + 1)))
                        pool.indirect_dma_start(out=AGG_A, out_offset=bass.IndirectOffsetOnAxis(ap=idx[:, s, 1:2], axis=0),
                                                in_=sums[:, s], in_offset=None,
                                                bounds_check=N_PAD - 1, oob_is_err=False).then_inc(put[s].handle, 16)
                    pipelined(pool, N_CHUNKS, [(0, gathers), (6, scatters)], A)

                @block.tensor
                def _(pe):
                    def sum_up(c, s, r):
                        pe.wait_ge(g["carry_lo"].handle, g["carry_lo"].after(c + 1))
                        if later(c, 2):
                            pe.wait_ge(g["sums_out"].handle, g["sums_out"].after(c - 1))
                        sel = SEL[:, bass.ds(c, 1), :].rearrange("p o m -> p (o m)")
                        for first, n in ((0, D), (D, HEADS)):
                            for half_ in range(2):
                                last = nc.tensor.matmul(pair(s)[:, first:first + n], sel,
                                                        rows_in[:, s % UNROLL, half_, first:first + n],
                                                        start=half_ == 0, stop=half_ == 1)
                        last.then_inc(g["summed"].handle, 1)
                    pipelined(pe, N_CHUNKS, [(0, sum_up)], A)

                @block.scalar
                def _(act):
                    def high(c, s, r):
                        act.wait_ge(g["weighed"].handle, g["weighed"].after(c + 1))
                        if later(c, UNROLL):
                            act.wait_ge(g["summed"].handle, g["summed"].after(c - UNROLL + 1))
                        act.activation(rows_in[:, s % UNROLL, 0], scaled[:, s % 2], ACT.Copy).then_inc(g["w_hi"].handle, 1)

                    def carry_high(c, s, r):
                        act.wait_ge(g["summed"].handle, g["summed"].after(c + 1))
                        if type(c) is not int or c + 1 < N_CHUNKS:
                            act.wait_ge(g["w_lo"].handle, g["w_lo"].after(c + 2))
                        act.activation(rows_in[0:1, (s + 1) % UNROLL, 0], pair(s)[0:1, :], ACT.Copy)\
                           .then_inc(g["carry_hi"].handle, 1)

                    def evict(c, s, r):
                        act.wait_ge(g["carry_lo"].handle, g["carry_lo"].after(c + 2))
                        if later(c, A):
                            wait_apart(act, apart_act, (put[s].handle, put[s].after(16 * r)))
                        act.activation(sums[:, s, WIDE:], top[:, bass.ds(c, 1), :].rearrange("p o h -> p (o h)"), ACT.Copy)
                        act.activation(sums[:, s, 0:WIDE], pair(s), ACT.Copy).then_inc(g["sums_out"].handle, 1)
                    pipelined(act, N_CHUNKS, [(0, high), (2, carry_high), (2, evict)], A, end=1)

                @block.vector
                def _(dve):
                    def weigh(c, s, r):
                        wait_apart(dve, apart_dve, (got[s].handle, got[s].after(16 * (r + 1))))
                        if later(c, 2):
                            wait_apart(dve, apart_dve, (g["w_lo"].handle, g["w_lo"].after(c - 1)))
                        w = weight[:, bass.ds(c, 1), :].rearrange("p o h -> p (o h)")
                        dve.tensor_tensor(scaled[:, s % 2, 0:D].rearrange("p (h k) -> p h k", h=HEADS),
                                          raw[:, s].rearrange("p (h k) -> p h k", h=HEADS),
                                          w.unsqueeze(2).to_broadcast([P, HEADS, HEAD_DIM]), ALU.mult)
                        dve.tensor_copy(scaled[:, s % 2, D:], w).then_inc(g["weighed"].handle, 1)

                    def low(c, s, r):
                        dve.wait_ge(g["w_hi"].handle, g["w_hi"].after(c + 1))
                        dve.tensor_tensor(rows_in[:, s % UNROLL, 1], scaled[:, s % 2], rows_in[:, s % UNROLL, 0],
                                          ALU.subtract).then_inc(g["w_lo"].handle, 1)
                        if type(c) is int and c == 0:
                            dve.wait_ge(g["w_lo"].handle, g["w_lo"].after(1))
                            dve.memset(rows_in[0:1, 0], 0.0).then_inc(g["carry_lo"].handle, 1)

                    def carry_low(c, s, r):
                        dve.wait_ge(g["carry_hi"].handle, g["carry_hi"].after(c + 1))
                        dve.tensor_tensor(rows_in[0:1, (s + 1) % UNROLL, 1], pair(s)[0:1, :],
                                          rows_in[0:1, (s + 1) % UNROLL, 0], ALU.subtract).then_inc(g["carry_lo"].handle, 1)
                    dve.memset(raw[0:1], 0.0).then_inc(g["v_step"].handle, 1)
                    pipelined(dve, N_CHUNKS, [(0, weigh), (2, carry_low), (0, low)], A)
            for s in range(UNROLL):
                for d_ in (load, gather2, gather, scatter):
                    d_[s].passed(16 * N_CHUNKS // A)
            for s in range(A):
                put[s].passed(16 * N_CHUNKS // A)
            g["v_step"].passed(1)
            for name, n in {"summed": 0, "carry_hi": 0, "carry_lo": 1, "sums_out": 0, "weighed": 0, "w_hi": 0,
                            "w_lo": 0}.items():
                g[name].passed(N_CHUNKS + n)

        def attention_output():
            WIDE = D + 2 * HEADS
            with ExitStack() as local:
                sums = sb("sums_in", [P, UNROLL, WIDE], f32, local)
                left = sb("left_in", [P, UNROLL, D], f32, local)
                right = sb("right_in", [P, UNROLL, D], f32, local)
                rest = sb("rest_in", [P, UNROLL, D], f32, local)
                both = sb("both", [P, 2, D], f32, local)
                leaky = sb("leaky", [P, 2, D], f32, local)
                prod = sb("prod", [P, 2, D], f32, local)
                near = sb("near", [P, 2, D], f32, local)
                near2 = sb("near2", [P, 2, D], f32, local)
                far = sb("far", [P, 2, D], f32, local)
                mixed = sb("mixed", [P, 2, D], f32, local)
                neg = sb("neg", [P, 2, D], f32, local)
                ex = sb("ex", [P, 2, D], f32, local)
                pos = sb("pos", [P, 2, D], f32, local)
                elu = sb("elu", [P, 2, D], f32, local)
                res = sb("res", [P, UNROLL, D], f32, local)
                own = sb("own", [P, UNROLL, HEADS], f32, local)
                m = sb("m", [P, UNROLL, HEADS], f32, local)
                dif = sb("dif", [P, UNROLL, 2, HEADS], f32, local)
                e = sb("e", [P, UNROLL, 2, HEADS], f32, local)
                den = sb("den", [P, UNROLL, HEADS], f32, local)
                coef = sb("coef", [P, UNROLL, 2, HEADS], f32, local)
                block = local.enter_context(nc.Block())
                g = sig
                wide = lambda a: a.unsqueeze(2).to_broadcast([P, HEADS, HEAD_DIM])
                heads = lambda a: a.rearrange("p (h k) -> p h k", h=HEADS)

                @block.sync
                def _(sp):
                    def loads(t, s, r):
                        if later(t, UNROLL):
                            wait_apart(sp, apart_sp, (g["out_lo"].handle, g["out_lo"].after(t - UNROLL + 1)))
                        for of, to in ((AGG_A, sums), (XL, left), (XR, right), (XH, rest)):
                            sp.dma_start(to[:, s], of[bass.ds(t * P, P), :]).then_inc(load[s].handle, 16)

                    def stores(t, s, r):
                        wait_apart(sp, apart_sp, (g["out_lo"].handle, g["out_lo"].after(t + 1)))
                        sp.dma_start(out[bass.ds(t * P, P), :], res[:, s]).then_inc(store[s].handle, 16)
                    pipelined(sp, N_TILES, [(0, loads), (3, stores)])
                    for s in range(UNROLL):
                        wait_apart(sp, apart_sp, (store[s].handle, store[s].after(16 * N_TILES // UNROLL)))

                @block.gpsimd
                def _(pool):
                    def add(t, s, r):
                        wait_apart(pool, apart_pool, (load[s].handle, load[s].after(64 * (r + 1))))
                        if later(t, 2):
                            wait_apart(pool, apart_pool, (g["hi_done"].handle, g["hi_done"].after(t - 1)))
                        pool.tensor_tensor(out=both[:, s % 2], in0=left[:, s], in1=right[:, s], op=ALU.add)\
                            .then_inc(g["x_step"].handle, 1)

                    def own_share(t, s, r):
                        wait_apart(pool, apart_pool, (g["norm"].handle, g["norm"].after(t + 1)))
                        if later(t, 2):
                            wait_apart(pool, apart_pool, (g["product"].handle, g["product"].after(t - 1)))
                        pool.tensor_tensor(out=heads(near[:, s % 2]), in0=heads(left[:, s]), in1=wide(coef[:, s, 1]),
                                           op=ALU.mult).then_inc(g["p_step"].handle, 1)
                        wait_apart(pool, apart_pool, (g["p_step"].handle, g["p_step"].after(t + 1)))
                        pool.tensor_tensor(out=near2[:, s % 2], in0=near[:, s % 2], in1=bias_out[:], op=ALU.add)\
                            .then_inc(g["placed"].handle, 1)
                    pipelined(pool, N_TILES, [(0, add), (1, own_share)])

                @block.scalar
                def _(act):
                    def exps(t, s, r):
                        act.wait_ge(g["squares"].handle, g["squares"].after(t + 1))
                        act.activation(e[:, s], dif[:, s], ACT.Exp).then_inc(g["a_step"].handle, 1)

                    def elu_parts(t, s, r):
                        q = g["w_hi"]
                        act.wait_ge(g["product"].handle, g["product"].after(t + 1))
                        if later(t, 2):
                            act.wait_ge(g["out_sum"].handle, g["out_sum"].after(t - 1))
                        act.activation(neg[:, s % 2], mixed[:, s % 2], ACT.Relu, scale=-1.0).then_inc(q.handle, 1)
                        act.activation(pos[:, s % 2], mixed[:, s % 2], ACT.Relu)
                        act.wait_ge(q.handle, q.after(t + 1))
                        act.activation(ex[:, s % 2], neg[:, s % 2], ACT.Exp, scale=-1.0).then_inc(g["out_hi"].handle, 1)
                    pipelined(act, N_TILES, [(0, exps), (1, elu_parts)])

                @block.vector
                def _(dve):
                    def own_score(t, s, r):
                        b = s % 2
                        q = g["y_step"]
                        dve.wait_ge(g["x_step"].handle, g["x_step"].after(t + 1))
                        dve.scalar_tensor_tensor(leaky[:, b], both[:, b], 0.2, both[:, b], ALU.mult, ALU.max)\
                           .then_inc(g["hi_done"].handle, 1)
                        wait_apart(dve, apart_dve, (g["hi_done"].handle, g["hi_done"].after(t + 1)))
                        dve.tensor_tensor(prod[:, b], leaky[:, b], att_row[:], ALU.mult).then_inc(q.handle, 1)
                        wait_apart(dve, apart_dve, (q.handle, q.after(3 * t + 1)))
                        dve.tensor_reduce(own[:, s], heads(prod[:, b]), AX.X, ALU.add).then_inc(q.handle, 1)
                        wait_apart(dve, apart_dve, (q.handle, q.after(3 * t + 2)))
                        dve.tensor_tensor(m[:, s], own[:, s], sums[:, s, D + HEADS:], ALU.max).then_inc(q.handle, 1)
                        wait_apart(dve, apart_dve, (q.handle, q.after(3 * t + 3)))
                        dve.tensor_tensor(dif[:, s, 0], sums[:, s, D + HEADS:], m[:, s], ALU.subtract)
                        dve.tensor_tensor(dif[:, s, 1], own[:, s], m[:, s], ALU.subtract).then_inc(g["squares"].handle, 1)

                    def coefficients(t, s, r):
                        q = g["ranked"]
                        wait_apart(dve, apart_dve, (g["a_step"].handle, g["a_step"].after(t + 1)))
                        dve.tensor_tensor(den[:, s], e[:, s, 0], sums[:, s, D:D + HEADS], ALU.mult).then_inc(q.handle, 1)
                        wait_apart(dve, apart_dve, (q.handle, q.after(4 * t + 1)))
                        dve.tensor_tensor(den[:, s], den[:, s], e[:, s, 1], ALU.add).then_inc(q.handle, 1)
                        wait_apart(dve, apart_dve, (q.handle, q.after(4 * t + 2)))
                        dve.tensor_scalar(den[:, s], den[:, s], 1e-16, None, ALU.max).then_inc(q.handle, 1)
                        wait_apart(dve, apart_dve, (q.handle, q.after(4 * t + 3)))
                        dve.reciprocal(den[:, s], den[:, s]).then_inc(q.handle, 1)
                        wait_apart(dve, apart_dve, (q.handle, q.after(4 * t + 4)))
                        dve.tensor_tensor(coef[:, s, 0], e[:, s, 0], den[:, s], ALU.mult)
                        dve.tensor_tensor(coef[:, s, 1], e[:, s, 1], den[:, s], ALU.mult).then_inc(g["norm"].handle, 1)

                    def mix(t, s, r):
                        b = s % 2
                        wait_apart(dve, apart_dve, (g["norm"].handle, g["norm"].after(t + 1)))
                        dve.tensor_tensor(heads(far[:, b]), heads(sums[:, s, 0:D]), wide(coef[:, s, 0]), ALU.mult)\
                           .then_inc(g["combined"].handle, 1)
                        dve.wait_ge(g["placed"].handle, g["placed"].after(t + 1))
                        wait_apart(dve, apart_dve, (g["combined"].handle, g["combined"].after(t + 1)))
                        if later(t, 2):
                            wait_apart(dve, apart_dve, (g["out_hi"].handle, g["out_hi"].after(t - 1)))
                        dve.tensor_tensor(mixed[:, b], far[:, b], near2[:, b], ALU.add).then_inc(g["product"].handle, 1)

                    def finish(t, s, r):
                        b = s % 2
                        dve.wait_ge(g["out_hi"].handle, g["out_hi"].after(t + 1))
                        dve.scalar_tensor_tensor(elu[:, b], ex[:, b], -1.0, pos[:, b], ALU.add, ALU.add)\
                           .then_inc(g["out_sum"].handle, 1)
                        wait_apart(dve, apart_dve, (g["out_sum"].handle, g["out_sum"].after(t + 1)))
                        if later(t, UNROLL):
                            wait_apart(dve, apart_dve, (store[s].handle, store[s].after(16 * r)))
                        dve.tensor_tensor(res[:, s], elu[:, b], rest[:, s], ALU.add).then_inc(g["out_lo"].handle, 1)
                    pipelined(dve, N_TILES, [(0, own_score), (2, finish), (1, coefficients), (1, mix)])

        def clear_sums():
            n = 8
            with ExitStack() as local:
                zero = sb("zero", [P, n, D + 2 * HEADS], f32, local)
                block = local.enter_context(nc.Block())
                v0 = sig["v_step"]

                @block.vector
                def _(dve):
                    dve.memset(zero[:], 0.0).then_inc(v0.handle, 1)
                    dve.wait_ge(v0.handle, v0.after(1))
                    dve.memset(zero[:, :, D + HEADS:], LOW).then_inc(v0.handle, 1)

                @block.sync
                def _(sp):
                    wait_apart(sp, apart_sp, (v0.handle, v0.after(2)))
                    for table, width in ((AGG_D, D), (AGG_S, D), (AGG_A, D + 2 * HEADS)):
                        for t in range(0, N_TILES, n):
                            sp.dma_start(table[t * P:(t + n) * P, :].rearrange("(t p) n -> p t n", p=P),
                                         zero[:, :, 0:width]).then_inc(once.handle, 16)
                    wait_apart(sp, apart_sp, (once.handle, once.after(16 * 3 * N_TILES // n)))
            v0.passed(2)
            once.passed(16 * 3 * N_TILES // n)

        own_in = [signal(f"own_in{s}") for s in range(UNROLL)]
        put_sems = [signal(f"put{s}") for s in range(2 * UNROLL)]
        total = sb("total", [P, N_TILES], f32)
        lane_col = sb("lane_col", [P, N_CHUNKS], f32)
        tile_col = sb("tile_col", [P, N_CHUNKS], f32)

        def flat(a, h):
            return bass.AP(a.tensor, h * HALF * EDGES, [[EDGES, HALF], [1, P + 1]])

        def by_source(h):
            return bass.AP(SORTED.tensor, 2 * h * HALF * EDGES, [[2 * EDGES, HALF], [1, 2 * (P + 1)]])

        def row(a):
            return a.rearrange("(o n) -> o n", o=1)
        dst_windows, src_windows = ([flat(a, h) for h in range(2)] for a in (dst_list, src_list))
        constants()
        clear_sums()
        edge_columns(src_windows, dst_windows, IDX_S)
        count_keys(inv_s, False, lane_col, tile_col, total)
        order_edges(lane_col, tile_col, total)
        edge_columns(dst_windows, src_windows, IDX_D)
        count_keys(inv_d, True, lane_col, tile_col, total)
        select_matrices()

        for layer in range(3):
            split_weights([(Ws_neigh[layer], w_out, False), (Ws_self[layer], w_own, False)],
                          [(bs[layer:layer + 1, :], bias_own)])
            if layer == 0:
                dense(x_in=x, ht=True)
            else:
                dense(own=U, agg=AGG_D, inverse=inv_d, norm=False, ht=True)
            aggregate(IDX_D, AGG_D, own_row=True)
        split_weights([(W1, w_out, True)], [(row(b1), bias_out)])
        dense(x_in=x, own=U, agg=AGG_D, inverse=inv_d, log_map=True, x_out=X1)
        aggregate(IDX_D, AGG_D)
        split_weights([(wn, w_out, False), (wc, w_own, False)], [(row(b2), bias_own)])
        dense(x_in=X1, agg=AGG_D, inverse=inv_d, exp_map=True, x_out=X2, ht=True)
        edge_columns([by_source(h) for h in range(2)], None, IDX_S)
        select_matrices()
        aggregate(IDX_S, AGG_S, own_row=True)
        split_weights([(W_l, w_out, False), (W_r, w_out2, False)],
                      [(row(att.rearrange("h k -> (h k)")), att_row), (row(b3), bias_out)])
        dense(x_in=X2, own=U, agg=AGG_S, inverse=inv_s, attention=True)
        edge_columns(dst_windows, src_windows, IDX_D)
        select_matrices()
        score = sb("score", [P, N_CHUNKS, HEADS], f32)
        top = sb("top", [P, N_CHUNKS, HEADS], f32)
        weight = sb("weight", [P, N_CHUNKS, HEADS], f32)
        attention_scores(score)
        attention_maxima(score, top, weight)
        attention_sums(top, weight)
        attention_output()


_INS = ["x", "src", "dst", "L0_gnn_Ws_self", "L0_gnn_Ws_neigh", "L0_gnn_bs", "L1_gnn_W", "L1_gnn_b", "L2_gnn_wc",
        "L2_gnn_wn", "L2_gnn_bias", "L3_gnn_W_l", "L3_gnn_W_r", "L3_gnn_att", "L3_gnn_bias"]


def kernel(**inputs):
    import numpy as np
    import concourse.bacc as bacc
    from concourse.bass_utils import run_bass_kernel_spmd

    nc = bacc.Bacc("TRN2", target_bir_lowering=False, num_devices=1)
    arrays, args = {}, []
    for name in _INS:
        a = np.ascontiguousarray(inputs[name])
        if name == "x":
            a = np.concatenate([a, np.zeros((N_PAD - N_NODES, D), a.dtype)])
        if name in ("src", "dst"):
            extra = np.minimum(N_NODES + np.arange(E_PAD - N_EDGES), N_PAD - 1).astype(a.dtype)
            edge = np.full((1,), -1, a.dtype)
            a = np.concatenate([edge, a, extra, edge])
        arrays[f"in_{name}"] = a
        args.append(nc.dram_tensor(f"in_{name}", a.shape, mybir.dt.from_np(a.dtype), kind="ExternalInput").ap())
    out = nc.dram_tensor("out_0", (N_PAD, D), mybir.dt.float32, kind="ExternalOutput").ap()

    def scratch(name, shape, dtype):
        return nc.dram_tensor(name, shape, dtype, kind="Internal").ap()

    gnn_program(nc, *args, out, scratch)
    r = run_bass_kernel_spmd(nc, [arrays], core_ids=[0])
    return r.results[0]["out_0"][:N_NODES]
```

```python
import concourse.bass as bass
from concourse import mybir
from contextlib import ExitStack

P = 128
D = 512
N_NODES = 10000
N_EDGES = 20000
HEADS = 8
HEAD_DIM = D // HEADS
UNROLL = 4
N_TILES = -(-N_NODES // (P * UNROLL)) * UNROLL
N_PAD = N_TILES * P
N_CHUNKS = -(-(N_EDGES + N_PAD - N_NODES) // (P * 2 * UNROLL)) * 2 * UNROLL
E_PAD = N_CHUNKS * P
HALF = N_CHUNKS // 2
BANK = 512
KT = D // P
W_SCALE = 256.0
EPS_LN = 1e-5
EPS_HYP = 1e-7
CLIP_HYP = 1.0 - 1e-7
LOW = -1e30


class Signal:

    def __init__(self, handle):
        self.handle = handle
        self.base = 0

    def after(self, n):
        return self.base + n

    def passed(self, n):
        self.base += n


def pipelined(eng, n, steps, unroll=UNROLL, end=0):
    rounds = n // unroll

    def body(i, j):
        for lag, step in steps:
            s, back = (j - lag) % unroll, (j - lag) // unroll
            if type(i) is int and not 0 <= i + back < rounds:
                continue
            step((i + back) * unroll + s, s, i + back)

    for i in (0, 1):
        for j in range(unroll):
            body(i, j)
    with eng.Fori(2, rounds - end) as i:
        for j in range(unroll):
            body(i, j)
    for i in range(rounds - end, rounds + 1 + (max(lag for lag, _ in steps) - 1) // unroll):
        for j in range(unroll):
            body(i, j)


def wait_apart(eng, step_sem, *waits):
    for sem, value in waits:
        eng.wait_ge(sem, value)
    eng.sem_inc(step_sem, 1)


def gnn_program(nc, x, src_list, dst_list, Ws_self, Ws_neigh, bs, W1, b1, wc, wn, b2, W_l, W_r, att, b3,
                out, dram):
    f32, f16, i32 = mybir.dt.float32, mybir.dt.float16, mybir.dt.int32
    ACT, ALU, AX = mybir.ActivationFunctionType, mybir.AluOpType, mybir.AxisListType

    def later(t, depth):
        return type(t) is not int or t >= depth

    Z = dram("Z", (N_PAD, 2 * D), f16)
    U = dram("U", (N_PAD, D), f32)
    HT = dram("HT", (N_TILES, P, 2 * D), f16)
    X1 = dram("X1", (N_PAD, D), f32)
    X2 = dram("X2", (N_PAD, D), f32)
    AGG = dram("AGG", (E_PAD + 1, D), f32)
    AGG_A = dram("AGG_A", (E_PAD + 1, D + 2 * HEADS), f32)
    XL = dram("XL", (N_PAD, D), f32)
    XR = dram("XR", (N_PAD, D), f32)
    XH = dram("XH", (N_PAD, D), f32)
    SORTED = dram("SORTED", (E_PAD, 2), i32)

    ctx = ExitStack()
    with ctx:
        made = {}

        def sb(name, shape, dt, where=ctx):
            made[name] = made.get(name, 0) + 1
            if made[name] > 1:
                name = f"{name}_{made[name]}"
            return where.enter_context(nc.sbuf_tensor(name, shape, dt))

        def signal(name):
            return Signal(ctx.enter_context(nc.semaphore(name)))

        ident = sb("ident", [P, P], f32)
        ident16 = sb("ident16", [P, P], f16)
        ones = sb("ones", [P, P], f32)
        below = sb("below", [P, P], f32)
        earlier = sb("earlier", [P, P], f32)
        lane_row = sb("lane_row", [P, P], f32)
        tile_row = sb("tile_row", [P, N_TILES], f32)
        later_chunk = sb("later_chunk", [HALF, 2, N_CHUNKS], f32)
        chunk_row = sb("chunk_row", [HALF, 2], f32)
        neg_half = sb("neg_half", [P, 1], f32)
        half = sb("half", [P, 1], f32)
        SEL = sb("SEL", [P, N_CHUNKS, P], f16)
        key_col = sb("key_col", [P, N_CHUNKS], f32)
        val_col = sb("val_col", [P, N_CHUNKS], f32)
        order_d, order_s = (
            {"value": sb(f"value_{o}", [P, N_CHUNKS], i32),
             "key": sb(f"key_{o}", [P, N_CHUNKS], i32),
             "last": sb(f"last_{o}", [P, N_TILES], i32),
             "first": sb(f"first_{o}", [P, N_TILES], f32),
             "inverse": sb(f"inverse_{o}", [P, N_TILES], f32),
             "flow": sb(f"flow_{o}", [HALF, 2, N_CHUNKS], f32),
             "join": sb(f"join_{o}", [HALF, 2], i32)}
            for o in ("d", "s"))
        w_own = sb("w_own", [P, 2, KT, D], f16)
        w_out = sb("w_out", [P, 2, KT, D], f16)
        w_out2 = sb("w_out2", [P, 2, KT, D], f16)
        bias_own = sb("bias_own", [P, D], f32)
        bias_out = sb("bias_out", [P, D], f32)
        att_row = sb("att_row", [P, D], f32)
        own_scores = sb("own_scores", [P, N_TILES, HEADS], f32)
        psum = ctx.enter_context(nc.psum_tensor("psum", [P, 8 * BANK], f32))
        banks = [psum[:, i * BANK:(i + 1) * BANK] for i in range(8)]

        load = [signal(f"load{s}") for s in range(UNROLL)]
        store = [signal(f"store{s}") for s in range(UNROLL)]
        gather = [signal(f"gather{s}") for s in range(UNROLL)]
        kept = [signal(f"kept{s}") for s in range(UNROLL)]
        scatter = [signal(f"scatter{s}") for s in range(UNROLL)]
        index = [signal(f"index{s}") for s in range(2)]
        once = signal("once")
        apart_sp, apart_dve, apart_pool, apart_act = (signal(f"apart{n}").handle for n in range(4))
        names = ("combined", "stats", "aggr", "rstd", "bias_ln", "eps_added", "h_done", "transposed", "hi_done",
                 "lo_done", "product", "out_hi", "out_lo", "out_sum", "squares", "norm", "summed", "carry_hi", "carry_lo",
                 "sums_out", "own_product", "own_out", "v_step", "a_step", "p_step", "t_step",
                 "onehot", "counted", "ranked", "placed", "weighed", "w_hi", "w_lo", "den_out",
                 "diag_done", "keys_row", "sel_done", "based", "looked", "pow_step", "x_step", "y_step")
        sig = {n: signal(n) for n in names}

        def chain(eng, ins, s):
            ins.then_inc(s.handle, 1)
            s.base += 1
            eng.wait_ge(s.handle, s.base)

        def constants():
            with nc.Block() as block:
                @block.gpsimd
                def _(pool):
                    p = sig["p_step"]
                    chain(pool, pool.memset(ones[:], 1.0), p)
                    chain(pool, pool.memset(neg_half[:], -0.5), p)
                    chain(pool, pool.memset(half[:], 0.5), p)
                    chain(pool, pool.affine_select(out=ident[:], in_=ones[:], compare_op=ALU.is_equal, fill=0.0,
                                                   base=0, pattern=[[-1, P]], channel_multiplier=1), p)
                    chain(pool, pool.affine_select(out=below[:], in_=ones[:], compare_op=ALU.is_gt, fill=0.0,
                                                   base=0, pattern=[[1, P]], channel_multiplier=-1), p)
                    chain(pool, pool.affine_select(out=earlier[:], in_=ones[:], compare_op=ALU.is_gt, fill=0.0,
                                                   base=0, pattern=[[-1, P]], channel_multiplier=1), p)
                    chain(pool, pool.tensor_copy(ident16[:], ident[:]), p)
                    chain(pool, pool.memset(later_chunk[:], 1.0), p)
                    for h in range(2):
                        chain(pool, pool.affine_select(out=later_chunk[:, h], in_=later_chunk[:, h], compare_op=ALU.is_gt,
                                                       fill=0.0, base=-h * HALF, pattern=[[1, N_CHUNKS]],
                                                       channel_multiplier=-1), p)
                    chain(pool, pool.iota(chunk_row[:], pattern=[[HALF * P, 2]], base=-1, channel_multiplier=P,
                                          allow_small_or_imprecise_dtypes=True), p)
                    chain(pool, pool.iota(lane_row[:], pattern=[[1, P]], base=0, channel_multiplier=0,
                                          allow_small_or_imprecise_dtypes=True), p)
                    chain(pool, pool.iota(tile_row[:], pattern=[[1, N_TILES]], base=0, channel_multiplier=0,
                                          allow_small_or_imprecise_dtypes=True), p)

        def edge_columns(keys_dram, vals_dram, order):
            with ExitStack() as local:
                rows = sb("edge_rows", [HALF, 2, 2, P], i32, local)
                rowsf = sb("edge_rowsf", [HALF, 2, 2, P], f32, local)
                diag = sb("edge_diag", [HALF, 2, HALF], f32, local)
                scrap = sb("edge_scrap", [HALF, 2, P], f32, local)
                ends = sb("edge_ends", [HALF, 2], f32, local)
                block = local.enter_context(nc.Block())
                n_loads = 2 if vals_dram is None else 4
                parts = rows.rearrange("p h k e -> p h (k e)").rearrange("p h (e k) -> p h k e", k=2) \
                    if vals_dram is None else rows[:]

                @block.sync
                def _(sp):
                    for h in range(2):
                        if vals_dram is None:
                            sp.dma_start(rows[:, h].rearrange("p k e -> p (k e)"), keys_dram[h]).then_inc(once.handle, 16)
                        else:
                            sp.dma_start(rows[:, h, 0], keys_dram[h]).then_inc(once.handle, 16)
                            sp.dma_start(rows[:, h, 1], vals_dram[h]).then_inc(once.handle, 16)

                @block.tensor
                def _(pe):
                    pe.wait_ge(sig["v_step"].handle, sig["v_step"].after(1))
                    for h in range(2):
                        for which in range(2):
                            last = nc.tensor.transpose(banks[which][:, h * HALF:(h + 1) * HALF],
                                                       rowsf[:, h, which], ident[0:HALF, 0:HALF])
                    last.then_inc(sig["t_step"].handle, 1)
                    pe.wait_ge(sig["v_step"].handle, sig["v_step"].after(3))
                    nc.tensor.matmul(banks[2][0:HALF, 0:N_CHUNKS], ones[0:HALF, 0:HALF],
                                     diag[:].rearrange("p h c -> p (h c)"), start=True, stop=True)\
                      .then_inc(sig["t_step"].handle, 1)

                @block.vector
                def _(dve):
                    v = Signal(sig["v_step"].handle)
                    v.base = sig["v_step"].base
                    dve.wait_ge(once.handle, once.after(16 * n_loads))
                    chain(dve, dve.tensor_copy(rowsf[:], parts), v)
                    for h in range(2):
                        chain(dve, dve.tensor_scalar(diag[:, h], ident[0:HALF, 0:HALF], rowsf[:, h, 0, 0:1], None,
                                                     ALU.mult), v)
                    for h in range(2):
                        chain(dve, dve.scalar_tensor_tensor(scrap[:, h], rowsf[:, h, 0], rowsf[:, h, 0, 0:1],
                                                            ones[0:HALF, :], ALU.is_equal, ALU.mult,
                                                            accum_out=ends[:, h:h + 1]), v)
                    chain(dve, dve.tensor_tensor(order["join"][:], ends[:], chunk_row[:], ALU.add), v)
                    dve.wait_ge(sig["t_step"].handle, sig["t_step"].after(1))
                    chain(dve, dve.tensor_copy(key_col[:], banks[0][:, 0:N_CHUNKS]), v)
                    chain(dve, dve.tensor_copy(val_col[:], banks[1][:, 0:N_CHUNKS]), v)
                    chain(dve, dve.tensor_copy(order["key"][:], key_col[:]), v)
                    chain(dve, dve.tensor_copy(order["value"][:], val_col[:]), v)
                    dve.wait_ge(sig["t_step"].handle, sig["t_step"].after(2))
                    for h in range(2):
                        chain(dve, dve.scalar_tensor_tensor(order["flow"][:, h], banks[2][0:HALF, 0:N_CHUNKS],
                                                            rowsf[:, h, 0, P - 1:P], later_chunk[:, h],
                                                            ALU.is_equal, ALU.mult), v)
            once.passed(16 * n_loads)
            sig["v_step"].passed(12)
            sig["t_step"].passed(2)

        def select_matrices():
            with ExitStack() as local:
                diag = sb("diag", [P, 2, UNROLL, P], f32, local)
                rounds = N_CHUNKS // UNROLL
                block = local.enter_context(nc.Block())
                dg, kr, sd = sig["diag_done"], sig["keys_row"], sig["sel_done"]

                def body_v(dve, q, half_, b):
                    if later(q, 2):
                        dve.wait_ge(kr.handle, kr.after(q - 1))
                    for j in range(UNROLL):
                        ins = dve.tensor_scalar(diag[:, b, j, :], ident[:], key_col[:, bass.ds(q * UNROLL + j, 1)],
                                                None, ALU.mult)
                    ins.then_inc(dg.handle, 1)

                def body_s(dve, q, half_, b):
                    dve.wait_ge(kr.handle, kr.after(q + 1))
                    for j in range(UNROLL):
                        c = bass.ds(q * UNROLL + j, 1)
                        ins = dve.tensor_scalar(SEL[:, c, :].rearrange("p o m -> p (o m)"), banks[b][:, j * P:(j + 1) * P],
                                                key_col[:, c], None, ALU.is_equal)
                    ins.then_inc(sd.handle, 1)

                @block.vector
                def _(dve):
                    body_v(dve, 0, 0, 0)
                    body_v(dve, 1, 0, 1)
                    body_s(dve, 0, 0, 0)
                    body_v(dve, 2, 0, 0)
                    body_s(dve, 1, 0, 1)
                    with dve.Fori(1, rounds // 2 - 1) as i:
                        body_v(dve, 2 * i + 1, 0, 1)
                        body_s(dve, 2 * i, 0, 0)
                        body_v(dve, 2 * i + 2, 0, 0)
                        body_s(dve, 2 * i + 1, 0, 1)
                    body_v(dve, rounds - 1, 0, 1)
                    body_s(dve, rounds - 2, 0, 0)
                    body_s(dve, rounds - 1, 0, 1)

                @block.tensor
                def _(pe):
                    def body(q, b):
                        pe.wait_ge(dg.handle, dg.after(q + 1))
                        if later(q, 2):
                            pe.wait_ge(sd.handle, sd.after(q - 1))
                        nc.tensor.matmul(banks[b][:], ones[:], diag[:, b].rearrange("p j m -> p (j m)"),
                                         start=True, stop=True).then_inc(kr.handle, 1)
                    body(0, 0)
                    body(1, 1)
                    with pe.Fori(1, rounds // 2) as i:
                        body(2 * i, 0)
                        body(2 * i + 1, 1)
            for s in (dg, kr, sd):
                s.passed(rounds)

        def count_keys(order, clamp, lane_col, tile_col):
            with ExitStack() as local:
                total = sb("total", [P, N_TILES], f32, local)
                col_sum = sb("col_sum", [P, N_TILES], f32, local)
                scan = sb("scan", [P, N_TILES], f32, local)
                end = sb("end", [P, N_TILES], f32, local)
                empty = sb("empty", [P, N_TILES], f32, local)
                inverse, first = order["inverse"], order["first"]
                key_i = sb("key_i", [P, 2, N_CHUNKS], i32, local)
                lane_hot = sb("lane_hot", [P, UNROLL, P], f16, local)
                tile_hot = sb("tile_hot", [P, UNROLL, N_TILES], f16, local)
                block = local.enter_context(nc.Block())
                hot, cnt, v0 = sig["onehot"], sig["counted"], sig["v_step"]

                @block.vector
                def _(dve):
                    v = Signal(v0.handle)
                    v.base = v0.base
                    chain(dve, dve.tensor_copy(key_i[:, 0, :], key_col[:]), v)
                    chain(dve, dve.tensor_scalar(key_i[:, 1, :], key_i[:, 0, :], P - 1, None, ALU.bitwise_and), v)
                    chain(dve, dve.tensor_copy(lane_col[:], key_i[:, 1, :]), v)
                    chain(dve, dve.tensor_scalar(key_i[:, 1, :], key_i[:, 0, :], 7, None, ALU.arith_shift_right), v)
                    chain(dve, dve.tensor_copy(tile_col[:], key_i[:, 1, :]), v)

                    def step(c, s, r):
                        if later(c, UNROLL):
                            dve.wait_ge(cnt.handle, cnt.after(c - UNROLL + 1))
                        dve.tensor_scalar(lane_hot[:, s, :], lane_row[:], lane_col[:, bass.ds(c, 1)], None, ALU.is_equal)
                        dve.tensor_scalar(tile_hot[:, s, :], tile_row[:], tile_col[:, bass.ds(c, 1)], None,
                                          ALU.is_equal).then_inc(hot.handle, 1)
                    pipelined(dve, N_CHUNKS, [(0, step)])
                    dve.wait_ge(cnt.handle, cnt.after(N_CHUNKS))
                    chain(dve, dve.tensor_copy(total[:], banks[0][:, 0:N_TILES]), v)
                    if clamp:
                        chain(dve, dve.tensor_scalar(inverse[:], total[:], 1.0, None, ALU.max), v)
                    else:
                        chain(dve, dve.tensor_copy(inverse[:], total[:]), v)
                    chain(dve, dve.reciprocal(inverse[:], inverse[:]), v)
                    dve.wait_ge(cnt.handle, cnt.after(N_CHUNKS + 1))
                    chain(dve, dve.tensor_copy(col_sum[:], banks[1][:, 0:N_TILES]), v)
                    chain(dve, dve.tensor_tensor_scan(scan[:], ones[:, 0:N_TILES], col_sum[:], 0.0, ALU.mult, ALU.add), v)
                    chain(dve, dve.tensor_tensor(scan[:], scan[:], col_sum[:], ALU.subtract), v)
                    chain(dve, dve.scalar_tensor_tensor(first[:], banks[2][:, 0:N_TILES], 1.0, scan[:], ALU.mult,
                                                        ALU.add), v)
                    chain(dve, dve.tensor_tensor(end[:], first[:], total[:], ALU.add), v)
                    chain(dve, dve.tensor_scalar(empty[:], total[:], 0.5, None, ALU.is_lt), v)
                    chain(dve, dve.tensor_scalar(col_sum[:], end[:], -1.0, E_PAD + 1.0, ALU.mult, ALU.add), v)
                    chain(dve, dve.tensor_tensor(empty[:], empty[:], col_sum[:], ALU.mult), v)
                    chain(dve, dve.scalar_tensor_tensor(order["last"][:], end[:], -1.0, empty[:], ALU.add, ALU.add), v)

                @block.tensor
                def _(pe):
                    for c in range(N_CHUNKS):
                        s = c % UNROLL
                        pe.wait_ge(hot.handle, hot.after(c + 1))
                        nc.tensor.matmul(banks[0][:, 0:N_TILES], lane_hot[:, s, :], tile_hot[:, s, :],
                                         start=c == 0, stop=c == N_CHUNKS - 1).then_inc(cnt.handle, 1)
                    pe.wait_ge(v0.handle, v0.after(6))
                    nc.tensor.matmul(banks[1][:, 0:N_TILES], ones[:], total[:], start=True, stop=True)
                    nc.tensor.matmul(banks[2][:, 0:N_TILES], below[:], total[:], start=True, stop=True)\
                      .then_inc(cnt.handle, 1)
            v0.passed(8 + 9)
            hot.passed(N_CHUNKS)
            cnt.passed(N_CHUNKS + 1)

        def weights_room(where, jobs):
            return sb("w_raw", [P, len(jobs), KT, D], f32, where) if jobs else None

        def load_weights(sp, raw, jobs, rows):
            for n, (w, _, _) in enumerate(jobs):
                sp.dma_start(raw[:, n], w.rearrange("(t p) n -> p t n", p=P)).then_inc(once.handle, 16)
            for row, tile in rows:
                sp.dma_start(tile[:], row.to_broadcast([P, D])).then_inc(once.handle, 16)

        def turn_weights(pe, raw, jobs, rows):
            if any(turn for _, _, turn in jobs):
                pe.wait_ge(once.handle, once.after(16 * (len(jobs) + len(rows))))
                for k in range(KT):
                    for m in range(KT):
                        last = nc.tensor.transpose(banks[4 + k][:, m * P:(m + 1) * P], raw[:, 0, m, k * P:(k + 1) * P],
                                                   ident[:])
                last.then_inc(sig["t_step"].handle, 1)

        def high_weights(act, raw, jobs, rows):
            if jobs or rows:
                act.wait_ge(once.handle, once.after(16 * (len(jobs) + len(rows))))
            for n, (_, w, turn) in enumerate(jobs):
                if turn:
                    act.wait_ge(sig["t_step"].handle, sig["t_step"].after(1))
                for k in range(KT):
                    act.activation(w[:, 0, k, :], banks[4 + k][:] if turn else raw[:, n, k, :], ACT.Copy, scale=W_SCALE)\
                       .then_inc(sig["w_hi"].handle, 1)

        def low_weights(dve, raw, jobs, rows):
            for n, (_, w, turn) in enumerate(jobs):
                for k in range(KT):
                    dve.wait_ge(sig["w_hi"].handle, sig["w_hi"].after(n * KT + k + 1))
                    dve.scalar_tensor_tensor(w[:, 1, k, :], banks[4 + k][:] if turn else raw[:, n, k, :], W_SCALE,
                                             w[:, 0, k, :], ALU.mult, ALU.subtract).then_inc(sig["w_lo"].handle, 1)

        def weights_passed(jobs, rows):
            once.passed(16 * (len(jobs) + len(rows)))
            sig["w_hi"].passed(KT * len(jobs))
            sig["w_lo"].passed(KT * len(jobs))
            sig["t_step"].passed(any(turn for _, _, turn in jobs))

        def split_weights(jobs, rows):
            with ExitStack() as local:
                raw = weights_room(local, jobs)
                block = local.enter_context(nc.Block())

                @block.sync
                def _(sp):
                    load_weights(sp, raw, jobs, rows)

                @block.tensor
                def _(pe):
                    turn_weights(pe, raw, jobs, rows)

                @block.scalar
                def _(act):
                    high_weights(act, raw, jobs, rows)

                @block.vector
                def _(dve):
                    low_weights(dve, raw, jobs, rows)
            weights_passed(jobs, rows)

        def products(bank_, left, w, ks, first, last):
            for k in ks:
                for a, b in ((0, 0), (1, 0), (0, 1)):
                    ins = nc.tensor.matmul(bank_[:], left[:, a, k, :], w[:, b, k, :],
                                           start=first and k == ks[0] and (a, b) == (0, 0),
                                           stop=last and k == ks[-1] and (a, b) == (0, 1))
            return ins

        def dense(x_in=None, own=None, order=None, exp_map=False, norm=True, log_map=False,
                  x_out=None, ht=False, attention=False, jobs=(), rows_=()):
            ins_of = [a for a in (x_in, own) if a is not None]
            combine = order is not None
            inverse = order["inverse"] if combine else None
            nl = len(ins_of)
            z_out = not attention
            ns = ht + (1 if z_out else 3)
            V = 2 * UNROLL
            F = 4 if exp_map else 2 if combine else 0
            L = F + 2 if exp_map or log_map else F + 1
            R = L + 6 if log_map else L + 2

            def tiles(eng, steps):
                pipelined(eng, N_TILES,
                          [(lag, lambda t, w, r, step=step: step(t, w % UNROLL, 2 * r + w // UNROLL, w)) for lag, step in steps],
                          V)
            with ExitStack() as local:
                inX = sb("inX", [P, UNROLL, D], f32, local) if x_in is not None else None
                inU = sb("inU", [P, UNROLL, D], f32, local) if own is not None else None
                inG = sb("inG", [P, UNROLL, D], f32, local) if combine else None
                place = sb("place", [P, UNROLL], i32, local)
                raw = weights_room(local, jobs)
                y = sb("y", [P, UNROLL, D], f32, local) if combine else inX
                part = sb("part", [P, 2, D], f32, local)
                scrap = sb("scrap", [P, 2, D], f32, local)
                h = sb("h", [P, 2, D], f32, local)
                hT = sb("hT", [P, UNROLL, 2, KT, P], f16, local)
                zout = sb("zout", [P, UNROLL, 2, D], f16, local) if z_out else None
                zsum = sb("zsum", [P, UNROLL, D], f32, local) if log_map else None
                xl = sb("xl", [P, UNROLL, D], f32, local) if attention else None
                xr = sb("xr", [P, UNROLL, D], f32, local) if attention else None
                xh = sb("xh", [P, UNROLL, D], f32, local) if attention else None
                both = sb("both", [P, 2, D], f32, local) if attention else None
                leaky = sb("leaky", [P, 2, D], f32, local) if attention else None
                six = sb("six", [P, V, 6], f32, local)
                mv = sb("mv", [P, V, 2], f32, local)
                small = sb("small", [P, V, 24], f32, local)
                VAR, RSTD, LNB, SS, NORM, NC_, REC, TANH, FAC = 0, 1, 2, 3, 4, 6, 8, 10, 11
                Q, LNQ, N2, SER, MASK, DIF, ONEP = 12, 13, 14, 15, 16, 17, 18

                nb = 4 if log_map else 2

                def sm(w, k, n=1):
                    return small[:, w, k:k + n]
                block = local.enter_context(nc.Block())
                g = sig
                rows = lambda t: bass.ds(t * P, P)

                @block.sync
                def _(sp):
                    def loads(t, s, r, w):
                        if later(t, UNROLL):
                            used = g["combined"] if combine else g["h_done"]
                            wait_apart(sp, apart_sp, (used.handle, used.after(t - UNROLL + 1)))
                        if x_in is not None:
                            sp.dma_start(inX[:, s], x_in[rows(t), :]).then_inc(load[s].handle, 16)
                        if own is not None:
                            sp.dma_start(inU[:, s], own[rows(t), :]).then_inc(load[s].handle, 16)

                    def stores(t, s, r, w):
                        wait_apart(sp, apart_sp, (g["out_lo"].handle, g["out_lo"].after(t + 1)))
                        if z_out:
                            sp.dma_start(Z[rows(t), :], zout[:, s].rearrange("p a n -> p (a n)")).then_inc(store[s].handle, 16)
                        else:
                            wait_apart(sp, apart_sp, (g["out_hi"].handle, g["out_hi"].after(t + 1)))
                            sp.dma_start(XL[rows(t), :], xl[:, s]).then_inc(store[s].handle, 16)
                            sp.dma_start(XR[rows(t), :], xr[:, s]).then_inc(store[s].handle, 16)
                            wait_apart(sp, apart_sp, (g["x_step"].handle, g["x_step"].after(t + 1)))
                            sp.dma_start(XH[rows(t), :], xh[:, s]).then_inc(store[s].handle, 16)
                        if ht:
                            sp.dma_start(HT[bass.ds(t, 1)].rearrange("o p n -> (o p) n"),
                                         hT[:, s].rearrange("p a k n -> p (a k n)")).then_inc(store[s].handle, 16)

                    def keep(t, s, r, w):
                        wait_apart(sp, apart_sp, (g["combined"].handle, g["combined"].after(t + 1)))
                        sp.dma_start(x_out[rows(t), :], y[:, s]).then_inc(kept[s].handle, 16)
                    load_weights(sp, raw, jobs, rows_)
                    tiles(sp, ([(F + 2, keep)] if x_out is not None else []) + [(R + 1, stores), (0, loads)])
                    for s in range(UNROLL):
                        wait_apart(sp, apart_sp, (store[s].handle, store[s].after(16 * ns * N_TILES // UNROLL)))
                        if x_out is not None:
                            wait_apart(sp, apart_sp, (kept[s].handle, kept[s].after(16 * N_TILES // UNROLL)))

                @block.vector
                def _(dve):
                    def combination(t, s, r, w):
                        if nl:
                            wait_apart(dve, apart_dve, (load[s].handle, load[s].after((r + 1) * (16 * nl))))
                        if combine:
                            wait_apart(dve, apart_dve, (gather[s].handle, gather[s].after(16 * (r + 1))))
                        if combine and later(t, UNROLL):
                            dve.wait_ge(g["h_done"].handle, g["h_done"].after(t - UNROLL + 1))
                            if x_out is not None:
                                dve.wait_ge(kept[s].handle, kept[s].after(16 * r))
                            if attention:
                                dve.wait_ge(g["x_step"].handle, g["x_step"].after(t - UNROLL + 1))
                        if exp_map:
                            f = g["v_step"]
                            dve.wait_ge(g["norm"].handle, g["norm"].after(t + 1))
                            dve.reciprocal(sm(w, REC), sm(w, NC_)).then_inc(g["y_step"].handle, 1)
                            dve.wait_ge(g["a_step"].handle, g["a_step"].after(t + 1))
                            wait_apart(dve, apart_dve, (g["y_step"].handle, g["y_step"].after(2 * t + 1)))
                            dve.scalar_tensor_tensor(sm(w, FAC), sm(w, TANH), sm(w, REC), inverse[:, bass.ds(t, 1)],
                                                     ALU.mult, ALU.mult).then_inc(g["y_step"].handle, 1)
                            wait_apart(dve, apart_dve, (g["y_step"].handle, g["y_step"].after(2 * t + 2)))
                            dve.scalar_tensor_tensor(y[:, s], inG[:, s], sm(w, FAC), inX[:, s], ALU.mult,
                                                     ALU.add).then_inc(g["combined"].handle, 1)
                        elif combine and x_in is None:
                            wait_apart(dve, apart_dve)
                            dve.scalar_tensor_tensor(y[:, s], inG[:, s], inverse[:, bass.ds(t, 1)], inU[:, s],
                                                     ALU.mult, ALU.add).then_inc(g["combined"].handle, 1)
                        elif combine:
                            wait_apart(dve, apart_dve)
                            dve.scalar_tensor_tensor(part[:, s % 2], inG[:, s], inverse[:, bass.ds(t, 1)], inU[:, s],
                                                     ALU.mult, ALU.add).then_inc(g["y_step"].handle, 1)
                            dve.wait_ge(g["y_step"].handle, g["y_step"].after(t + 1))
                            dve.tensor_tensor(y[:, s], part[:, s % 2], inX[:, s], ALU.add)\
                               .then_inc(g["combined"].handle, 1)
                        if norm:
                            if combine:
                                dve.wait_ge(g["combined"].handle, g["combined"].after(t + 1))
                            dve.bn_stats(six[:, w], y[:, s]).then_inc(g["stats"].handle, 1)
                            wait_apart(dve, apart_dve, (g["stats"].handle, g["stats"].after(t + 1)))
                            dve.bn_aggr(mv[:, w], six[:, w]).then_inc(g["aggr"].handle, 1)

                    def log_factor(t, s, r, w):
                        v = g["ranked"]
                        dve.wait_ge(g["norm"].handle, g["norm"].after(t + 1))
                        dve.reciprocal(sm(w, REC, 2), sm(w, NC_, 2)).then_inc(v.handle, 1)
                        wait_apart(dve, apart_dve, (v.handle, v.after(2 * t + 1)))
                        dve.tensor_tensor(sm(w, Q), sm(w, REC + 1), sm(w, ONEP), ALU.mult).then_inc(v.handle, 1)

                    def log_factor_end(t, s, r, w):
                        v = g["sel_done"]
                        wait_apart(dve, apart_dve, (g["a_step"].handle, g["a_step"].after(t + 1)))
                        dve.tensor_scalar(sm(w, LNQ), sm(w, LNQ), sm(w, REC), 0.5 / W_SCALE, ALU.mult, ALU.mult).then_inc(v.handle, 1)
                        wait_apart(dve, apart_dve, (v.handle, v.after(2 * t + 1)), (g["placed"].handle, g["placed"].after(t + 1)))
                        dve.scalar_tensor_tensor(sm(w, DIF), sm(w, SER), 1.0 / W_SCALE, sm(w, LNQ), ALU.mult, ALU.subtract).then_inc(v.handle, 1)
                        wait_apart(dve, apart_dve, (v.handle, v.after(2 * t + 2)))
                        dve.scalar_tensor_tensor(sm(w, FAC), sm(w, DIF), sm(w, MASK), sm(w, LNQ), ALU.mult,
                                                 ALU.add).then_inc(g["weighed"].handle, 1)

                    def low(t, s, r, w):
                        dve.wait_ge(g["hi_done"].handle, g["hi_done"].after(t + 1))
                        dve.tensor_tensor(hT[:, s, 1].rearrange("p k n -> p (k n)"), banks[s % 2][:],
                                          hT[:, s, 0].rearrange("p k n -> p (k n)"), ALU.subtract)\
                           .then_inc(g["lo_done"].handle, 1)

                    def results_sum(t, s, r, w):
                        dve.wait_ge(g["weighed"].handle, g["weighed"].after(t + 1))
                        dve.wait_ge(g["product"].handle, g["product"].after(t + 1))
                        if later(t, UNROLL):
                            dve.wait_ge(g["out_lo"].handle, g["out_lo"].after(t - UNROLL + 1))
                        dve.scalar_tensor_tensor(zsum[:, s], banks[2 + s % nb][:], sm(w, FAC), bias_out[:], ALU.mult,
                                                 ALU.add).then_inc(g["out_sum"].handle, 1)

                    def results(t, s, r, w):
                        if log_map:
                            dve.wait_ge(g["out_hi"].handle, g["out_hi"].after(t + 1))
                            dve.tensor_tensor(zout[:, s, 1], zsum[:, s], zout[:, s, 0], ALU.subtract)\
                               .then_inc(g["out_lo"].handle, 1)
                        elif z_out:
                            dve.wait_ge(g["out_hi"].handle, g["out_hi"].after(t + 1))
                            dve.scalar_tensor_tensor(zout[:, s, 1], banks[2 + s % nb][:], 1.0 / W_SCALE, zout[:, s, 0],
                                                     ALU.mult, ALU.subtract).then_inc(g["out_lo"].handle, 1)
                        else:
                            dve.wait_ge(g["product"].handle, g["product"].after(t + 1))
                            if later(t, UNROLL):
                                dve.wait_ge(store[s].handle, store[s].after(r * (16 * ns)))
                                dve.wait_ge(g["p_step"].handle, g["p_step"].after(t - UNROLL + 1))
                            dve.tensor_scalar(xr[:, s], banks[4 + s % 2][:], 1.0 / W_SCALE, None, ALU.mult)\
                               .then_inc(g["out_lo"].handle, 1)
                    def own_score(t, s, r, w):
                        q = g["ranked"]
                        dve.wait_ge(g["p_step"].handle, g["p_step"].after(t + 1))
                        dve.scalar_tensor_tensor(leaky[:, s % 2], both[:, s % 2], 0.2, both[:, s % 2], ALU.mult, ALU.max)\
                           .then_inc(q.handle, 1)
                        wait_apart(dve, apart_dve, (q.handle, q.after(3 * t + 1)))
                        dve.tensor_tensor(both[:, s % 2], leaky[:, s % 2], att_row[:], ALU.mult).then_inc(q.handle, 1)
                        wait_apart(dve, apart_dve, (q.handle, q.after(3 * t + 2)))
                        dve.tensor_reduce(own_scores[:, bass.ds(t, 1), :].rearrange("p o h -> p (o h)"),
                                          both[:, s % 2].rearrange("p (h k) -> p h k", h=HEADS), AX.X, ALU.add)\
                           .then_inc(q.handle, 1)
                    steps = [(F, combination), (R, results), (L, low)]
                    if log_map:
                        steps = [(R, results), (F, combination), (L + 4, log_factor_end), (L + 4, results_sum),
                                 (L + 2, log_factor), (L, low)]
                    if attention:
                        steps.append((R + 1, own_score))
                    low_weights(dve, raw, jobs, rows_)
                    tiles(dve, steps)

                @block.gpsimd
                def _(pool):
                    def gathers(t, s, r, w):
                        q = g["looked"]
                        if later(t, UNROLL):
                            wait_apart(pool, apart_pool, (gather[s].handle, gather[s].after(16 * r)))
                            wait_apart(pool, apart_pool, (g["combined"].handle, g["combined"].after(t - UNROLL + 1)))
                        pool.tensor_copy(place[:, s:s + 1], order["last"][:, bass.ds(t, 1)]).then_inc(q.handle, 1)
                        wait_apart(pool, apart_pool, (q.handle, q.after(t + 1)))
                        pool.indirect_dma_start(out=inG[:, s], out_offset=None, in_=AGG,
                                                in_offset=bass.IndirectOffsetOnAxis(ap=place[:, s:s + 1], axis=0),
                                                bounds_check=E_PAD, oob_is_err=False).then_inc(gather[s].handle, 16)

                    def mean_norm(t, s, r, w):
                        n = g["pow_step"]
                        wait_apart(pool, apart_pool, (g["squares"].handle, g["squares"].after(t + 1)))
                        pool.tensor_tensor(out=sm(w, NORM), in0=sm(w, SS), in1=half[:], op=ALU.pow).then_inc(n.handle, 1)
                        wait_apart(pool, apart_pool, (n.handle, n.after(t + 1)))
                        pool.tensor_scalar(sm(w, NC_), sm(w, NORM), EPS_HYP, None, ALU.max).then_inc(g["norm"].handle, 1)

                    def ln_scale(t, s, r, w):
                        wait_apart(pool, apart_pool, (g["aggr"].handle, g["aggr"].after(t + 1)))
                        pool.tensor_scalar(sm(w, VAR), mv[:, w, 1:2], EPS_LN, None, ALU.add)\
                            .then_inc(g["eps_added"].handle, 1)
                        wait_apart(pool, apart_pool, (g["eps_added"].handle, g["eps_added"].after(t + 1)))
                        pool.tensor_tensor(out=sm(w, RSTD), in0=sm(w, VAR), in1=neg_half[:], op=ALU.pow)\
                            .then_inc(g["rstd"].handle, 1)
                        wait_apart(pool, apart_pool, (g["rstd"].handle, g["rstd"].after(t + 1)))
                        pool.tensor_scalar(sm(w, LNB), mv[:, w, 0:1], sm(w, RSTD), -1.0, ALU.mult, ALU.mult)\
                            .then_inc(g["bias_ln"].handle, 1)

                    def clipped_norm(t, s, r, w):
                        n, m = g["pow_step"], g["p_step"]
                        wait_apart(pool, apart_pool, (g["squares"].handle, g["squares"].after(t + 1)))
                        pool.tensor_tensor(out=sm(w, NORM), in0=sm(w, SS), in1=half[:], op=ALU.pow).then_inc(n.handle, 1)
                        wait_apart(pool, apart_pool, (n.handle, n.after(t + 1)))
                        pool.tensor_scalar(sm(w, NC_), sm(w, NORM), EPS_HYP, CLIP_HYP, ALU.max, ALU.min)\
                            .then_inc(m.handle, 1)
                        wait_apart(pool, apart_pool, (m.handle, m.after(4 * t + 1)))
                        pool.tensor_scalar(sm(w, ONEP), sm(w, NC_), 1.0, None, ALU.add)
                        pool.tensor_scalar(sm(w, NC_ + 1), sm(w, NC_), -1.0, 1.0, ALU.mult, ALU.add)\
                            .then_inc(g["norm"].handle, 1)
                        pool.tensor_scalar(sm(w, MASK), sm(w, NC_), 0.1, None, ALU.is_lt)
                        pool.tensor_tensor(out=sm(w, N2), in0=sm(w, NC_), in1=sm(w, NC_), op=ALU.mult).then_inc(m.handle, 1)
                        wait_apart(pool, apart_pool, (m.handle, m.after(4 * t + 2)))
                        pool.tensor_scalar(sm(w, SER), sm(w, N2), 1.0 / 7, 1.0 / 5, ALU.mult, ALU.add).then_inc(m.handle, 1)
                        wait_apart(pool, apart_pool, (m.handle, m.after(4 * t + 3)))
                        pool.tensor_scalar(sm(w, Q + 8), sm(w, SER), sm(w, N2), 1.0 / 3, ALU.mult, ALU.add).then_inc(m.handle, 1)
                        wait_apart(pool, apart_pool, (m.handle, m.after(4 * t + 4)))
                        pool.tensor_scalar(sm(w, SER), sm(w, Q + 8), sm(w, N2), 1.0, ALU.mult, ALU.add)\
                            .then_inc(g["placed"].handle, 1)

                    def residual(t, s, r, w):
                        wait_apart(pool, apart_pool, (g["h_done"].handle, g["h_done"].after(t + 1)))
                        if later(t, UNROLL):
                            wait_apart(pool, apart_pool, (store[s].handle, store[s].after(r * (16 * ns))))
                        pool.tensor_tensor(out=xh[:, s], in0=y[:, s], in1=h[:, s % 2], op=ALU.add)\
                            .then_inc(g["x_step"].handle, 1)
                    def add(t, s, r, w):
                        wait_apart(pool, apart_pool, (g["out_lo"].handle, g["out_lo"].after(t + 1)))
                        wait_apart(pool, apart_pool, (g["out_hi"].handle, g["out_hi"].after(t + 1)))
                        if later(t, 2):
                            wait_apart(pool, apart_pool, (g["ranked"].handle, g["ranked"].after(3 * (t - 1))))
                        pool.tensor_tensor(out=both[:, s % 2], in0=xl[:, s], in1=xr[:, s], op=ALU.add)\
                            .then_inc(g["p_step"].handle, 1)
                    steps = ([(3, mean_norm)] if exp_map else []) + ([(L + 1, clipped_norm)] if log_map else []) \
                        + ([(0, gathers)] if combine else []) + ([(F, ln_scale)] if norm else []) \
                        + ([(L, residual), (R + 1, add)] if attention else [])
                    if steps:
                        tiles(pool, steps)

                @block.scalar
                def _(act):
                    def mean_squares(t, s, r, w):
                        wait_apart(act, apart_act, (gather[s].handle, gather[s].after(16 * (r + 1))))
                        if later(t, 2):
                            wait_apart(act, apart_act, (g["squares"].handle, g["squares"].after(t - 1)))
                        act.activation(scrap[:, s % 2], inG[:, s], ACT.Square, scale=inverse[:, bass.ds(t, 1)],
                                       accum_out=sm(w, SS)).then_inc(g["squares"].handle, 1)

                    def tanh_norm(t, s, r, w):
                        act.wait_ge(g["norm"].handle, g["norm"].after(t + 1))
                        act.activation(sm(w, TANH), sm(w, NC_), ACT.Tanh).then_inc(g["a_step"].handle, 1)

                    def hidden(t, s, r, w):
                        if later(t, 2):
                            act.wait_ge(g["transposed"].handle, g["transposed"].after(t - 1))
                            if attention:
                                act.wait_ge(g["x_step"].handle, g["x_step"].after(t - 1))
                        if norm:
                            act.wait_ge(g["bias_ln"].handle, g["bias_ln"].after(t + 1))
                            act.activation(h[:, s % 2], y[:, s], ACT.Relu, bias=sm(w, LNB), scale=sm(w, RSTD))\
                               .then_inc(g["h_done"].handle, 1)
                        else:
                            act.wait_ge(g["combined"].handle, g["combined"].after(t + 1))
                            act.activation(h[:, s % 2], y[:, s], ACT.Relu).then_inc(g["h_done"].handle, 1)
                        if log_map:
                            wait_apart(act, apart_act, (g["h_done"].handle, g["h_done"].after(t + 1)))
                            act.activation(scrap[:, s % 2], h[:, s % 2], ACT.Square, accum_out=sm(w, SS))\
                               .then_inc(g["squares"].handle, 1)

                    def high(t, s, r, w):
                        act.wait_ge(g["transposed"].handle, g["transposed"].after(t + 1))
                        if later(t, UNROLL):
                            act.wait_ge(g["product"].handle, g["product"].after(t - UNROLL + 1))
                            if ht:
                                act.wait_ge(store[s].handle, store[s].after(r * (16 * ns)))
                        act.activation(hT[:, s, 0].rearrange("p k n -> p (k n)"), banks[s % 2][:], ACT.Copy)\
                           .then_inc(g["hi_done"].handle, 1)

                    def results(t, s, r, w):
                        if later(t, UNROLL):
                            act.wait_ge(store[s].handle, store[s].after(r * (16 * ns)))
                            if attention:
                                act.wait_ge(g["p_step"].handle, g["p_step"].after(t - UNROLL + 1))
                        if log_map:
                            act.wait_ge(g["out_sum"].handle, g["out_sum"].after(t + 1))
                            act.activation(zout[:, s, 0], zsum[:, s], ACT.Copy).then_inc(g["out_hi"].handle, 1)
                        else:
                            act.wait_ge(g["product"].handle, g["product"].after(t + 1))
                            act.activation(zout[:, s, 0] if z_out else xl[:, s], banks[2 + s % 2][:], ACT.Copy,
                                           scale=1.0 / W_SCALE).then_inc(g["out_hi"].handle, 1)

                    def log_norm(t, s, r, w):
                        act.wait_ge(g["ranked"].handle, g["ranked"].after(2 * t + 2))
                        act.activation(sm(w, LNQ), sm(w, Q), ACT.Ln).then_inc(g["a_step"].handle, 1)
                    steps = [(L, hidden), (L + 5 if log_map else L + 2, results), (L, high)]
                    if exp_map:
                        steps = [(2, mean_squares), (3, tanh_norm)] + steps
                    if log_map:
                        steps = [(L + 3, log_norm)] + steps
                    high_weights(act, raw, jobs, rows_)
                    tiles(act, steps)

                @block.tensor
                def _(pe):
                    def turn(t, s, r, w):
                        pe.wait_ge(g["h_done"].handle, g["h_done"].after(t + 1))
                        if later(t, 2):
                            pe.wait_ge(g["lo_done"].handle, g["lo_done"].after(t - 1))
                        for k in range(KT):
                            last = nc.tensor.transpose(banks[s % 2][:, k * P:(k + 1) * P], h[:, s % 2, k * P:(k + 1) * P],
                                                       ident[:])
                        last.then_inc(g["transposed"].handle, 1)

                    def multiply(t, s, r, w):
                        pe.wait_ge(g["lo_done"].handle, g["lo_done"].after(t + 1))
                        if later(t, nb):
                            b = g["out_sum"] if log_map else g["out_lo"]
                            pe.wait_ge(b.handle, b.after(t - nb + 1))
                            if attention:
                                pe.wait_ge(g["out_hi"].handle, g["out_hi"].after(t - 1))
                        last = products(banks[2 + s % nb], hT[:, s], w_out, range(KT), True, True)
                        if attention:
                            last = products(banks[4 + s % 2], hT[:, s], w_out2, range(KT), True, True)
                        last.then_inc(g["product"].handle, 1)
                    tiles(pe, [(0, turn), (1, multiply)])
            for s in range(UNROLL):
                load[s].passed(16 * nl * N_TILES // UNROLL)
                store[s].passed(16 * ns * N_TILES // UNROLL)
                gather[s].passed(16 * combine * N_TILES // UNROLL)
                kept[s].passed(16 * (x_out is not None) * N_TILES // UNROLL)
            weights_passed(jobs, rows_)
            done = {"looked": combine, "h_done": 1, "transposed": 1, "hi_done": 1, "lo_done": 1, "product": 1, "out_hi": 1, "out_lo": 1,
                    "combined": combine, "stats": norm, "aggr": norm, "rstd": norm, "bias_ln": norm, "eps_added": norm,
                    "squares": exp_map or log_map, "norm": exp_map or log_map, "pow_step": exp_map or log_map,
                    "a_step": exp_map or log_map, "x_step": attention, "out_sum": log_map, "weighed": log_map,
                    "placed": log_map, "sel_done": 2 * log_map, "ranked": 2 * log_map + 3 * attention, "p_step": 4 * log_map + attention,
                    "y_step": 2 * exp_map + (combine and x_in is not None and not exp_map)}
            for name, n in done.items():
                g[name].passed(int(n) * N_TILES)

        def aggregate(order, own=False, jobs=(), rows_=()):
            A = 2 * UNROLL
            with ExitStack() as local:
                rows_in = sb("rows_in", [P, A, 2, D], f16, local)
                sums = sb("sums", [P, A, D], f32, local)
                idx = sb("idx", [P, A], i32, local)
                hT = sb("hT_in", [P, UNROLL, 2, KT, P], f16, local) if own else None
                u = sb("u_out", [P, UNROLL, D], f32, local) if own else None
                raw = weights_room(local, jobs)
                block = local.enter_context(nc.Block())
                g = sig
                got = gather + scatter
                put = put_sems

                @block.sync
                def _(sp):
                    def sums_store(c, s, r):
                        wait_apart(sp, apart_sp, (g["sums_out"].handle, g["sums_out"].after(c + 1)))
                        sp.dma_start(AGG[bass.ds(c * P, P), :], sums[:, s]).then_inc(put[s].handle, 16)

                    def own_load(c, s, r):
                        if s % 2:
                            return
                        t = r * UNROLL + s // 2
                        if later(t, UNROLL):
                            wait_apart(sp, apart_sp, (g["own_product"].handle, g["own_product"].after(t - UNROLL + 1)))
                        sp.dma_start(hT[:, s // 2].rearrange("p a k n -> p (a k n)"),
                                     HT[bass.ds(t, 1)].rearrange("o p n -> (o p) n")).then_inc(own_in[s // 2].handle, 16)

                    def own_store(c, s, r):
                        if s % 2:
                            return
                        t = r * UNROLL + s // 2
                        wait_apart(sp, apart_sp, (g["own_out"].handle, g["own_out"].after(t + 1)))
                        sp.dma_start(U[bass.ds(t * P, P), :], u[:, s // 2]).then_inc(store[s // 2].handle, 16)
                    load_weights(sp, raw, jobs, rows_)
                    pipelined(sp, N_CHUNKS, ([(0, own_load), (6, own_store)] if own else []) + [(5, sums_store)], A)
                    if own:
                        for s in range(UNROLL):
                            wait_apart(sp, apart_sp, (store[s].handle, store[s].after(16 * N_TILES // UNROLL)))
                    for s in range(A):
                        wait_apart(sp, apart_sp, (put[s].handle, put[s].after(16 * N_CHUNKS // A)))

                @block.gpsimd
                def _(pool):
                    def gathers(c, s, r):
                        wait_apart(pool, apart_pool, (g["looked"].handle, g["looked"].after(c + 1)))
                        if later(c, A):
                            wait_apart(pool, apart_pool, (g["summed"].handle, g["summed"].after(c - A + 1)))
                        pool.indirect_dma_start(out=rows_in[:, s].rearrange("p a n -> p (a n)"), out_offset=None, in_=Z,
                                                in_offset=bass.IndirectOffsetOnAxis(ap=idx[:, s:s + 1], axis=0),
                                                bounds_check=N_PAD - 1, oob_is_err=False).then_inc(got[s].handle, 16)
                    pipelined(pool, N_CHUNKS, [(0, gathers)], A)

                @block.tensor
                def _(pe):
                    def sum_up(c, s, r):
                        pe.wait_ge(got[s].handle, got[s].after(16 * (r + 1)))
                        if later(c, 2):
                            pe.wait_ge(g["sums_out"].handle, g["sums_out"].after(c - 1))
                        sel = SEL[:, bass.ds(c, 1), :].rearrange("p o m -> p (o m)")
                        nc.tensor.matmul(banks[s % 2][:], sel, rows_in[:, s, 0], start=True, stop=False)
                        nc.tensor.matmul(banks[s % 2][:], sel, rows_in[:, s, 1], start=False, stop=True)\
                          .then_inc(g["summed"].handle, 1)

                    def own_part(c, s, r):
                        t = r * UNROLL + s // 2
                        b = 2 + s // 2 % 2
                        if s % 2 == 0:
                            pe.wait_ge(own_in[s // 2].handle, own_in[s // 2].after(16 * (r + 1)))
                            if later(t, 2):
                                pe.wait_ge(g["own_out"].handle, g["own_out"].after(t - 1))
                            products(banks[b], hT[:, s // 2], w_own, range(0, KT // 2), True, False)
                        else:
                            products(banks[b], hT[:, s // 2], w_own, range(KT // 2, KT), False, True)\
                                .then_inc(g["own_product"].handle, 1)
                    turn_weights(pe, raw, jobs, rows_)
                    pipelined(pe, N_CHUNKS, ([(0, own_part)] if own else []) + [(0, sum_up)], A)

                @block.scalar
                def _(act):
                    def evict(c, s, r):
                        act.wait_ge(g["summed"].handle, g["summed"].after(c + 1))
                        if later(c, A):
                            act.wait_ge(put[s].handle, put[s].after(16 * r))
                        act.activation(sums[:, s], banks[s % 2][:], ACT.Copy).then_inc(g["sums_out"].handle, 1)
                    high_weights(act, raw, jobs, rows_)
                    pipelined(act, N_CHUNKS, [(0, evict)], A)

                @block.vector
                def _(dve):
                    def indices(c, s, r):
                        if later(c, A):
                            wait_apart(dve, apart_dve, (got[s].handle, got[s].after(16 * r)))
                        dve.tensor_copy(idx[:, s:s + 1], order["value"][:, bass.ds(c, 1)]).then_inc(g["looked"].handle, 1)

                    def own_evict(c, s, r):
                        if s % 2 == 0:
                            return
                        t = r * UNROLL + s // 2
                        dve.wait_ge(g["own_product"].handle, g["own_product"].after(t + 1))
                        if later(t, UNROLL):
                            dve.wait_ge(store[s // 2].handle, store[s // 2].after(16 * r))
                        dve.scalar_tensor_tensor(u[:, s // 2], banks[2 + s // 2 % 2][:], 1.0 / W_SCALE, bias_own[:],
                                                 ALU.mult, ALU.add).then_inc(g["own_out"].handle, 1)
                    pipelined(dve, N_CHUNKS, [(0, indices)] + ([(5, own_evict)] if own else []), A)
                    low_weights(dve, raw, jobs, rows_)
            for s in range(UNROLL):
                for d_ in (gather, scatter):
                    d_[s].passed(16 * N_CHUNKS // A)
                if own:
                    own_in[s].passed(16 * N_TILES // UNROLL)
                    store[s].passed(16 * N_TILES // UNROLL)
            for s in range(A):
                put[s].passed(16 * N_CHUNKS // A)
            for name in ("summed", "looked", "sums_out"):
                g[name].passed(N_CHUNKS)
            if own:
                g["own_product"].passed(N_TILES)
                g["own_out"].passed(N_TILES)
            weights_passed(jobs, rows_)

        def join_chunks(table, width, order):
            full = table.shape[1]
            with ExitStack() as local:
                tails = sb("tails", [HALF, 2, width], f32, local)
                fixed = sb("fixed", [HALF, 2, full], f32, local)
                block = local.enter_context(nc.Block())
                v0, t0 = sig["v_step"], sig["t_step"]

                @block.sync
                def _(sp):
                    sp.dma_start(tails[:], bass.AP(table.tensor, (P - 1) * full,
                                                   [[P * full, HALF], [HALF * P * full, 2], [1, width]]))\
                      .then_inc(once.handle, 16)

                @block.gpsimd
                def _(pool):
                    for h in range(2):
                        pool.indirect_dma_start(out=fixed[:, h], out_offset=None, in_=table,
                                                in_offset=bass.IndirectOffsetOnAxis(ap=order["join"][:, h:h + 1], axis=0),
                                                bounds_check=E_PAD - 1, oob_is_err=False).then_inc(gather[h].handle, 16)
                    pool.wait_ge(once.handle, once.after(16))
                    pool.wait_ge(v0.handle, v0.after(1))
                    for h in range(2):
                        pool.indirect_dma_start(out=table,
                                                out_offset=bass.IndirectOffsetOnAxis(ap=order["join"][:, h:h + 1], axis=0),
                                                in_=fixed[:, h], in_offset=None,
                                                bounds_check=E_PAD - 1, oob_is_err=False).then_inc(scatter[h].handle, 16)
                    for h in range(2):
                        pool.wait_ge(scatter[h].handle, scatter[h].after(16))

                @block.tensor
                def _(pe):
                    pe.wait_ge(once.handle, once.after(16))
                    for h in range(2):
                        for first in range(0, width, BANK):
                            n = min(BANK, width - first)
                            for g in range(2):
                                last = nc.tensor.matmul(banks[2 * h + first // BANK][0:HALF, 0:n],
                                                        order["flow"][:, g, h * HALF:(h + 1) * HALF],
                                                        tails[:, g, first:first + n], start=g == 0, stop=g == 1)
                    last.then_inc(t0.handle, 1)

                @block.vector
                def _(dve):
                    dve.wait_ge(t0.handle, t0.after(1))
                    for h in range(2):
                        dve.wait_ge(gather[h].handle, gather[h].after(16))
                        for first in range(0, width, BANK):
                            n = min(BANK, width - first)
                            last = dve.tensor_tensor(fixed[:, h, first:first + n], fixed[:, h, first:first + n],
                                                     banks[2 * h + first // BANK][0:HALF, 0:n], ALU.add)
                    last.then_inc(v0.handle, 1)
            once.passed(16)
            t0.passed(1)
            v0.passed(1)
            for h in range(2):
                gather[h].passed(16)
                scatter[h].passed(16)

        def order_edges(lane_col, tile_col, order):
            with ExitStack() as local:
                S = UNROLL
                pairs = sb("pairs", [P, N_CHUNKS, 2], i32, local)
                lane_hot = sb("lane_hot", [P, S, P], f16, local)
                tile_hot = sb("tile_hot", [P, S, N_TILES], f32, local)
                tile_hot16 = sb("tile_hot16", [P, S, N_TILES], f16, local)
                lane_turned = sb("lane_turned", [P, S, P], f32, local)
                diag = sb("diag", [P, S, P], f32, local)
                scrap = sb("scrap", [P, S, P], f32, local)
                scrap2 = sb("scrap2", [P, S, N_TILES], f32, local)
                base = sb("base", [P, S, N_TILES], f32, local)
                rank = sb("rank", [P, S], f32, local)
                ahead = sb("ahead", [P, S], f32, local)
                place_i = sb("place_i", [P, S], i32, local)
                pair = sb("pair", [P, S, 2], i32, local)
                block = local.enter_context(nc.Block())
                g = sig
                v0 = g["v_step"]

                @block.sync
                def _(sp):
                    for s in range(S):
                        wait_apart(sp, apart_sp, (scatter[s].handle, scatter[s].after(16 * N_CHUNKS // S)))

                @block.gpsimd
                def _(pool):
                    def put(c, s, r):
                        wait_apart(pool, apart_pool, (g["placed"].handle, g["placed"].after(c + 1)))
                        pool.indirect_dma_start(out=SORTED,
                                                out_offset=bass.IndirectOffsetOnAxis(ap=place_i[:, s:s + 1], axis=0),
                                                in_=pair[:, s], in_offset=None, bounds_check=E_PAD - 1,
                                                oob_is_err=False).then_inc(scatter[s].handle, 16)
                    pipelined(pool, N_CHUNKS, [(0, put)])

                @block.tensor
                def _(pe):
                    def spread(c, s, r):
                        b = s % 2
                        pe.wait_ge(g["onehot"].handle, g["onehot"].after(c + 1))
                        if later(c, 2):
                            pe.wait_ge(g["a_step"].handle, g["a_step"].after(c - 1))
                            pe.wait_ge(g["ranked"].handle, g["ranked"].after(c - 1))
                            pe.wait_ge(g["based"].handle, g["based"].after(c - 1))
                        nc.tensor.transpose(banks[b].bitcast(f16)[:, 0:P], lane_hot[:, s], ident16[:])
                        nc.tensor.matmul(banks[2 + b][:, 0:P], ones[:], diag[:, s], start=True, stop=True)
                        nc.tensor.matmul(banks[4 + b][:, 0:N_TILES], lane_hot[:, s], tile_hot16[:, s], start=True,
                                         stop=True).then_inc(g["counted"].handle, 1)

                    def look_up(c, s, r):
                        pe.wait_ge(g["a_step"].handle, g["a_step"].after(c + 1))
                        pe.wait_ge(g["based"].handle, g["based"].after(c + 1))
                        if later(c, 2):
                            pe.wait_ge(g["placed"].handle, g["placed"].after(c - 1))
                        nc.tensor.matmul(banks[6 + s % 2][:, 0:N_TILES], lane_turned[:, s], base[:, s], start=True,
                                         stop=True).then_inc(g["looked"].handle, 1)
                    pipelined(pe, N_CHUNKS, [(0, spread), (1, look_up)])

                @block.scalar
                def _(act):
                    def turned(c, s, r):
                        act.wait_ge(g["counted"].handle, g["counted"].after(c + 1))
                        if later(c, S):
                            act.wait_ge(g["looked"].handle, g["looked"].after(c - S + 1))
                        act.activation(lane_turned[:, s], banks[s % 2].bitcast(f16)[:, 0:P], ACT.Copy)\
                           .then_inc(g["a_step"].handle, 1)
                    pipelined(act, N_CHUNKS, [(0, turned)])

                @block.vector
                def _(dve):
                    v = Signal(v0.handle)
                    v.base = v0.base
                    chain(dve, dve.tensor_copy(pairs[:, :, 0], key_col[:]), v)
                    chain(dve, dve.tensor_copy(pairs[:, :, 1], val_col[:]), v)
                    dve.tensor_copy(base[:, 0], order["first"][:]).then_inc(g["based"].handle, 1)

                    def hot(c, s, r):
                        if later(c, S):
                            dve.wait_ge(g["counted"].handle, g["counted"].after(c - S + 1))
                        one = bass.ds(c, 1)
                        dve.tensor_scalar(lane_hot[:, s], lane_row[:], lane_col[:, one], None, ALU.is_equal)
                        dve.tensor_scalar(tile_hot[:, s], tile_row[:], tile_col[:, one], None, ALU.is_equal)
                        dve.tensor_scalar(tile_hot16[:, s], tile_row[:], tile_col[:, one], None, ALU.is_equal)
                        dve.tensor_scalar(diag[:, s], ident[:], key_col[:, one], None, ALU.mult)\
                           .then_inc(g["onehot"].handle, 1)

                    def rest(c, s, r):
                        one = bass.ds(c, 1)
                        dve.wait_ge(g["counted"].handle, g["counted"].after(c + 1))
                        wait_apart(dve, apart_dve, (g["based"].handle, g["based"].after(c + 1)))
                        dve.tensor_tensor(base[:, (s + 1) % S], base[:, s], banks[4 + s % 2][:, 0:N_TILES], ALU.add)\
                           .then_inc(g["based"].handle, 1)
                        dve.scalar_tensor_tensor(scrap[:, s], banks[2 + s % 2][:, 0:P], key_col[:, one], earlier[:],
                                                 ALU.is_equal, ALU.mult, accum_out=rank[:, s:s + 1])\
                           .then_inc(g["ranked"].handle, 1)

                    def place(c, s, r):
                        one = bass.ds(c, 1)
                        wait_apart(dve, apart_dve, (g["looked"].handle, g["looked"].after(c + 1)))
                        dve.scalar_tensor_tensor(scrap2[:, s], banks[6 + s % 2][:, 0:N_TILES], 1.0, tile_hot[:, s],
                                                 ALU.mult, ALU.mult, accum_out=ahead[:, s:s + 1])\
                           .then_inc(g["sel_done"].handle, 1)
                        if later(c, S):
                            wait_apart(dve, apart_dve, (scatter[s].handle, scatter[s].after(16 * r)))
                        dve.tensor_copy(pair[:, s], pairs[:, one, :].rearrange("p o k -> p (o k)"))
                        wait_apart(dve, apart_dve, (g["sel_done"].handle, g["sel_done"].after(c + 1)))
                        dve.tensor_tensor(place_i[:, s:s + 1], rank[:, s:s + 1], ahead[:, s:s + 1], ALU.add)\
                           .then_inc(g["placed"].handle, 1)
                    pipelined(dve, N_CHUNKS, [(0, hot), (1, rest), (2, place)])
            v0.passed(2)
            for s in range(S):
                scatter[s].passed(16 * N_CHUNKS // S)
            for name in ("onehot", "counted", "a_step", "looked", "ranked", "sel_done", "placed"):
                g[name].passed(N_CHUNKS)
            g["based"].passed(N_CHUNKS + 1)

        def attention_scores(score):
            A = 2 * UNROLL
            with ExitStack() as local:
                left = sb("left", [P, A, D], f32, local)
                right = sb("right", [P, A, D], f32, local)
                both = sb("both", [P, 4, D], f32, local)
                leaky = sb("leaky", [P, 2, D], f32, local)
                prod = sb("prod", [P, 2, D], f32, local)
                idx = sb("idx", [P, A, 2], i32, local)
                block = local.enter_context(nc.Block())
                g = sig
                got = gather + scatter

                @block.gpsimd
                def _(pool):
                    def gathers(c, s, r):
                        wait_apart(pool, apart_pool, (g["looked"].handle, g["looked"].after(c + 1)))
                        if later(c, A):
                            wait_apart(pool, apart_pool, (g["summed"].handle, g["summed"].after(c - A + 1)))
                        for rows, table, k in ((left, XL, 0), (right, XR, 1)):
                            pool.indirect_dma_start(out=rows[:, s], out_offset=None, in_=table,
                                                    in_offset=bass.IndirectOffsetOnAxis(ap=idx[:, s, k:k + 1], axis=0),
                                                    bounds_check=N_PAD - 1, oob_is_err=False).then_inc(got[s].handle, 16)
                    pipelined(pool, N_CHUNKS, [(0, gathers)], A)

                @block.scalar
                def _(act):
                    def indices(c, s, r):
                        if later(c, A):
                            wait_apart(act, apart_act, (got[s].handle, got[s].after(32 * r)))
                        act.activation(idx[:, s, 0:1], order_d["value"][:, bass.ds(c, 1)], ACT.Copy)
                        act.activation(idx[:, s, 1:2], order_d["key"][:, bass.ds(c, 1)], ACT.Copy)\
                           .then_inc(g["looked"].handle, 1)

                    def copy(c, s, r):
                        act.wait_ge(g["summed"].handle, g["summed"].after(c + 1))
                        if later(c, 4):
                            act.wait_ge(g["x_step"].handle, g["x_step"].after(c - 3))
                        act.activation(both[:, s % 4], banks[s % 4][:], ACT.Copy).then_inc(g["a_step"].handle, 1)
                    pipelined(act, N_CHUNKS, [(0, indices), (5, copy)], A)

                @block.tensor
                def _(pe):
                    def add(c, s, r):
                        pe.wait_ge(got[s].handle, got[s].after(32 * (r + 1)))
                        if later(c, 4):
                            pe.wait_ge(g["a_step"].handle, g["a_step"].after(c - 3))
                        nc.tensor.matmul(banks[s % 4][:], ident[:], left[:, s], start=True, stop=False)
                        nc.tensor.matmul(banks[s % 4][:], ident[:], right[:, s], start=False, stop=True)\
                          .then_inc(g["summed"].handle, 1)
                    pipelined(pe, N_CHUNKS, [(0, add)], A)

                @block.vector
                def _(dve):
                    def leaky_relu(c, s, r):
                        dve.wait_ge(g["a_step"].handle, g["a_step"].after(c + 1))
                        if later(c, 2):
                            wait_apart(dve, apart_dve, (g["weighed"].handle, g["weighed"].after(c - 1)))
                        dve.scalar_tensor_tensor(leaky[:, s % 2], both[:, s % 4], 0.2, both[:, s % 4], ALU.mult, ALU.max)\
                           .then_inc(g["x_step"].handle, 1)

                    def weigh(c, s, r):
                        wait_apart(dve, apart_dve, (g["x_step"].handle, g["x_step"].after(c + 1)))
                        if later(c, 2):
                            wait_apart(dve, apart_dve, (g["y_step"].handle, g["y_step"].after(c - 1)))
                        dve.tensor_tensor(prod[:, s % 2], leaky[:, s % 2], att_row[:], ALU.mult).then_inc(g["weighed"].handle, 1)

                    def head_sums(c, s, r):
                        wait_apart(dve, apart_dve, (g["weighed"].handle, g["weighed"].after(c + 1)))
                        dve.tensor_reduce(score[:, bass.ds(c, 1), :].rearrange("p o h -> p (o h)"),
                                          prod[:, s % 2].rearrange("p (h k) -> p h k", h=HEADS), AX.X, ALU.add)\
                           .then_inc(g["y_step"].handle, 1)
                    pipelined(dve, N_CHUNKS, [(0, leaky_relu), (0, weigh), (0, head_sums)], A)
            for s in range(UNROLL):
                gather[s].passed(32 * N_CHUNKS // A)
                scatter[s].passed(32 * N_CHUNKS // A)
            for name in ("looked", "summed", "a_step", "x_step", "weighed", "y_step"):
                g[name].passed(N_CHUNKS)

        def attention_maxima(score, top, weight):
            Q = 4
            J = N_CHUNKS // Q
            W = J * P
            LANES = P // Q
            with ExitStack() as local:
                turned = sb("turned", [P, 1 + W], f32, local)
                keys = sb("keys", [P, W + 2], i32, local)
                gap = sb("gap", [P, W], f32, local)
                start = sb("start", [P, 1], f32, local)
                spread = sb("spread", [P, J, Q, LANES], f32, local)
                block = local.enter_context(nc.Block())
                g = sig
                v0, t0, a0 = g["v_step"], g["t_step"], g["a_step"]
                B = J // UNROLL
                N_SCAN = 3 + 2 * (2 + 2 * Q)

                @block.sync
                def _(sp):
                    for q in range(Q):
                        sp.dma_start(keys[q * LANES:(q + 1) * LANES, :],
                                     bass.AP(dst_list.tensor, q * W, [[0, LANES], [1, W + 2]])).then_inc(once.handle, 16)

                @block.tensor
                def _(pe):
                    pe.wait_ge(v0.handle, v0.after(2))
                    for b in range(B):
                        if b >= 2:
                            pe.wait_ge(a0.handle, a0.after(b - 1))
                        for n in range(UNROLL):
                            j = b * UNROLL + n
                            last = nc.tensor.transpose(banks[b % 2][:, n * P:(n + 1) * P],
                                                       spread[:, j].rearrange("p q l -> p (q l)"), ident[:])
                        last.then_inc(t0.handle, 1)
                    pe.wait_ge(v0.handle, v0.after(N_SCAN))
                    for b in range(B):
                        pe.wait_ge(a0.handle, a0.after(max(B, B + b - 1)))
                        for n in range(UNROLL):
                            j = b * UNROLL + n
                            last = nc.tensor.transpose(banks[b % 2][:, n * P:(n + 1) * P],
                                                       turned[:, 1 + j * P:1 + (j + 1) * P], ident[:])
                        last.then_inc(t0.handle, 1)

                @block.scalar
                def _(act):
                    for b in range(B):
                        act.wait_ge(t0.handle, t0.after(b + 1))
                        act.activation(turned[:, 1 + b * UNROLL * P:1 + (b + 1) * UNROLL * P],
                                       banks[b % 2][:], ACT.Copy)\
                           .then_inc(a0.handle, 1)
                    for b in range(B):
                        act.wait_ge(t0.handle, t0.after(B + b + 1))
                        for n in range(UNROLL):
                            j = b * UNROLL + n
                            last = act.activation(top[:].rearrange("p (q j) h -> p j q h", q=Q)[:, j],
                                                  banks[b % 2][:, n * P:(n + 1) * P]
                                                  .rearrange("p (q l) -> p q l", q=Q)[:, :, 0:HEADS], ACT.Copy)
                        last.then_inc(a0.handle, 1)
                    act.wait_ge(v0.handle, v0.after(N_SCAN + 1))
                    act.activation(weight[:], weight[:], ACT.Exp).then_inc(a0.handle, 1)

                @block.vector
                def _(dve):
                    v = Signal(v0.handle)
                    v.base = v0.base
                    lanes = lambda q: slice(q * LANES, (q + 1) * LANES)
                    chain(dve, dve.memset(spread[:], 0.0), v)
                    chain(dve, dve.tensor_copy(spread[:, :, :, 0:HEADS],
                                               score[:].rearrange("p (q j) h -> p j q h", q=Q)), v)
                    dve.wait_ge(once.handle, once.after(16 * Q))
                    chain(dve, dve.memset(turned[:, 0:1], 0.0), v)
                    for back in (False, True):
                        other = keys[:, 2:W + 2] if back else keys[:, 0:W]
                        chain(dve, dve.tensor_tensor(gap[:], keys[:, 1:W + 1], other, ALU.is_equal), v)
                        chain(dve, dve.tensor_scalar(gap[:], gap[:], -1.0, -LOW, ALU.add, ALU.mult), v)
                        if not back:
                            dve.wait_ge(a0.handle, a0.after(B))
                        for n in range(Q):
                            q = Q - 1 - n if back else n
                            prior = q + 1 if back else q - 1
                            if n == 0:
                                chain(dve, dve.memset(start[lanes(q), :], LOW), v)
                            else:
                                end = turned[lanes(prior), 1:2] if back else turned[lanes(prior), W:W + 1]
                                chain(dve, dve.tensor_copy(start[lanes(q), :], end), v)
                            line = turned[lanes(q), 1:W + 1]
                            flags = gap[lanes(q), :]
                            if back:
                                line, flags = turned[lanes(q), W:0:-1], gap[lanes(q), ::-1]
                            chain(dve, dve.tensor_tensor_scan(line, flags, line, start[lanes(q), 0:1], ALU.add, ALU.max), v)
                    dve.wait_ge(a0.handle, a0.after(2 * B))
                    dve.tensor_tensor(weight[:], score[:], top[:], ALU.subtract).then_inc(v.handle, 1)
            once.passed(16 * Q)
            v0.passed(N_SCAN + 1)
            t0.passed(2 * B)
            a0.passed(2 * B + 1)

        def attention_sums(top, weight):
            A = 2 * UNROLL
            WIDE = D + HEADS
            with ExitStack() as local:
                raw = sb("raw", [P, A, D], f32, local)
                rows_in = sb("rows_in", [P, UNROLL, 2, WIDE], f16, local)
                scaled = sb("scaled", [P, UNROLL, WIDE], f32, local)
                sums = sb("sums", [P, A, WIDE + HEADS], f32, local)
                idx = sb("idx", [P, A], i32, local)
                block = local.enter_context(nc.Block())
                g = sig
                got = gather + scatter
                put = put_sems
                pair = lambda s: psum[:, (s % UNROLL) * 2 * BANK:(s % UNROLL) * 2 * BANK + WIDE]

                @block.sync
                def _(sp):
                    def sums_store(c, s, r):
                        wait_apart(sp, apart_sp, (g["sums_out"].handle, g["sums_out"].after(c + 1)))
                        sp.dma_start(AGG_A[bass.ds(c * P, P), :], sums[:, s]).then_inc(put[s].handle, 16)
                    pipelined(sp, N_CHUNKS, [(0, sums_store)], A)
                    for s in range(A):
                        wait_apart(sp, apart_sp, (put[s].handle, put[s].after(16 * N_CHUNKS // A)))

                @block.gpsimd
                def _(pool):
                    def gathers(c, s, r):
                        if later(c, A):
                            wait_apart(pool, apart_pool, (got[s].handle, got[s].after(16 * r)))
                            wait_apart(pool, apart_pool, (g["weighed"].handle, g["weighed"].after(c - A + 1)))
                        pool.tensor_copy(idx[:, s:s + 1], order_d["value"][:, bass.ds(c, 1)]).then_inc(g["looked"].handle, 1)
                        wait_apart(pool, apart_pool, (g["looked"].handle, g["looked"].after(c + 1)))
                        pool.indirect_dma_start(out=raw[:, s], out_offset=None, in_=XL,
                                                in_offset=bass.IndirectOffsetOnAxis(ap=idx[:, s:s + 1], axis=0),
                                                bounds_check=N_PAD - 1, oob_is_err=False).then_inc(got[s].handle, 16)
                    pipelined(pool, N_CHUNKS, [(0, gathers)], A)

                @block.tensor
                def _(pe):
                    def sum_up(c, s, r):
                        pe.wait_ge(g["w_lo"].handle, g["w_lo"].after(c + 1))
                        if later(c, UNROLL):
                            pe.wait_ge(g["sums_out"].handle, g["sums_out"].after(c - UNROLL + 1))
                        sel = SEL[:, bass.ds(c, 1), :].rearrange("p o m -> p (o m)")
                        for first, n in ((0, D), (D, HEADS)):
                            for half_ in range(2):
                                last = nc.tensor.matmul(pair(s)[:, first:first + n], sel,
                                                        rows_in[:, s % UNROLL, half_, first:first + n],
                                                        start=half_ == 0, stop=half_ == 1)
                        last.then_inc(g["summed"].handle, 1)
                    pipelined(pe, N_CHUNKS, [(0, sum_up)], A)

                @block.scalar
                def _(act):
                    def high(c, s, r):
                        act.wait_ge(g["weighed"].handle, g["weighed"].after(c + 1))
                        if later(c, UNROLL):
                            act.wait_ge(g["summed"].handle, g["summed"].after(c - UNROLL + 1))
                        act.activation(rows_in[:, s % UNROLL, 0], scaled[:, s % UNROLL], ACT.Copy).then_inc(g["w_hi"].handle, 1)

                    def evict(c, s, r):
                        act.wait_ge(g["summed"].handle, g["summed"].after(c + 1))
                        if later(c, A):
                            wait_apart(act, apart_act, (put[s].handle, put[s].after(16 * r)))
                        act.activation(sums[:, s, WIDE:], top[:, bass.ds(c, 1), :].rearrange("p o h -> p (o h)"), ACT.Copy)
                        act.activation(sums[:, s, 0:WIDE], pair(s), ACT.Copy).then_inc(g["sums_out"].handle, 1)
                    pipelined(act, N_CHUNKS, [(0, high), (2, evict)], A)

                @block.vector
                def _(dve):
                    def weigh(c, s, r):
                        wait_apart(dve, apart_dve, (got[s].handle, got[s].after(16 * (r + 1))))
                        if later(c, UNROLL):
                            wait_apart(dve, apart_dve, (g["w_lo"].handle, g["w_lo"].after(c - UNROLL + 1)))
                        w = weight[:, bass.ds(c, 1), :].rearrange("p o h -> p (o h)")
                        dve.tensor_tensor(scaled[:, s % UNROLL, 0:D].rearrange("p (h k) -> p h k", h=HEADS),
                                          raw[:, s].rearrange("p (h k) -> p h k", h=HEADS),
                                          w.unsqueeze(2).to_broadcast([P, HEADS, HEAD_DIM]), ALU.mult)
                        dve.tensor_copy(scaled[:, s % UNROLL, D:], w).then_inc(g["weighed"].handle, 1)

                    def low(c, s, r):
                        dve.wait_ge(g["w_hi"].handle, g["w_hi"].after(c + 1))
                        dve.tensor_tensor(rows_in[:, s % UNROLL, 1], scaled[:, s % UNROLL], rows_in[:, s % UNROLL, 0],
                                          ALU.subtract).then_inc(g["w_lo"].handle, 1)
                    pipelined(dve, N_CHUNKS, [(0, weigh), (2, low)], A)
            for s in range(UNROLL):
                for d_ in (gather, scatter):
                    d_[s].passed(16 * N_CHUNKS // A)
            for s in range(A):
                put[s].passed(16 * N_CHUNKS // A)
            for name in ("summed", "sums_out", "looked", "weighed", "w_hi", "w_lo"):
                g[name].passed(N_CHUNKS)

        def attention_output():
            WIDE = D + 2 * HEADS
            V = 2 * UNROLL
            with ExitStack() as local:
                sums = sb("sums_in", [P, UNROLL, WIDE], f32, local)
                left = sb("left_in", [P, UNROLL, D], f32, local)
                rest = sb("rest_in", [P, UNROLL, D], f32, local)
                near = sb("near", [P, UNROLL, D], f32, local)
                near2 = sb("near2", [P, UNROLL, D], f32, local)
                far = sb("far", [P, UNROLL, D], f32, local)
                mixed = sb("mixed", [P, UNROLL, D], f32, local)
                neg = sb("neg", [P, 2, D], f32, local)
                ex = sb("ex", [P, UNROLL, D], f32, local)
                pos = sb("pos", [P, UNROLL, D], f32, local)
                elu = sb("elu", [P, 2, D], f32, local)
                res = sb("res", [P, UNROLL, D], f32, local)
                place = sb("place", [P, UNROLL], i32, local)
                m = sb("m", [P, V, HEADS], f32, local)
                dif = sb("dif", [P, V, 2, HEADS], f32, local)
                e = sb("e", [P, V, 2, HEADS], f32, local)
                den = sb("den", [P, V, HEADS], f32, local)
                coef = sb("coef", [P, V, 2, HEADS], f32, local)
                block = local.enter_context(nc.Block())
                g = sig
                wide = lambda a: a.unsqueeze(2).to_broadcast([P, HEADS, HEAD_DIM])
                heads = lambda a: a.rearrange("p (h k) -> p h k", h=HEADS)

                def tiles(eng, steps):
                    pipelined(eng, N_TILES,
                              [(lag, lambda t, w, r, step=step: step(t, w % UNROLL, 2 * r + w // UNROLL, w))
                               for lag, step in steps], V)

                @block.sync
                def _(sp):
                    def load_left(t, s, r, w):
                        if later(t, UNROLL):
                            wait_apart(sp, apart_sp, (g["p_step"].handle, g["p_step"].after(t - UNROLL + 1)))
                        sp.dma_start(left[:, s], XL[bass.ds(t * P, P), :]).then_inc(load[s].handle, 16)

                    def load_rest(t, s, r, w):
                        if later(t, UNROLL):
                            wait_apart(sp, apart_sp, (g["out_lo"].handle, g["out_lo"].after(t - UNROLL + 1)))
                        sp.dma_start(rest[:, s], XH[bass.ds(t * P, P), :]).then_inc(own_in[s].handle, 16)

                    def stores(t, s, r, w):
                        wait_apart(sp, apart_sp, (g["out_lo"].handle, g["out_lo"].after(t + 1)))
                        sp.dma_start(out[bass.ds(t * P, P), :], res[:, s]).then_inc(store[s].handle, 16)
                    tiles(sp, [(0, load_left), (4, load_rest), (8, stores)])
                    for s in range(UNROLL):
                        wait_apart(sp, apart_sp, (store[s].handle, store[s].after(16 * N_TILES // UNROLL)))

                @block.gpsimd
                def _(pool):
                    def gathers(t, s, r, w):
                        q = g["looked"]
                        if later(t, UNROLL):
                            wait_apart(pool, apart_pool, (gather[s].handle, gather[s].after(16 * r)))
                            wait_apart(pool, apart_pool, (g["combined"].handle, g["combined"].after(t - UNROLL + 1)))
                        pool.tensor_copy(place[:, s:s + 1], order_d["last"][:, bass.ds(t, 1)]).then_inc(q.handle, 1)
                        wait_apart(pool, apart_pool, (q.handle, q.after(t + 1)))
                        pool.indirect_dma_start(out=sums[:, s], out_offset=None, in_=AGG_A,
                                                in_offset=bass.IndirectOffsetOnAxis(ap=place[:, s:s + 1], axis=0),
                                                bounds_check=E_PAD, oob_is_err=False).then_inc(gather[s].handle, 16)

                    def own_share(t, s, r, w):
                        wait_apart(pool, apart_pool, (load[s].handle, load[s].after(16 * (r + 1))))
                        wait_apart(pool, apart_pool, (g["norm"].handle, g["norm"].after(t + 1)))
                        if later(t, UNROLL):
                            wait_apart(pool, apart_pool, (g["product"].handle, g["product"].after(t - UNROLL + 1)))
                        pool.tensor_tensor(out=heads(near[:, s]), in0=heads(left[:, s]), in1=wide(coef[:, w, 1]),
                                           op=ALU.mult).then_inc(g["p_step"].handle, 1)
                        wait_apart(pool, apart_pool, (g["p_step"].handle, g["p_step"].after(t + 1)))
                        pool.tensor_tensor(out=near2[:, s], in0=near[:, s], in1=bias_out[:], op=ALU.add)\
                            .then_inc(g["placed"].handle, 1)
                    tiles(pool, [(0, gathers), (4, own_share)])

                @block.scalar
                def _(act):
                    def exps(t, s, r, w):
                        act.wait_ge(g["squares"].handle, g["squares"].after(t + 1))
                        act.activation(e[:, w], dif[:, w], ACT.Exp).then_inc(g["a_step"].handle, 1)

                    def elu_parts(t, s, r, w):
                        q = g["w_hi"]
                        act.wait_ge(g["product"].handle, g["product"].after(t + 1))
                        if later(t, UNROLL):
                            act.wait_ge(g["out_sum"].handle, g["out_sum"].after(t - UNROLL + 1))
                        act.activation(neg[:, s % 2], mixed[:, s], ACT.Relu, scale=-1.0).then_inc(q.handle, 1)
                        act.activation(pos[:, s], mixed[:, s], ACT.Relu)
                        act.wait_ge(q.handle, q.after(t + 1))
                        act.activation(ex[:, s], neg[:, s % 2], ACT.Exp, scale=-1.0).then_inc(g["out_hi"].handle, 1)
                    tiles(act, [(2, exps), (5, elu_parts)])

                @block.vector
                def _(dve):
                    def differences(t, s, r, w):
                        q = g["y_step"]
                        dve.wait_ge(gather[s].handle, gather[s].after(16 * (r + 1)))
                        dve.tensor_tensor(m[:, w], own_scores[:, bass.ds(t, 1), :].rearrange("p o h -> p (o h)"),
                                          sums[:, s, D + HEADS:], ALU.max).then_inc(q.handle, 1)
                        wait_apart(dve, apart_dve, (q.handle, q.after(t + 1)))
                        dve.tensor_tensor(dif[:, w, 0], sums[:, s, D + HEADS:], m[:, w], ALU.subtract)
                        dve.tensor_tensor(dif[:, w, 1], own_scores[:, bass.ds(t, 1), :].rearrange("p o h -> p (o h)"),
                                          m[:, w], ALU.subtract).then_inc(g["squares"].handle, 1)

                    def coefficients(t, s, r, w):
                        q = g["ranked"]
                        dve.wait_ge(g["a_step"].handle, g["a_step"].after(t + 1))
                        dve.tensor_tensor(den[:, w], e[:, w, 0], sums[:, s, D:D + HEADS], ALU.mult).then_inc(q.handle, 1)
                        wait_apart(dve, apart_dve, (q.handle, q.after(4 * t + 1)))
                        dve.tensor_tensor(den[:, w], den[:, w], e[:, w, 1], ALU.add).then_inc(q.handle, 1)
                        wait_apart(dve, apart_dve, (q.handle, q.after(4 * t + 2)))
                        dve.tensor_scalar(den[:, w], den[:, w], 1e-16, None, ALU.max).then_inc(q.handle, 1)
                        wait_apart(dve, apart_dve, (q.handle, q.after(4 * t + 3)))
                        dve.reciprocal(den[:, w], den[:, w]).then_inc(q.handle, 1)
                        wait_apart(dve, apart_dve, (q.handle, q.after(4 * t + 4)))
                        dve.tensor_tensor(coef[:, w, 0], e[:, w, 0], den[:, w], ALU.mult)
                        dve.tensor_tensor(coef[:, w, 1], e[:, w, 1], den[:, w], ALU.mult).then_inc(g["norm"].handle, 1)

                    def weigh(t, s, r, w):
                        wait_apart(dve, apart_dve, (g["norm"].handle, g["norm"].after(t + 1)))
                        dve.tensor_tensor(heads(far[:, s]), heads(sums[:, s, 0:D]), wide(coef[:, w, 0]), ALU.mult)\
                           .then_inc(g["combined"].handle, 1)

                    def mix(t, s, r, w):
                        dve.wait_ge(g["placed"].handle, g["placed"].after(t + 1))
                        wait_apart(dve, apart_dve, (g["combined"].handle, g["combined"].after(t + 1)))
                        if later(t, UNROLL):
                            wait_apart(dve, apart_dve, (g["out_hi"].handle, g["out_hi"].after(t - UNROLL + 1)))
                        dve.tensor_tensor(mixed[:, s], far[:, s], near2[:, s], ALU.add).then_inc(g["product"].handle, 1)

                    def finish(t, s, r, w):
                        dve.wait_ge(g["out_hi"].handle, g["out_hi"].after(t + 1))
                        dve.scalar_tensor_tensor(elu[:, s % 2], ex[:, s], -1.0, pos[:, s], ALU.add, ALU.add)\
                           .then_inc(g["out_sum"].handle, 1)
                        wait_apart(dve, apart_dve, (g["out_sum"].handle, g["out_sum"].after(t + 1)),
                                   (own_in[s].handle, own_in[s].after(16 * (r + 1))))
                        if later(t, UNROLL):
                            wait_apart(dve, apart_dve, (store[s].handle, store[s].after(16 * r)))
                        dve.tensor_tensor(res[:, s], elu[:, s % 2], rest[:, s], ALU.add).then_inc(g["out_lo"].handle, 1)
                    tiles(dve, [(2, differences), (3, coefficients), (3, weigh), (5, mix), (6, finish)])

        def clear_rows():
            with ExitStack() as local:
                zero = sb("zero", [1, D + 2 * HEADS], f32, local)
                block = local.enter_context(nc.Block())
                v0 = sig["v_step"]

                @block.vector
                def _(dve):
                    dve.memset(zero[:, 0:D + HEADS], 0.0).then_inc(v0.handle, 1)
                    dve.memset(zero[:, D + HEADS:], LOW).then_inc(v0.handle, 1)

                @block.sync
                def _(sp):
                    wait_apart(sp, apart_sp, (v0.handle, v0.after(2)))
                    sp.dma_start(AGG[E_PAD:E_PAD + 1, :], zero[:, 0:D]).then_inc(once.handle, 16)
                    sp.dma_start(AGG_A[E_PAD:E_PAD + 1, :], zero[:]).then_inc(once.handle, 16)
                    wait_apart(sp, apart_sp, (once.handle, once.after(32)))
            v0.passed(2)
            once.passed(32)

        own_in = [signal(f"own_in{s}") for s in range(UNROLL)]
        put_sems = [signal(f"put{s}") for s in range(2 * UNROLL)]
        lane_col = sb("lane_col", [P, N_CHUNKS], f32)
        tile_col = sb("tile_col", [P, N_CHUNKS], f32)

        def listed(a):
            return [bass.AP(a.tensor, 1 + h * HALF * P, [[P, HALF], [1, P]]) for h in range(2)]
        pairs_by_source = [bass.AP(SORTED.tensor, 2 * h * HALF * P, [[2 * P, HALF], [1, 2 * P]]) for h in range(2)]

        def row(a):
            return a.rearrange("(o n) -> o n", o=1)

        constants()
        clear_rows()
        edge_columns(listed(src_list), listed(dst_list), order_s)
        count_keys(order_s, False, lane_col, tile_col)
        order_edges(lane_col, tile_col, order_s)
        edge_columns(listed(dst_list), listed(src_list), order_d)
        count_keys(order_d, True, lane_col, tile_col)
        select_matrices()

        split_weights([(Ws_neigh[0], w_out, False)], [])
        for layer in range(3):
            own_weights = dict(jobs=[(Ws_self[layer], w_own, False)], rows_=[(bs[layer:layer + 1, :], bias_own)])
            if layer == 0:
                dense(x_in=x, ht=True, **own_weights)
            else:
                dense(own=U, order=order_d, norm=False, ht=True, **own_weights)
            aggregate(order_d, own=True, jobs=[(Ws_neigh[layer + 1], w_out, False)] if layer < 2 else [(W1, w_out, True)],
                      rows_=[(row(b1), bias_out)] if layer == 2 else [])
            join_chunks(AGG, D, order_d)
        dense(x_in=x, own=U, order=order_d, log_map=True, x_out=X1)
        aggregate(order_d, jobs=[(wn, w_out, False)])
        join_chunks(AGG, D, order_d)
        dense(x_in=X1, order=order_d, exp_map=True, x_out=X2, ht=True, jobs=[(wc, w_own, False)],
              rows_=[(row(b2), bias_own)])
        edge_columns(pairs_by_source, None, order_s)
        select_matrices()
        aggregate(order_s, own=True, jobs=[(W_l, w_out, False), (W_r, w_out2, False)],
                  rows_=[(row(att.rearrange("h k -> (h k)")), att_row), (row(b3), bias_out)])
        join_chunks(AGG, D, order_s)
        dense(x_in=X2, own=U, order=order_s, attention=True)
        edge_columns(listed(dst_list), listed(src_list), order_d)
        select_matrices()
        score = sb("score", [P, N_CHUNKS, HEADS], f32)
        top = sb("top", [P, N_CHUNKS, HEADS], f32)
        weight = sb("weight", [P, N_CHUNKS, HEADS], f32)
        attention_scores(score)
        attention_maxima(score, top, weight)
        attention_sums(top, weight)
        join_chunks(AGG_A, D + HEADS, order_d)
        attention_output()


_INS = ["x", "src", "dst", "L0_gnn_Ws_self", "L0_gnn_Ws_neigh", "L0_gnn_bs", "L1_gnn_W", "L1_gnn_b", "L2_gnn_wc",
        "L2_gnn_wn", "L2_gnn_bias", "L3_gnn_W_l", "L3_gnn_W_r", "L3_gnn_att", "L3_gnn_bias"]


def kernel(**inputs):
    import numpy as np
    import concourse.bacc as bacc
    from concourse.bass_utils import run_bass_kernel_spmd

    nc = bacc.Bacc("TRN2", target_bir_lowering=False, num_devices=1)
    arrays, args = {}, []
    for name in _INS:
        a = np.ascontiguousarray(inputs[name])
        if name == "x":
            a = np.concatenate([a, np.zeros((N_PAD - N_NODES, D), a.dtype)])
        if name in ("src", "dst"):
            extra = np.minimum(N_NODES + np.arange(E_PAD - N_EDGES), N_PAD - 1).astype(a.dtype)
            edge = np.full((1,), -1, a.dtype)
            a = np.concatenate([edge, a, extra, edge])
        arrays[f"in_{name}"] = a
        args.append(nc.dram_tensor(f"in_{name}", a.shape, mybir.dt.from_np(a.dtype), kind="ExternalInput").ap())
    out = nc.dram_tensor("out_0", (N_PAD, D), mybir.dt.float32, kind="ExternalOutput").ap()

    def scratch(name, shape, dtype):
        return nc.dram_tensor(name, shape, dtype, kind="Internal").ap()

    gnn_program(nc, *args, out, scratch)
    r = run_bass_kernel_spmd(nc, [arrays], core_ids=[0])
    return r.results[0]["out_0"][:N_NODES]
```

```python
import concourse.bass as bass
from concourse import mybir
from contextlib import ExitStack

P = 128
D = 512
N_NODES = 10000
N_EDGES = 20000
HEADS = 8
HEAD_DIM = D // HEADS
UNROLL = 4
N_TILES = -(-N_NODES // (P * 2 * UNROLL)) * 2 * UNROLL
N_PAD = N_TILES * P
N_CHUNKS = -(-(N_EDGES + N_PAD - N_NODES) // (P * 2 * UNROLL)) * 2 * UNROLL
E_PAD = N_CHUNKS * P
HALF = N_CHUNKS // 2
BANK = 512
KT = D // P
W_SCALE = 256.0
EPS_LN = 1e-5
EPS_HYP = 1e-7
CLIP_HYP = 1.0 - 1e-7
LOW = -1e30


class Signal:

    def __init__(self, handle):
        self.handle = handle
        self.base = 0

    def after(self, n):
        return self.base + n

    def passed(self, n):
        self.base += n


def pipelined(eng, n, steps, unroll=UNROLL, end=0):
    rounds = n // unroll

    def body(i, j):
        for lag, step in steps:
            s, back = (j - lag) % unroll, (j - lag) // unroll
            if type(i) is int and not 0 <= i + back < rounds:
                continue
            step((i + back) * unroll + s, s, i + back)

    for i in (0, 1):
        for j in range(unroll):
            body(i, j)
    with eng.Fori(2, rounds - end) as i:
        for j in range(unroll):
            body(i, j)
    for i in range(rounds - end, rounds + 1 + (max(lag for lag, _ in steps) - 1) // unroll):
        for j in range(unroll):
            body(i, j)


def wait_apart(eng, step_sem, *waits):
    for sem, value in waits:
        eng.wait_ge(sem, value)
    eng.sem_inc(step_sem, 1)


def gnn_program(nc, x, src_list, dst_list, Ws_self, Ws_neigh, bs, W1, b1, wc, wn, b2, W_l, W_r, att, b3,
                out, dram):
    f32, f16, i32 = mybir.dt.float32, mybir.dt.float16, mybir.dt.int32
    ACT, ALU, AX = mybir.ActivationFunctionType, mybir.AluOpType, mybir.AxisListType

    def later(t, depth):
        return type(t) is not int or t >= depth

    Z = dram("Z", (N_PAD, 2 * D), f16)
    U = dram("U", (N_PAD, D), f32)
    HT = dram("HT", (N_TILES, P, 2 * D), f16)
    X1 = dram("X1", (N_PAD, D), f32)
    X2 = dram("X2", (N_PAD, D), f32)
    AGG = dram("AGG", (E_PAD + 1, D), f32)
    AGG_A = dram("AGG_A", (E_PAD + 1, D + 2 * HEADS), f32)
    XL = dram("XL", (N_PAD, D), f32)
    XR = dram("XR", (N_PAD, D), f32)
    XH = dram("XH", (N_PAD, D), f32)
    SORTED = dram("SORTED", (E_PAD, 2), i32)

    ctx = ExitStack()
    with ctx:
        made = {}

        def sb(name, shape, dt, where=ctx):
            made[name] = made.get(name, 0) + 1
            if made[name] > 1:
                name = f"{name}_{made[name]}"
            return where.enter_context(nc.sbuf_tensor(name, shape, dt))

        def signal(name):
            return Signal(ctx.enter_context(nc.semaphore(name)))

        ident = sb("ident", [P, P], f32)
        ident16 = sb("ident16", [P, P], f16)
        ones = sb("ones", [P, P], f32)
        below = sb("below", [P, P], f32)
        earlier = sb("earlier", [P, P], f32)
        lane_row = sb("lane_row", [P, P], f32)
        tile_row = sb("tile_row", [P, N_TILES], f32)
        later_chunk = sb("later_chunk", [HALF, 2, N_CHUNKS], f32)
        chunk_row = sb("chunk_row", [HALF, 2], f32)
        neg_half = sb("neg_half", [P, 1], f32)
        half = sb("half", [P, 1], f32)
        SEL = sb("SEL", [P, N_CHUNKS, P], f16)
        order_d, order_s = (
            {"value": sb(f"value_{o}", [P, N_CHUNKS], i32),
             "value_f": sb(f"value_f_{o}", [P, N_CHUNKS], f32),
             "key_f": sb(f"key_f_{o}", [P, N_CHUNKS], f32),
             "lane": sb(f"lane_{o}", [P, N_CHUNKS], f32),
             "tile": sb(f"tile_{o}", [P, N_CHUNKS], f32),
             "key": sb(f"key_{o}", [P, N_CHUNKS], i32),
             "last": sb(f"last_{o}", [P, N_TILES], i32),
             "first": sb(f"first_{o}", [P, N_TILES], f32),
             "inverse": sb(f"inverse_{o}", [P, N_TILES], f32),
             "flow": sb(f"flow_{o}", [HALF, 2, N_CHUNKS], f32),
             "join": sb(f"join_{o}", [HALF, 2], i32)}
            for o in ("d", "s"))
        w_own = sb("w_own", [P, 2, KT, D], f16)
        w_out = sb("w_out", [P, 2, KT, D], f16)
        w_out2 = sb("w_out2", [P, 2, KT, D], f16)
        bias_own = sb("bias_own", [P, D], f32)
        bias_out = sb("bias_out", [P, D], f32)
        att_row = sb("att_row", [P, D], f32)
        own_scores = sb("own_scores", [P, N_TILES, HEADS], f32)
        psum = ctx.enter_context(nc.psum_tensor("psum", [P, 8 * BANK], f32))
        banks = [psum[:, i * BANK:(i + 1) * BANK] for i in range(8)]

        load = [signal(f"load{s}") for s in range(UNROLL)]
        store = [signal(f"store{s}") for s in range(UNROLL)]
        gather = [signal(f"gather{s}") for s in range(UNROLL)]
        kept = [signal(f"kept{s}") for s in range(UNROLL)]
        scatter = [signal(f"scatter{s}") for s in range(UNROLL)]
        own_in = [signal(f"own_in{s}") for s in range(UNROLL)]
        put_sems = [signal(f"put{s}") for s in range(2 * UNROLL)]
        pair_sems = [signal(f"pairs{s}") for s in range(2 * UNROLL)]
        once = signal("once")
        apart_sp, apart_dve, apart_pool, apart_act = (signal(f"apart{n}").handle for n in range(4))
        names = ("combined", "stats", "aggr", "rstd", "bias_ln", "eps_added", "h_done", "transposed", "hi_done",
                 "lo_done", "product", "out_hi", "out_lo", "out_sum", "squares", "norm", "summed",
                 "sums_out", "own_product", "own_out", "v_step", "a_step", "p_step", "t_step",
                 "onehot", "counted", "ranked", "placed", "weighed", "w_hi", "w_lo",
                 "diag_done", "keys_row", "sel_done", "based", "looked", "found", "row_counted",
                 "turned", "pow_step", "x_step", "y_step")
        sig = {n: signal(n) for n in names}

        def chain(eng, ins, s):
            ins.then_inc(s.handle, 1)
            s.base += 1
            eng.wait_ge(s.handle, s.base)

        def constants():
            with nc.Block() as block:
                @block.gpsimd
                def _(pool):
                    p = sig["p_step"]
                    chain(pool, pool.memset(ones[:], 1.0), p)
                    chain(pool, pool.memset(neg_half[:], -0.5), p)
                    chain(pool, pool.memset(half[:], 0.5), p)
                    chain(pool, pool.affine_select(out=ident[:], in_=ones[:], compare_op=ALU.is_equal, fill=0.0,
                                                   base=0, pattern=[[-1, P]], channel_multiplier=1), p)
                    chain(pool, pool.affine_select(out=below[:], in_=ones[:], compare_op=ALU.is_gt, fill=0.0,
                                                   base=0, pattern=[[1, P]], channel_multiplier=-1), p)
                    chain(pool, pool.affine_select(out=earlier[:], in_=ones[:], compare_op=ALU.is_gt, fill=0.0,
                                                   base=0, pattern=[[-1, P]], channel_multiplier=1), p)
                    chain(pool, pool.tensor_copy(ident16[:], ident[:]), p)
                    chain(pool, pool.memset(later_chunk[:], 1.0), p)
                    for h in range(2):
                        chain(pool, pool.affine_select(out=later_chunk[:, h], in_=later_chunk[:, h], compare_op=ALU.is_gt,
                                                       fill=0.0, base=-h * HALF, pattern=[[1, N_CHUNKS]],
                                                       channel_multiplier=-1), p)
                    chain(pool, pool.iota(chunk_row[:], pattern=[[HALF * P, 2]], base=-1, channel_multiplier=P,
                                          allow_small_or_imprecise_dtypes=True), p)
                    chain(pool, pool.iota(lane_row[:], pattern=[[1, P]], base=0, channel_multiplier=0,
                                          allow_small_or_imprecise_dtypes=True), p)
                    chain(pool, pool.iota(tile_row[:], pattern=[[1, N_TILES]], base=0, channel_multiplier=0,
                                          allow_small_or_imprecise_dtypes=True), p)

        def edge_columns(keys_dram, vals_dram, order):
            with ExitStack() as local:
                rows = sb("edge_rows", [HALF, 2, 2, P], i32, local)
                rowsf = sb("edge_rowsf", [HALF, 2, 2, P], f32, local)
                diag = sb("edge_diag", [HALF, 2, HALF], f32, local)
                scrap = sb("edge_scrap", [HALF, 2, P], f32, local)
                key_part = sb("edge_key_part", [P, N_CHUNKS], i32, local)
                ends = sb("edge_ends", [HALF, 2], f32, local)
                block = local.enter_context(nc.Block())
                n_loads = 2 if vals_dram is None else 4
                parts = rows.rearrange("p h k e -> p h (k e)").rearrange("p h (e k) -> p h k e", k=2) \
                    if vals_dram is None else rows[:]

                @block.sync
                def _(sp):
                    for h in range(2):
                        if vals_dram is None:
                            sp.dma_start(rows[:, h].rearrange("p k e -> p (k e)"), keys_dram[h]).then_inc(once.handle, 16)
                        else:
                            sp.dma_start(rows[:, h, 0], keys_dram[h]).then_inc(once.handle, 16)
                            sp.dma_start(rows[:, h, 1], vals_dram[h]).then_inc(once.handle, 16)

                @block.tensor
                def _(pe):
                    pe.wait_ge(sig["v_step"].handle, sig["v_step"].after(1))
                    for h in range(2):
                        for which in range(2):
                            last = nc.tensor.transpose(banks[which][:, h * HALF:(h + 1) * HALF],
                                                       rowsf[:, h, which], ident[0:HALF, 0:HALF])
                    last.then_inc(sig["t_step"].handle, 1)
                    pe.wait_ge(sig["v_step"].handle, sig["v_step"].after(3))
                    nc.tensor.matmul(banks[2][0:HALF, 0:N_CHUNKS], ones[0:HALF, 0:HALF],
                                     diag[:].rearrange("p h c -> p (h c)"), start=True, stop=True)\
                      .then_inc(sig["t_step"].handle, 1)

                @block.vector
                def _(dve):
                    v = Signal(sig["v_step"].handle)
                    v.base = sig["v_step"].base
                    dve.wait_ge(once.handle, once.after(16 * n_loads))
                    chain(dve, dve.tensor_copy(rowsf[:], parts), v)
                    for h in range(2):
                        chain(dve, dve.tensor_scalar(diag[:, h], ident[0:HALF, 0:HALF], rowsf[:, h, 0, 0:1], None,
                                                     ALU.mult), v)
                    for h in range(2):
                        chain(dve, dve.scalar_tensor_tensor(scrap[:, h], rowsf[:, h, 0], rowsf[:, h, 0, 0:1],
                                                            ones[0:HALF, :], ALU.is_equal, ALU.mult,
                                                            accum_out=ends[:, h:h + 1]), v)
                    chain(dve, dve.tensor_tensor(order["join"][:], ends[:], chunk_row[:], ALU.add), v)
                    dve.wait_ge(sig["t_step"].handle, sig["t_step"].after(1))
                    chain(dve, dve.tensor_copy(order["key_f"][:], banks[0][:, 0:N_CHUNKS]), v)
                    chain(dve, dve.tensor_copy(order["value_f"][:], banks[1][:, 0:N_CHUNKS]), v)
                    chain(dve, dve.tensor_copy(order["key"][:], order["key_f"][:]), v)
                    chain(dve, dve.tensor_copy(order["value"][:], order["value_f"][:]), v)
                    for part, n, op in (("lane", P - 1, ALU.bitwise_and), ("tile", 7, ALU.arith_shift_right)):
                        chain(dve, dve.tensor_scalar(key_part[:], order["key"][:], n, None, op), v)
                        chain(dve, dve.tensor_copy(order[part][:], key_part[:]), v)
                    dve.wait_ge(sig["t_step"].handle, sig["t_step"].after(2))
                    for h in range(2):
                        chain(dve, dve.scalar_tensor_tensor(order["flow"][:, h], banks[2][0:HALF, 0:N_CHUNKS],
                                                            rowsf[:, h, 0, P - 1:P], later_chunk[:, h],
                                                            ALU.is_equal, ALU.mult), v)
            once.passed(16 * n_loads)
            sig["v_step"].passed(16)
            sig["t_step"].passed(2)

        A_ = 2 * UNROLL

        def side_room(where, select, count, sort):
            room = {}
            if select:
                room["diag"] = sb("diag", [P, 2, UNROLL, P], f32, where)
            if count:
                room["lane_hot"] = sb("lane_hot", [P, UNROLL, len(count), P], f16, where)
                room["tile_hot"] = sb("tile_hot", [P, UNROLL, len(count), N_TILES], f16, where)
                for name in ("total", "col_sum", "scan", "end", "empty"):
                    room[name] = sb(name, [P, len(count), N_TILES], f32, where)
            if sort:
                for name, width, dt in (("lane_hot", P, f16), ("tile_hot", N_TILES, f16), ("pairs", 2 * N_CHUNKS // A_, i32),
                                        ("lane_turned", P, f32), ("diag", P, f32), ("scrap", P, f32),
                                        ("scrap2", N_TILES, f32), ("base", N_TILES, f32), ("pair", 2, i32)):
                    room[name] = sb("sort_" + name, [P, A_, width], dt, where)
                for name, dt in (("rank", f32), ("ahead", f32), ("place", i32)):
                    room[name] = sb("sort_" + name, [P, A_], dt, where)
            return room

        def side_passed(select, count, sort):
            if select:
                sig["diag_done"].passed(N_CHUNKS // UNROLL)
                sig["keys_row"].passed(N_CHUNKS // UNROLL)
                sig["sel_done"].passed(N_CHUNKS)
            if count:
                sig["onehot"].passed(N_CHUNKS)
                sig["counted"].passed(N_CHUNKS + 1)
                sig["v_step"].passed((3 + 9) * len(count))
            if sort:
                for name in ("onehot", "diag_done", "row_counted", "turned", "found", "ranked", "weighed", "placed"):
                    sig[name].passed(N_CHUNKS)
                sig["based"].passed(N_CHUNKS + 1)
                for s in range(A_):
                    pair_sems[s].passed(16 * N_CHUNKS // A_)

        def select_act(act, order, room):
            dg, kr = sig["diag_done"], sig["keys_row"]
            if not order:
                return []

            def diagonal(c, s, r):
                b, j = s // UNROLL, s % UNROLL
                q = 2 * r + b
                if j == 0 and later(q, 2):
                    wait_apart(act, apart_act, (kr.handle, kr.after(q - 1)))
                ins = act.activation(room["diag"][:, b, j, :], ident[:], ACT.Copy, scale=order["key_f"][:, bass.ds(c, 1)])
                if j == UNROLL - 1:
                    ins.then_inc(dg.handle, 1)
            return [(0, diagonal)]

        def select_dve(dve, order, room):
            kr, sd = sig["keys_row"], sig["sel_done"]
            if not order:
                return []

            def compare(c, s, r):
                b, j = s // UNROLL, s % UNROLL
                q = 2 * r + b
                one = bass.ds(c, 1)
                if j == 0:
                    wait_apart(dve, apart_dve, (kr.handle, kr.after(q + 1)))
                dve.tensor_scalar(SEL[:, one, :].rearrange("p o m -> p (o m)"), banks[6 + b][:, j * P:(j + 1) * P],
                                  order["key_f"][:, one], None, ALU.is_equal).then_inc(sd.handle, 1)
            return [(5, compare)]

        def select_pe(pe, select, room):
            dg, kr, sd = sig["diag_done"], sig["keys_row"], sig["sel_done"]

            def keys_row(c, s, r):
                b, j = s // UNROLL, s % UNROLL
                q = 2 * r + b
                if j < UNROLL - 1:
                    return
                pe.wait_ge(dg.handle, dg.after(q + 1))
                if later(q, 2):
                    pe.wait_ge(sd.handle, sd.after(UNROLL * (q - 1)))
                nc.tensor.matmul(banks[6 + b][:], ones[:], room["diag"][:, b].rearrange("p j m -> p (j m)"),
                                 start=True, stop=True).then_inc(kr.handle, 1)
            return [(0, keys_row)] if select else []

        def count_dve(dve, count, room):
            def one_hot(c, s, r):
                b = s % UNROLL
                if later(c, UNROLL):
                    wait_apart(dve, apart_dve, (sig["counted"].handle, sig["counted"].after(c - UNROLL + 1)))
                for n, (order, _) in enumerate(count):
                    one = bass.ds(c, 1)
                    dve.tensor_scalar(room["lane_hot"][:, b, n], lane_row[:], order["lane"][:, one], None, ALU.is_equal)
                    last = dve.tensor_scalar(room["tile_hot"][:, b, n], tile_row[:], order["tile"][:, one], None,
                                             ALU.is_equal)
                last.then_inc(sig["onehot"].handle, 1)
            return [(0, one_hot)] if count else []

        def count_pe(pe, count, room):
            def multiply(c, s, r):
                b = s % UNROLL
                pe.wait_ge(sig["onehot"].handle, sig["onehot"].after(c + 1))
                for n in range(len(count)):
                    last = nc.tensor.matmul(banks[4 + n][:, 0:N_TILES], room["lane_hot"][:, b, n], room["tile_hot"][:, b, n],
                                            start=type(c) is int and c == 0, stop=type(c) is int and c == N_CHUNKS - 1)
                last.then_inc(sig["counted"].handle, 1)
            return [(1, multiply)] if count else []

        def count_end_pe(pe, count, room):
            if not count:
                return
            pe.wait_ge(sig["v_step"].handle, sig["v_step"].after(3 * len(count)))
            for n in range(len(count)):
                nc.tensor.matmul(banks[4 + n][:, 0:N_TILES], ones[:], room["total"][:, n], start=True, stop=True)
                last = nc.tensor.matmul(banks[4 + n][:, P:P + N_TILES], below[:], room["total"][:, n], start=True, stop=True)
            last.then_inc(sig["counted"].handle, 1)

        def count_end_dve(dve, count, room):
            if not count:
                return
            v = Signal(sig["v_step"].handle)
            v.base = sig["v_step"].base
            dve.wait_ge(sig["counted"].handle, sig["counted"].after(N_CHUNKS))
            for n, (order, clamp) in enumerate(count):
                total, inverse = room["total"][:, n], order["inverse"]
                chain(dve, dve.tensor_copy(total, banks[4 + n][:, 0:N_TILES]), v)
                chain(dve, dve.tensor_scalar(inverse[:], total, 1.0 if clamp else 0.0, None, ALU.max), v)
                chain(dve, dve.reciprocal(inverse[:], inverse[:]), v)
            dve.wait_ge(sig["counted"].handle, sig["counted"].after(N_CHUNKS + 1))
            for n, (order, _) in enumerate(count):
                total, first = room["total"][:, n], order["first"]
                col_sum, scan, end, empty = (room[k][:, n] for k in ("col_sum", "scan", "end", "empty"))
                chain(dve, dve.tensor_copy(col_sum, banks[4 + n][:, 0:N_TILES]), v)
                chain(dve, dve.tensor_tensor_scan(scan, ones[:, 0:N_TILES], col_sum, 0.0, ALU.mult, ALU.add), v)
                chain(dve, dve.tensor_tensor(scan, scan, col_sum, ALU.subtract), v)
                chain(dve, dve.scalar_tensor_tensor(first[:], banks[4 + n][:, P:P + N_TILES], 1.0, scan, ALU.mult,
                                                    ALU.add), v)
                chain(dve, dve.tensor_tensor(end, first[:], total, ALU.add), v)
                chain(dve, dve.tensor_scalar(empty, total, 0.5, None, ALU.is_lt), v)
                chain(dve, dve.tensor_scalar(col_sum, end, -1.0, E_PAD + 1.0, ALU.mult, ALU.add), v)
                chain(dve, dve.tensor_tensor(empty, empty, col_sum, ALU.mult), v)
                chain(dve, dve.scalar_tensor_tensor(order["last"][:], end, -1.0, empty, ALU.add, ALU.add), v)

        def pairs(room):
            return room["pairs"].rearrange("p a b -> p (a b)").rearrange("p (c k) -> p c k", k=2)

        def sort_start(dve, order, room):
            if order:
                for k, name in enumerate(("key", "value")):
                    last = dve.tensor_copy(pairs(room)[:, :, k:k + 1], order[name][:].unsqueeze(2))
                chain(dve, last, sig["t_step"])
                dve.tensor_copy(room["base"][:, 0], order["first"][:]).then_inc(sig["based"].handle, 1)

        def sort_dve(dve, order, room):
            g = sig

            def one_hot(c, s, r):
                one = bass.ds(c, 1)
                if later(c, A_):
                    wait_apart(dve, apart_dve, (g["row_counted"].handle, g["row_counted"].after(c - A_ + 1)),
                               (g["weighed"].handle, g["weighed"].after(c - A_ + 1)))
                dve.tensor_scalar(room["lane_hot"][:, s], lane_row[:], order["lane"][:, one], None, ALU.is_equal)
                dve.tensor_scalar(room["tile_hot"][:, s], tile_row[:], order["tile"][:, one], None, ALU.is_equal)\
                   .then_inc(g["onehot"].handle, 1)

            def count_on(c, s, r):
                n = 5 + 2 * (s % 2)
                one = bass.ds(c, 1)
                wait_apart(dve, apart_dve, (g["row_counted"].handle, g["row_counted"].after(c + 1)),
                           (g["based"].handle, g["based"].after(c + 1)))
                if later(c, A_):
                    wait_apart(dve, apart_dve, (g["found"].handle, g["found"].after(c - A_ + 2)))
                dve.tensor_tensor(room["base"][:, (s + 1) % A_], room["base"][:, s], banks[n][:, P:P + N_TILES], ALU.add)\
                   .then_inc(g["based"].handle, 1)
                dve.scalar_tensor_tensor(room["scrap"][:, s], banks[n][:, 0:P], order["key_f"][:, one], earlier[:],
                                         ALU.is_equal, ALU.mult, accum_out=room["rank"][:, s:s + 1])\
                   .then_inc(g["ranked"].handle, 1)

            def place(c, s, r):
                one = bass.ds(c, 1)
                wait_apart(dve, apart_dve, (g["found"].handle, g["found"].after(c + 1)))
                dve.scalar_tensor_tensor(room["scrap2"][:, s], banks[6][:, 0:N_TILES], 1.0, room["tile_hot"][:, s],
                                         ALU.mult, ALU.mult, accum_out=room["ahead"][:, s:s + 1])\
                   .then_inc(g["weighed"].handle, 1)
                if later(c, A_):
                    wait_apart(dve, apart_dve, (pair_sems[s].handle, pair_sems[s].after(16 * r)))
                dve.tensor_copy(room["pair"][:, s], pairs(room)[:, one].rearrange("p o k -> p (o k)"))

            def place_end(c, s, r):
                wait_apart(dve, apart_dve, (g["weighed"].handle, g["weighed"].after(c + 1)))
                dve.tensor_tensor(room["place"][:, s:s + 1], room["rank"][:, s:s + 1], room["ahead"][:, s:s + 1], ALU.add)\
                   .then_inc(g["placed"].handle, 1)
            return [(4, place), (2, count_on), (4, place_end), (0, one_hot)] if order else []

        def sort_pe(pe, order, room):
            g = sig

            def spread(c, s, r):
                n = 5 + 2 * (s % 2)
                pe.wait_ge(g["onehot"].handle, g["onehot"].after(c + 1))
                pe.wait_ge(g["diag_done"].handle, g["diag_done"].after(c + 1))
                if later(c, 1):
                    pe.wait_ge(g["turned"].handle, g["turned"].after(c))
                if later(c, 2):
                    pe.wait_ge(g["ranked"].handle, g["ranked"].after(c - 1))
                nc.tensor.transpose(banks[4].bitcast(f16)[:, 0:P], room["lane_hot"][:, s], ident16[:])
                nc.tensor.matmul(banks[n][:, 0:P], ones[:], room["diag"][:, s], start=True, stop=True)
                nc.tensor.matmul(banks[n][:, P:P + N_TILES], room["lane_hot"][:, s], room["tile_hot"][:, s], start=True,
                                 stop=True).then_inc(g["row_counted"].handle, 1)

            def look_up(c, s, r):
                pe.wait_ge(g["turned"].handle, g["turned"].after(c + 1))
                pe.wait_ge(g["based"].handle, g["based"].after(c + 1))
                if later(c, 1):
                    pe.wait_ge(g["weighed"].handle, g["weighed"].after(c))
                nc.tensor.matmul(banks[6][:, 0:N_TILES], room["lane_turned"][:, s], room["base"][:, s], start=True,
                                 stop=True).then_inc(g["found"].handle, 1)
            return [(1, spread), (3, look_up)] if order else []

        def sort_act(act, order, room):
            g = sig

            def turned(c, s, r):
                act.wait_ge(g["row_counted"].handle, g["row_counted"].after(c + 1))
                if later(c, A_):
                    act.wait_ge(g["found"].handle, g["found"].after(c - A_ + 1))
                act.activation(room["lane_turned"][:, s], banks[4].bitcast(f16)[:, 0:P], ACT.Copy)\
                   .then_inc(g["turned"].handle, 1)

            def diagonal(c, s, r):
                if later(c, A_):
                    act.wait_ge(g["row_counted"].handle, g["row_counted"].after(c - A_ + 1))
                act.activation(room["diag"][:, s], ident[:], ACT.Copy, scale=order["key_f"][:, bass.ds(c, 1)])\
                   .then_inc(g["diag_done"].handle, 1)
            return [(0, diagonal), (1, turned)] if order else []

        def sort_pool(pool, order, room):
            g = sig

            def put(c, s, r):
                wait_apart(pool, apart_pool, (g["placed"].handle, g["placed"].after(c + 1)))
                pool.indirect_dma_start(out=SORTED,
                                        out_offset=bass.IndirectOffsetOnAxis(ap=room["place"][:, s:s + 1], axis=0),
                                        in_=room["pair"][:, s], in_offset=None, bounds_check=E_PAD - 1,
                                        oob_is_err=False).then_inc(pair_sems[s].handle, 16)
            return [(7, put)] if order else []

        def sort_end(sp, order):
            if order:
                for s in range(A_):
                    wait_apart(sp, apart_sp, (pair_sems[s].handle, pair_sems[s].after(16 * N_CHUNKS // A_)))

        def weights_room(where, jobs):
            return sb("w_raw", [P, len(jobs), KT, D], f32, where) if jobs else None

        def load_weights(sp, raw, jobs, rows):
            for n, (w, _, _) in enumerate(jobs):
                sp.dma_start(raw[:, n], w.rearrange("(t p) n -> p t n", p=P)).then_inc(once.handle, 16)
            for row, tile in rows:
                sp.dma_start(tile[:], row.to_broadcast([P, D])).then_inc(once.handle, 16)

        def turn_weights(pe, raw, jobs, rows):
            if any(turn for _, _, turn in jobs):
                pe.wait_ge(once.handle, once.after(16 * (len(jobs) + len(rows))))
                for k in range(KT):
                    for m in range(KT):
                        last = nc.tensor.transpose(banks[4 + k][:, m * P:(m + 1) * P], raw[:, 0, m, k * P:(k + 1) * P],
                                                   ident[:])
                last.then_inc(sig["t_step"].handle, 1)

        def high_weights(act, raw, jobs, rows):
            if jobs or rows:
                act.wait_ge(once.handle, once.after(16 * (len(jobs) + len(rows))))
            for n, (_, w, turn) in enumerate(jobs):
                if turn:
                    act.wait_ge(sig["t_step"].handle, sig["t_step"].after(1))
                for k in range(KT):
                    act.activation(w[:, 0, k, :], banks[4 + k][:] if turn else raw[:, n, k, :], ACT.Copy, scale=W_SCALE)\
                       .then_inc(sig["w_hi"].handle, 1)

        def low_weights(dve, raw, jobs, rows):
            for n, (_, w, turn) in enumerate(jobs):
                for k in range(KT):
                    dve.wait_ge(sig["w_hi"].handle, sig["w_hi"].after(n * KT + k + 1))
                    dve.scalar_tensor_tensor(w[:, 1, k, :], banks[4 + k][:] if turn else raw[:, n, k, :], W_SCALE,
                                             w[:, 0, k, :], ALU.mult, ALU.subtract).then_inc(sig["w_lo"].handle, 1)

        def weights_passed(jobs, rows):
            once.passed(16 * (len(jobs) + len(rows)))
            sig["w_hi"].passed(KT * len(jobs))
            sig["w_lo"].passed(KT * len(jobs))
            sig["t_step"].passed(any(turn for _, _, turn in jobs))

        def split_weights(jobs, rows):
            with ExitStack() as local:
                raw = weights_room(local, jobs)
                block = local.enter_context(nc.Block())

                @block.sync
                def _(sp):
                    load_weights(sp, raw, jobs, rows)

                @block.tensor
                def _(pe):
                    turn_weights(pe, raw, jobs, rows)

                @block.scalar
                def _(act):
                    high_weights(act, raw, jobs, rows)

                @block.vector
                def _(dve):
                    low_weights(dve, raw, jobs, rows)
            weights_passed(jobs, rows)

        def products(bank_, left, w, ks, first, last):
            for k in ks:
                for a, b in ((0, 0), (1, 0), (0, 1)):
                    ins = nc.tensor.matmul(bank_[:], left[:, a, k, :], w[:, b, k, :],
                                           start=first and k == ks[0] and (a, b) == (0, 0),
                                           stop=last and k == ks[-1] and (a, b) == (0, 1))
            return ins

        def dense(x_in=None, own=None, order=None, exp_map=False, norm=True, log_map=False,
                  x_out=None, ht=False, attention=False, jobs=(), rows_=()):
            ins_of = [a for a in (x_in, own) if a is not None]
            combine = order is not None
            inverse = order["inverse"] if combine else None
            nl = len(ins_of)
            z_out = not attention
            ns = ht + (1 if z_out else 3)
            V = 2 * UNROLL
            F = 4 if exp_map else 2
            L = F + 2 if exp_map or log_map else F + 1
            R = L + 6 if log_map else L + 2

            def tiles(eng, steps):
                pipelined(eng, N_TILES,
                          [(lag, lambda t, w, r, step=step: step(t, w % UNROLL, 2 * r + w // UNROLL, w)) for lag, step in steps],
                          V)
            with ExitStack() as local:
                inX = sb("inX", [P, UNROLL, D], f32, local) if x_in is not None else None
                inU = sb("inU", [P, UNROLL, D], f32, local) if own is not None else None
                inG = sb("inG", [P, UNROLL, D], f32, local) if combine else None
                place = sb("place", [P, UNROLL], i32, local)
                raw = weights_room(local, jobs)
                y = sb("y", [P, UNROLL, D], f32, local) if combine else inX
                part = sb("part", [P, 2, D], f32, local)
                scrap = sb("scrap", [P, 2, D], f32, local)
                h = sb("h", [P, 2, D], f32, local)
                hT = sb("hT", [P, UNROLL, 2, KT, P], f16, local)
                zout = sb("zout", [P, UNROLL, 2, D], f16, local) if z_out else None
                zsum = sb("zsum", [P, UNROLL, D], f32, local) if log_map else None
                xl = sb("xl", [P, UNROLL, D], f32, local) if attention else None
                xr = sb("xr", [P, UNROLL, D], f32, local) if attention else None
                xh = sb("xh", [P, UNROLL, D], f32, local) if attention else None
                both = sb("both", [P, UNROLL, D], f32, local) if attention else None
                leaky = sb("leaky", [P, 2, D], f32, local) if attention else None
                six = sb("six", [P, V, 6], f32, local)
                mv = sb("mv", [P, V, 2], f32, local)
                small = sb("small", [P, V, 24], f32, local)
                VAR, RSTD, LNB, SS, NORM, NC_, REC, TANH, FAC = 0, 1, 2, 3, 4, 6, 8, 10, 11
                Q, LNQ, N2, SER, MASK, DIF, ONEP = 12, 13, 14, 15, 16, 17, 18

                nb = 4 if log_map else 2

                def sm(w, k, n=1):
                    return small[:, w, k:k + n]
                block = local.enter_context(nc.Block())
                g = sig
                rows = lambda t: bass.ds(t * P, P)

                @block.sync
                def _(sp):
                    def loads(t, s, r, w):
                        if later(t, UNROLL):
                            used = g["combined"] if combine else g["h_done"]
                            wait_apart(sp, apart_sp, (used.handle, used.after(t - UNROLL + 1)))
                        if x_in is not None:
                            sp.dma_start(inX[:, s], x_in[rows(t), :]).then_inc(load[s].handle, 16)
                        if own is not None:
                            sp.dma_start(inU[:, s], own[rows(t), :]).then_inc(load[s].handle, 16)

                    def stores(t, s, r, w):
                        wait_apart(sp, apart_sp, (g["out_lo"].handle, g["out_lo"].after(t + 1)))
                        if z_out:
                            sp.dma_start(Z[rows(t), :], zout[:, s].rearrange("p a n -> p (a n)")).then_inc(store[s].handle, 16)
                        else:
                            wait_apart(sp, apart_sp, (g["out_hi"].handle, g["out_hi"].after(t + 1)))
                            sp.dma_start(XL[rows(t), :], xl[:, s]).then_inc(store[s].handle, 16)
                            sp.dma_start(XR[rows(t), :], xr[:, s]).then_inc(store[s].handle, 16)
                            wait_apart(sp, apart_sp, (g["x_step"].handle, g["x_step"].after(t + 1)))
                            sp.dma_start(XH[rows(t), :], xh[:, s]).then_inc(store[s].handle, 16)
                        if ht:
                            sp.dma_start(HT[bass.ds(t, 1)].rearrange("o p n -> (o p) n"),
                                         hT[:, s].rearrange("p a k n -> p (a k n)")).then_inc(store[s].handle, 16)

                    def keep(t, s, r, w):
                        wait_apart(sp, apart_sp, (g["combined"].handle, g["combined"].after(t + 1)))
                        sp.dma_start(x_out[rows(t), :], y[:, s]).then_inc(kept[s].handle, 16)
                    load_weights(sp, raw, jobs, rows_)
                    tiles(sp, ([(F + 2, keep)] if x_out is not None else []) + [(R + 1, stores), (0, loads)])
                    for s in range(UNROLL):
                        wait_apart(sp, apart_sp, (store[s].handle, store[s].after(16 * ns * N_TILES // UNROLL)))
                        if x_out is not None:
                            wait_apart(sp, apart_sp, (kept[s].handle, kept[s].after(16 * N_TILES // UNROLL)))

                @block.vector
                def _(dve):
                    def ready(t, s, r):
                        if nl:
                            wait_apart(dve, apart_dve, (load[s].handle, load[s].after((r + 1) * (16 * nl))))
                        if combine:
                            wait_apart(dve, apart_dve, (gather[s].handle, gather[s].after(16 * (r + 1))))
                        if combine and later(t, UNROLL):
                            dve.wait_ge(g["h_done"].handle, g["h_done"].after(t - UNROLL + 1))
                            if x_out is not None:
                                dve.wait_ge(kept[s].handle, kept[s].after(16 * r))
                            if attention:
                                dve.wait_ge(g["x_step"].handle, g["x_step"].after(t - UNROLL + 1))

                    def begin(t, s, r, w):
                        if exp_map:
                            dve.wait_ge(g["norm"].handle, g["norm"].after(t + 1))
                            dve.reciprocal(sm(w, REC), sm(w, NC_)).then_inc(g["y_step"].handle, 1)
                        elif combine and x_in is not None:
                            ready(t, s, r)
                            wait_apart(dve, apart_dve)
                            dve.scalar_tensor_tensor(part[:, s % 2], inG[:, s], inverse[:, bass.ds(t, 1)], inU[:, s],
                                                     ALU.mult, ALU.add).then_inc(g["y_step"].handle, 1)
                        elif combine:
                            ready(t, s, r)
                            wait_apart(dve, apart_dve)
                            dve.scalar_tensor_tensor(y[:, s], inG[:, s], inverse[:, bass.ds(t, 1)], inU[:, s],
                                                     ALU.mult, ALU.add).then_inc(g["combined"].handle, 1)
                        else:
                            ready(t, s, r)

                    def go_on(t, s, r, w):
                        if exp_map:
                            dve.wait_ge(g["a_step"].handle, g["a_step"].after(t + 1))
                            wait_apart(dve, apart_dve, (g["y_step"].handle, g["y_step"].after(2 * t + 1)))
                            dve.scalar_tensor_tensor(sm(w, FAC), sm(w, TANH), sm(w, REC), inverse[:, bass.ds(t, 1)],
                                                     ALU.mult, ALU.mult).then_inc(g["y_step"].handle, 1)
                        elif combine and x_in is not None:
                            dve.wait_ge(g["y_step"].handle, g["y_step"].after(t + 1))
                            dve.tensor_tensor(y[:, s], part[:, s % 2], inX[:, s], ALU.add)\
                               .then_inc(g["combined"].handle, 1)

                    def go_on2(t, s, r, w):
                        if exp_map:
                            ready(t, s, r)
                            wait_apart(dve, apart_dve, (g["y_step"].handle, g["y_step"].after(2 * t + 2)))
                            dve.scalar_tensor_tensor(y[:, s], inG[:, s], sm(w, FAC), inX[:, s], ALU.mult,
                                                     ALU.add).then_inc(g["combined"].handle, 1)

                    def statistics(t, s, r, w):
                        if norm:
                            if combine:
                                dve.wait_ge(g["combined"].handle, g["combined"].after(t + 1))
                            dve.bn_stats(six[:, w], y[:, s]).then_inc(g["stats"].handle, 1)

                    def mean_and_variance(t, s, r, w):
                        if norm:
                            wait_apart(dve, apart_dve, (g["stats"].handle, g["stats"].after(t + 1)))
                            dve.bn_aggr(mv[:, w], six[:, w]).then_inc(g["aggr"].handle, 1)

                    def log_factor(t, s, r, w):
                        v = g["ranked"]
                        dve.wait_ge(g["norm"].handle, g["norm"].after(t + 1))
                        dve.reciprocal(sm(w, REC), sm(w, NC_)).then_inc(v.handle, 1)
                        dve.wait_ge(g["a_step"].handle, g["a_step"].after(t + 1))
                        dve.tensor_tensor(sm(w, LNQ), sm(w, ONEP), sm(w, Q), ALU.subtract).then_inc(v.handle, 1)

                    def log_factor_end(t, s, r, w):
                        v = g["sel_done"]
                        wait_apart(dve, apart_dve, (g["ranked"].handle, g["ranked"].after(2 * t + 2)))
                        dve.tensor_scalar(sm(w, LNQ), sm(w, LNQ), sm(w, REC), 0.5 / W_SCALE, ALU.mult, ALU.mult).then_inc(v.handle, 1)
                        wait_apart(dve, apart_dve, (v.handle, v.after(2 * t + 1)), (g["placed"].handle, g["placed"].after(t + 1)))
                        dve.scalar_tensor_tensor(sm(w, DIF), sm(w, SER), 1.0 / W_SCALE, sm(w, LNQ), ALU.mult, ALU.subtract).then_inc(v.handle, 1)
                        wait_apart(dve, apart_dve, (v.handle, v.after(2 * t + 2)))
                        dve.scalar_tensor_tensor(sm(w, FAC), sm(w, DIF), sm(w, MASK), sm(w, LNQ), ALU.mult,
                                                 ALU.add).then_inc(g["weighed"].handle, 1)

                    def low(t, s, r, w):
                        dve.wait_ge(g["hi_done"].handle, g["hi_done"].after(t + 1))
                        dve.tensor_tensor(hT[:, s, 1].rearrange("p k n -> p (k n)"), banks[s % 2][:],
                                          hT[:, s, 0].rearrange("p k n -> p (k n)"), ALU.subtract)\
                           .then_inc(g["lo_done"].handle, 1)

                    def results_sum(t, s, r, w):
                        dve.wait_ge(g["weighed"].handle, g["weighed"].after(t + 1))
                        dve.wait_ge(g["product"].handle, g["product"].after(t + 1))
                        if later(t, UNROLL):
                            dve.wait_ge(g["out_lo"].handle, g["out_lo"].after(t - UNROLL + 1))
                        dve.scalar_tensor_tensor(zsum[:, s], banks[2 + s % nb][:], sm(w, FAC), bias_out[:], ALU.mult,
                                                 ALU.add).then_inc(g["out_sum"].handle, 1)

                    def results(t, s, r, w):
                        if log_map:
                            dve.wait_ge(g["out_hi"].handle, g["out_hi"].after(t + 1))
                            dve.tensor_tensor(zout[:, s, 1], zsum[:, s], zout[:, s, 0], ALU.subtract)\
                               .then_inc(g["out_lo"].handle, 1)
                        elif z_out:
                            dve.wait_ge(g["out_hi"].handle, g["out_hi"].after(t + 1))
                            dve.scalar_tensor_tensor(zout[:, s, 1], banks[2 + s % nb][:], 1.0 / W_SCALE, zout[:, s, 0],
                                                     ALU.mult, ALU.subtract).then_inc(g["out_lo"].handle, 1)
                        else:
                            dve.wait_ge(g["product"].handle, g["product"].after(t + 1))
                            if later(t, UNROLL):
                                dve.wait_ge(store[s].handle, store[s].after(r * (16 * ns)))
                                dve.wait_ge(g["p_step"].handle, g["p_step"].after(t - UNROLL + 1))
                            dve.tensor_scalar(xr[:, s], banks[4 + s % 2][:], 1.0 / W_SCALE, None, ALU.mult)\
                               .then_inc(g["out_lo"].handle, 1)
                    def own_leaky(t, s, r, w):
                        dve.wait_ge(g["p_step"].handle, g["p_step"].after(t + 1))
                        if later(t, 2):
                            wait_apart(dve, apart_dve, (g["sel_done"].handle, g["sel_done"].after(t - 1)))
                        dve.scalar_tensor_tensor(leaky[:, s % 2], both[:, s], 0.2, both[:, s], ALU.mult, ALU.max)\
                           .then_inc(g["diag_done"].handle, 1)

                    def own_product(t, s, r, w):
                        wait_apart(dve, apart_dve, (g["diag_done"].handle, g["diag_done"].after(t + 1)))
                        dve.tensor_tensor(both[:, s], leaky[:, s % 2], att_row[:], ALU.mult).then_inc(g["sel_done"].handle, 1)

                    def own_sums(t, s, r, w):
                        wait_apart(dve, apart_dve, (g["sel_done"].handle, g["sel_done"].after(t + 1)))
                        dve.tensor_reduce(own_scores[:, bass.ds(t, 1), :].rearrange("p o h -> p (o h)"),
                                          both[:, s].rearrange("p (h k) -> p h k", h=HEADS), AX.X, ALU.add)\
                           .then_inc(g["ranked"].handle, 1)
                    steps = [(F, begin), (R, results), (F, go_on)]
                    if log_map:
                        steps += [(L + 4, log_factor_end), (F, statistics), (L, low), (F, mean_and_variance),
                                  (L + 4, results_sum), (L + 3, log_factor)]
                    elif attention:
                        steps += [(R + 2, own_leaky), (F, statistics), (R + 2, own_product), (F, mean_and_variance), (L, low),
                                  (R + 2, own_sums)]
                    else:
                        steps = [(F, begin), (F, go_on), (F, go_on2), (F, statistics), (F, mean_and_variance),
                                 (R, results), (L, low)]
                    low_weights(dve, raw, jobs, rows_)
                    tiles(dve, steps)

                @block.gpsimd
                def _(pool):
                    def places(t, s, r, w):
                        if later(t, UNROLL):
                            wait_apart(pool, apart_pool, (gather[s].handle, gather[s].after(16 * r)))
                        pool.tensor_copy(place[:, s:s + 1], order["last"][:, bass.ds(t, 1)]).then_inc(g["looked"].handle, 1)

                    def gathers(t, s, r, w):
                        if later(t, UNROLL):
                            wait_apart(pool, apart_pool, (g["combined"].handle, g["combined"].after(t - UNROLL + 1)))
                        wait_apart(pool, apart_pool, (g["looked"].handle, g["looked"].after(t + 1)))
                        pool.indirect_dma_start(out=inG[:, s], out_offset=None, in_=AGG,
                                                in_offset=bass.IndirectOffsetOnAxis(ap=place[:, s:s + 1], axis=0),
                                                bounds_check=E_PAD, oob_is_err=False).then_inc(gather[s].handle, 16)

                    def mean_norm(t, s, r, w):
                        n = g["pow_step"]
                        wait_apart(pool, apart_pool, (g["squares"].handle, g["squares"].after(t + 1)))
                        pool.tensor_tensor(out=sm(w, NORM), in0=sm(w, SS), in1=half[:], op=ALU.pow).then_inc(n.handle, 1)
                        wait_apart(pool, apart_pool, (n.handle, n.after(t + 1)))
                        pool.tensor_scalar(sm(w, NC_), sm(w, NORM), EPS_HYP, None, ALU.max).then_inc(g["norm"].handle, 1)

                    def ln_scale(t, s, r, w):
                        wait_apart(pool, apart_pool, (g["aggr"].handle, g["aggr"].after(t + 1)))
                        pool.tensor_scalar(sm(w, VAR), mv[:, w, 1:2], EPS_LN, None, ALU.add)\
                            .then_inc(g["eps_added"].handle, 1)
                        wait_apart(pool, apart_pool, (g["eps_added"].handle, g["eps_added"].after(t + 1)))
                        pool.tensor_tensor(out=sm(w, RSTD), in0=sm(w, VAR), in1=neg_half[:], op=ALU.pow)\
                            .then_inc(g["rstd"].handle, 1)
                        wait_apart(pool, apart_pool, (g["rstd"].handle, g["rstd"].after(t + 1)))
                        pool.tensor_scalar(sm(w, LNB), mv[:, w, 0:1], sm(w, RSTD), -1.0, ALU.mult, ALU.mult)\
                            .then_inc(g["bias_ln"].handle, 1)

                    def norm_of_h(t, s, r, w):
                        wait_apart(pool, apart_pool, (g["squares"].handle, g["squares"].after(t + 1)))
                        pool.tensor_tensor(out=sm(w, NORM), in0=sm(w, SS), in1=half[:], op=ALU.pow)\
                            .then_inc(g["pow_step"].handle, 1)

                    def clip(t, s, r, w):
                        wait_apart(pool, apart_pool, (g["pow_step"].handle, g["pow_step"].after(t + 1)))
                        pool.tensor_scalar(sm(w, NC_), sm(w, NORM), EPS_HYP, CLIP_HYP, ALU.max, ALU.min)\
                            .then_inc(g["norm"].handle, 1)

                    def square(t, s, r, w):
                        wait_apart(pool, apart_pool, (g["norm"].handle, g["norm"].after(t + 1)))
                        pool.tensor_tensor(out=sm(w, N2), in0=sm(w, NC_), in1=sm(w, NC_), op=ALU.mult)\
                            .then_inc(g["p_step"].handle, 1)
                        pool.tensor_scalar(sm(w, MASK), sm(w, NC_), 0.1, None, ALU.is_lt)

                    def series(t, s, r, w):
                        m = g["found"]
                        wait_apart(pool, apart_pool, (g["p_step"].handle, g["p_step"].after(t + 1)))
                        pool.tensor_scalar(sm(w, SER), sm(w, N2), 1.0 / 7, 1.0 / 5, ALU.mult, ALU.add).then_inc(m.handle, 1)
                        wait_apart(pool, apart_pool, (m.handle, m.after(2 * t + 1)))
                        pool.tensor_scalar(sm(w, SER + 5), sm(w, SER), sm(w, N2), 1.0 / 3, ALU.mult, ALU.add).then_inc(m.handle, 1)
                        wait_apart(pool, apart_pool, (m.handle, m.after(2 * t + 2)))
                        pool.tensor_scalar(sm(w, SER), sm(w, SER + 5), sm(w, N2), 1.0, ALU.mult, ALU.add)\
                            .then_inc(g["placed"].handle, 1)

                    def residual(t, s, r, w):
                        wait_apart(pool, apart_pool, (g["h_done"].handle, g["h_done"].after(t + 1)))
                        if later(t, UNROLL):
                            wait_apart(pool, apart_pool, (store[s].handle, store[s].after(r * (16 * ns))))
                        pool.tensor_tensor(out=xh[:, s], in0=y[:, s], in1=h[:, s % 2], op=ALU.add)\
                            .then_inc(g["x_step"].handle, 1)
                    def add(t, s, r, w):
                        wait_apart(pool, apart_pool, (g["out_lo"].handle, g["out_lo"].after(t + 1)))
                        wait_apart(pool, apart_pool, (g["out_hi"].handle, g["out_hi"].after(t + 1)))
                        if later(t, UNROLL):
                            wait_apart(pool, apart_pool, (g["ranked"].handle, g["ranked"].after(t - UNROLL + 1)))
                        pool.tensor_tensor(out=both[:, s], in0=xl[:, s], in1=xr[:, s], op=ALU.add)\
                            .then_inc(g["p_step"].handle, 1)
                    steps = ([(3, mean_norm)] if exp_map else []) + ([(L + 1, norm_of_h), (0, places), (L + 1, clip), (0, gathers), (L + 1, square)] if log_map else
                                [(0, places), (0, gathers)] if combine else []) \
                        + ([(R + 1, add), (L + 1, residual)] if attention else []) \
                        + ([(L + 2, series)] if log_map else []) + ([(F, ln_scale)] if norm else [])
                    if steps:
                        tiles(pool, steps)

                @block.scalar
                def _(act):
                    def mean_squares(t, s, r, w):
                        wait_apart(act, apart_act, (gather[s].handle, gather[s].after(16 * (r + 1))))
                        if later(t, 2):
                            wait_apart(act, apart_act, (g["squares"].handle, g["squares"].after(t - 1)))
                        act.activation(scrap[:, s % 2], inG[:, s], ACT.Square, scale=inverse[:, bass.ds(t, 1)],
                                       accum_out=sm(w, SS)).then_inc(g["squares"].handle, 1)

                    def tanh_norm(t, s, r, w):
                        act.wait_ge(g["norm"].handle, g["norm"].after(t + 1))
                        act.activation(sm(w, TANH), sm(w, NC_), ACT.Tanh).then_inc(g["a_step"].handle, 1)

                    def hidden(t, s, r, w):
                        if later(t, 2):
                            act.wait_ge(g["transposed"].handle, g["transposed"].after(t - 1))
                            if attention:
                                act.wait_ge(g["x_step"].handle, g["x_step"].after(t - 1))
                        if norm:
                            act.wait_ge(g["bias_ln"].handle, g["bias_ln"].after(t + 1))
                            act.activation(h[:, s % 2], y[:, s], ACT.Relu, bias=sm(w, LNB), scale=sm(w, RSTD))\
                               .then_inc(g["h_done"].handle, 1)
                        else:
                            act.wait_ge(g["combined"].handle, g["combined"].after(t + 1))
                            act.activation(h[:, s % 2], y[:, s], ACT.Relu).then_inc(g["h_done"].handle, 1)
                        if log_map:
                            wait_apart(act, apart_act, (g["h_done"].handle, g["h_done"].after(t + 1)))
                            act.activation(scrap[:, s % 2], h[:, s % 2], ACT.Square, accum_out=sm(w, SS))\
                               .then_inc(g["squares"].handle, 1)

                    def high(t, s, r, w):
                        act.wait_ge(g["transposed"].handle, g["transposed"].after(t + 1))
                        if later(t, UNROLL):
                            act.wait_ge(g["product"].handle, g["product"].after(t - UNROLL + 1))
                            if ht:
                                act.wait_ge(store[s].handle, store[s].after(r * (16 * ns)))
                        act.activation(hT[:, s, 0].rearrange("p k n -> p (k n)"), banks[s % 2][:], ACT.Copy)\
                           .then_inc(g["hi_done"].handle, 1)

                    def results(t, s, r, w):
                        if later(t, UNROLL):
                            act.wait_ge(store[s].handle, store[s].after(r * (16 * ns)))
                            if attention:
                                act.wait_ge(g["p_step"].handle, g["p_step"].after(t - UNROLL + 1))
                        if log_map:
                            act.wait_ge(g["out_sum"].handle, g["out_sum"].after(t + 1))
                            act.activation(zout[:, s, 0], zsum[:, s], ACT.Copy).then_inc(g["out_hi"].handle, 1)
                        else:
                            act.wait_ge(g["product"].handle, g["product"].after(t + 1))
                            act.activation(zout[:, s, 0] if z_out else xl[:, s], banks[2 + s % 2][:], ACT.Copy,
                                           scale=1.0 / W_SCALE).then_inc(g["out_hi"].handle, 1)

                    def log_norm(t, s, r, w):
                        act.wait_ge(g["norm"].handle, g["norm"].after(t + 1))
                        act.activation(sm(w, ONEP), sm(w, NC_), ACT.Ln, bias=ones[:, 0:1])
                        act.activation(sm(w, Q), sm(w, NC_), ACT.Ln, bias=ones[:, 0:1], scale=-1.0)\
                           .then_inc(g["a_step"].handle, 1)
                    steps = [(L, hidden), (L + 5 if log_map else L + 2, results), (L, high)]
                    if exp_map:
                        steps = [(2, mean_squares), (3, tanh_norm)] + steps
                    if log_map:
                        steps = [(L + 2, log_norm)] + steps
                    high_weights(act, raw, jobs, rows_)
                    tiles(act, steps)

                @block.tensor
                def _(pe):
                    def turn(t, s, r, w):
                        pe.wait_ge(g["h_done"].handle, g["h_done"].after(t + 1))
                        if later(t, 2):
                            pe.wait_ge(g["lo_done"].handle, g["lo_done"].after(t - 1))
                        for k in range(KT):
                            last = nc.tensor.transpose(banks[s % 2][:, k * P:(k + 1) * P], h[:, s % 2, k * P:(k + 1) * P],
                                                       ident[:])
                        last.then_inc(g["transposed"].handle, 1)

                    def multiply(t, s, r, w):
                        pe.wait_ge(g["lo_done"].handle, g["lo_done"].after(t + 1))
                        if later(t, nb):
                            b = g["out_sum"] if log_map else g["out_lo"]
                            pe.wait_ge(b.handle, b.after(t - nb + 1))
                            if attention:
                                pe.wait_ge(g["out_hi"].handle, g["out_hi"].after(t - 1))
                        last = products(banks[2 + s % nb], hT[:, s], w_out, range(KT), True, True)
                        if attention:
                            last = products(banks[4 + s % 2], hT[:, s], w_out2, range(KT), True, True)
                        last.then_inc(g["product"].handle, 1)
                    tiles(pe, [(0, turn), (1, multiply)])
            for s in range(UNROLL):
                load[s].passed(16 * nl * N_TILES // UNROLL)
                store[s].passed(16 * ns * N_TILES // UNROLL)
                gather[s].passed(16 * combine * N_TILES // UNROLL)
                kept[s].passed(16 * (x_out is not None) * N_TILES // UNROLL)
            weights_passed(jobs, rows_)
            done = {"looked": combine, "h_done": 1, "transposed": 1, "hi_done": 1, "lo_done": 1, "product": 1, "out_hi": 1, "out_lo": 1,
                    "combined": combine, "stats": norm, "aggr": norm, "rstd": norm, "bias_ln": norm, "eps_added": norm,
                    "squares": exp_map or log_map, "norm": exp_map or log_map, "pow_step": exp_map or log_map,
                    "a_step": exp_map or log_map, "x_step": attention, "out_sum": log_map, "weighed": log_map,
                    "placed": log_map, "sel_done": 2 * log_map + attention, "diag_done": attention, "ranked": 2 * log_map + attention, "p_step": log_map + attention, "found": 2 * log_map,
                    "y_step": 2 * exp_map + (combine and x_in is not None and not exp_map)}
            for name, n in done.items():
                g[name].passed(int(n) * N_TILES)

        def aggregate(order, own=False, jobs=(), rows_=(), select=False, count=(), sort=None):
            A = 2 * UNROLL
            late = A if select else 0
            with ExitStack() as local:
                side = side_room(local, select, count, sort)
                rows_in = sb("rows_in", [P, A, 2, D], f16, local)
                sums = sb("sums", [P, A, D], f32, local)
                idx = sb("idx", [P, A], i32, local)
                hT = sb("hT_in", [P, UNROLL, 2, KT, P], f16, local) if own else None
                u = sb("u_out", [P, UNROLL, D], f32, local) if own else None
                raw = weights_room(local, jobs)
                block = local.enter_context(nc.Block())
                g = sig
                got = gather + scatter
                put = put_sems

                @block.sync
                def _(sp):
                    def sums_store(c, s, r):
                        wait_apart(sp, apart_sp, (g["sums_out"].handle, g["sums_out"].after(c + 1)))
                        sp.dma_start(AGG[bass.ds(c * P, P), :], sums[:, s]).then_inc(put[s].handle, 16)

                    def own_load(c, s, r):
                        if s % 2:
                            return
                        t = r * UNROLL + s // 2
                        if later(t, UNROLL):
                            wait_apart(sp, apart_sp, (g["own_product"].handle, g["own_product"].after(t - UNROLL + 1)))
                        sp.dma_start(hT[:, s // 2].rearrange("p a k n -> p (a k n)"),
                                     HT[bass.ds(t, 1)].rearrange("o p n -> (o p) n")).then_inc(own_in[s // 2].handle, 16)

                    def own_store(c, s, r):
                        if s % 2:
                            return
                        t = r * UNROLL + s // 2
                        wait_apart(sp, apart_sp, (g["own_out"].handle, g["own_out"].after(t + 1)))
                        sp.dma_start(U[bass.ds(t * P, P), :], u[:, s // 2]).then_inc(store[s // 2].handle, 16)
                    load_weights(sp, raw, jobs, rows_)
                    pipelined(sp, N_CHUNKS, ([(0, own_load), (6, own_store)] if own else []) + [(5 + late, sums_store)], A)
                    sort_end(sp, sort)
                    if own:
                        for s in range(UNROLL):
                            wait_apart(sp, apart_sp, (store[s].handle, store[s].after(16 * N_TILES // UNROLL)))
                    for s in range(A):
                        wait_apart(sp, apart_sp, (put[s].handle, put[s].after(16 * N_CHUNKS // A)))

                @block.gpsimd
                def _(pool):
                    def gathers(c, s, r):
                        wait_apart(pool, apart_pool, (g["looked"].handle, g["looked"].after(c + 1)))
                        if later(c, A):
                            wait_apart(pool, apart_pool, (g["summed"].handle, g["summed"].after(c - A + 1)))
                        pool.indirect_dma_start(out=rows_in[:, s].rearrange("p a n -> p (a n)"), out_offset=None, in_=Z,
                                                in_offset=bass.IndirectOffsetOnAxis(ap=idx[:, s:s + 1], axis=0),
                                                bounds_check=N_PAD - 1, oob_is_err=False).then_inc(got[s].handle, 16)
                    pipelined(pool, N_CHUNKS, [(0, gathers)] + sort_pool(pool, sort, side), A)

                @block.tensor
                def _(pe):
                    def sum_up(c, s, r):
                        if select:
                            pe.wait_ge(g["sel_done"].handle, g["sel_done"].after(c + 1))
                        pe.wait_ge(got[s].handle, got[s].after(16 * (r + 1)))
                        if later(c, 2):
                            pe.wait_ge(g["sums_out"].handle, g["sums_out"].after(c - 1))
                        sel = SEL[:, bass.ds(c, 1), :].rearrange("p o m -> p (o m)")
                        nc.tensor.matmul(banks[s % 2][:], sel, rows_in[:, s, 0], start=True, stop=False)
                        nc.tensor.matmul(banks[s % 2][:], sel, rows_in[:, s, 1], start=False, stop=True)\
                          .then_inc(g["summed"].handle, 1)

                    def own_part(c, s, r):
                        t = r * UNROLL + s // 2
                        b = 2 + s // 2 % 2
                        if s % 2 == 0:
                            pe.wait_ge(own_in[s // 2].handle, own_in[s // 2].after(16 * (r + 1)))
                            if later(t, 2):
                                pe.wait_ge(g["own_out"].handle, g["own_out"].after(t - 1))
                            products(banks[b], hT[:, s // 2], w_own, range(0, KT // 2), True, False)
                        else:
                            products(banks[b], hT[:, s // 2], w_own, range(KT // 2, KT), False, True)\
                                .then_inc(g["own_product"].handle, 1)
                    turn_weights(pe, raw, jobs, rows_)
                    pipelined(pe, N_CHUNKS, select_pe(pe, select, side) + count_pe(pe, count, side) + sort_pe(pe, sort, side)
                              + ([(0, own_part)] if own else []) + [(late, sum_up)], A, end=1)
                    count_end_pe(pe, count, side)

                @block.scalar
                def _(act):
                    def evict(c, s, r):
                        act.wait_ge(g["summed"].handle, g["summed"].after(c + 1))
                        if later(c, A):
                            act.wait_ge(put[s].handle, put[s].after(16 * r))
                        act.activation(sums[:, s], banks[s % 2][:], ACT.Copy).then_inc(g["sums_out"].handle, 1)
                    high_weights(act, raw, jobs, rows_)
                    pipelined(act, N_CHUNKS, select_act(act, select and order, side) + sort_act(act, sort, side)
                              + [(1 + late, evict)], A)

                @block.vector
                def _(dve):
                    def indices(c, s, r):
                        if later(c, A):
                            wait_apart(dve, apart_dve, (got[s].handle, got[s].after(16 * r)))
                        dve.tensor_copy(idx[:, s:s + 1], order["value"][:, bass.ds(c, 1)]).then_inc(g["looked"].handle, 1)

                    def own_evict(c, s, r):
                        if s % 2 == 0:
                            return
                        t = r * UNROLL + s // 2
                        dve.wait_ge(g["own_product"].handle, g["own_product"].after(t + 1))
                        if later(t, UNROLL):
                            dve.wait_ge(store[s // 2].handle, store[s // 2].after(16 * r))
                        dve.scalar_tensor_tensor(u[:, s // 2], banks[2 + s // 2 % 2][:], 1.0 / W_SCALE, bias_own[:],
                                                 ALU.mult, ALU.add).then_inc(g["own_out"].handle, 1)
                    low_weights(dve, raw, jobs, rows_)
                    sort_start(dve, sort, side)
                    pipelined(dve, N_CHUNKS, [(0, indices)] + select_dve(dve, select and order, side)
                              + count_dve(dve, count, side) + sort_dve(dve, sort, side)
                              + ([(1, own_evict)] if own else []), A)
                    count_end_dve(dve, count, side)
            for s in range(UNROLL):
                for d_ in (gather, scatter):
                    d_[s].passed(16 * N_CHUNKS // A)
                if own:
                    own_in[s].passed(16 * N_TILES // UNROLL)
                    store[s].passed(16 * N_TILES // UNROLL)
            for s in range(A):
                put[s].passed(16 * N_CHUNKS // A)
            for name in ("summed", "looked", "sums_out"):
                g[name].passed(N_CHUNKS)
            side_passed(select, count, sort)
            if own:
                g["own_product"].passed(N_TILES)
                g["own_out"].passed(N_TILES)
            weights_passed(jobs, rows_)

        def join_chunks(table, width, order):
            full = table.shape[1]
            with ExitStack() as local:
                tails = sb("tails", [HALF, 2, width], f32, local)
                fixed = sb("fixed", [HALF, 2, full], f32, local)
                block = local.enter_context(nc.Block())
                v0, t0 = sig["v_step"], sig["t_step"]

                @block.sync
                def _(sp):
                    sp.dma_start(tails[:], bass.AP(table.tensor, (P - 1) * full,
                                                   [[P * full, HALF], [HALF * P * full, 2], [1, width]]))\
                      .then_inc(once.handle, 16)

                @block.gpsimd
                def _(pool):
                    for h in range(2):
                        pool.indirect_dma_start(out=fixed[:, h], out_offset=None, in_=table,
                                                in_offset=bass.IndirectOffsetOnAxis(ap=order["join"][:, h:h + 1], axis=0),
                                                bounds_check=E_PAD - 1, oob_is_err=False).then_inc(gather[h].handle, 16)
                    pool.wait_ge(once.handle, once.after(16))
                    for h in range(2):
                        pool.wait_ge(v0.handle, v0.after(h + 1))
                        pool.indirect_dma_start(out=table,
                                                out_offset=bass.IndirectOffsetOnAxis(ap=order["join"][:, h:h + 1], axis=0),
                                                in_=fixed[:, h], in_offset=None,
                                                bounds_check=E_PAD - 1, oob_is_err=False).then_inc(scatter[h].handle, 16)
                    for h in range(2):
                        pool.wait_ge(scatter[h].handle, scatter[h].after(16))

                @block.tensor
                def _(pe):
                    pe.wait_ge(once.handle, once.after(16))
                    for h in range(2):
                        for first in range(0, width, BANK):
                            n = min(BANK, width - first)
                            for g in range(h + 1):
                                last = nc.tensor.matmul(banks[2 * h + first // BANK][0:HALF, 0:n],
                                                        order["flow"][:, g, h * HALF:(h + 1) * HALF],
                                                        tails[:, g, first:first + n], start=g == 0, stop=g == h)
                        last.then_inc(t0.handle, 1)

                @block.vector
                def _(dve):
                    for h in range(2):
                        dve.wait_ge(t0.handle, t0.after(h + 1))
                        dve.wait_ge(gather[h].handle, gather[h].after(16))
                        for first in range(0, width, BANK):
                            n = min(BANK, width - first)
                            last = dve.tensor_tensor(fixed[:, h, first:first + n], fixed[:, h, first:first + n],
                                                     banks[2 * h + first // BANK][0:HALF, 0:n], ALU.add)
                        last.then_inc(v0.handle, 1)
            once.passed(16)
            t0.passed(2)
            v0.passed(2)
            for h in range(2):
                gather[h].passed(16)
                scatter[h].passed(16)

        def attention_scores(score):
            A = 2 * UNROLL
            with ExitStack() as local:
                side = side_room(local, True, (), None)
                left = sb("left", [P, A, D], f32, local)
                right = sb("right", [P, A, D], f32, local)
                both = sb("both", [P, 4, D], f32, local)
                leaky = sb("leaky", [P, 4, D], f32, local)
                prod = sb("prod", [P, 4, D], f32, local)
                idx = sb("idx", [P, A, 2], i32, local)
                block = local.enter_context(nc.Block())
                g = sig
                got = gather + scatter

                @block.gpsimd
                def _(pool):
                    def gathers(c, s, r):
                        wait_apart(pool, apart_pool, (g["looked"].handle, g["looked"].after(c + 1)))
                        if later(c, A):
                            wait_apart(pool, apart_pool, (g["summed"].handle, g["summed"].after(c - A + 1)))
                        for rows, table, k in ((left, XL, 0), (right, XR, 1)):
                            pool.indirect_dma_start(out=rows[:, s], out_offset=None, in_=table,
                                                    in_offset=bass.IndirectOffsetOnAxis(ap=idx[:, s, k:k + 1], axis=0),
                                                    bounds_check=N_PAD - 1, oob_is_err=False).then_inc(got[s].handle, 16)
                    pipelined(pool, N_CHUNKS, [(0, gathers)], A)

                @block.scalar
                def _(act):
                    def indices(c, s, r):
                        if later(c, A):
                            wait_apart(act, apart_act, (got[s].handle, got[s].after(32 * r)))
                        act.activation(idx[:, s, 0:1], order_d["value"][:, bass.ds(c, 1)], ACT.Copy)
                        act.activation(idx[:, s, 1:2], order_d["key"][:, bass.ds(c, 1)], ACT.Copy)\
                           .then_inc(g["looked"].handle, 1)

                    def copy(c, s, r):
                        act.wait_ge(g["summed"].handle, g["summed"].after(c + 1))
                        if later(c, 4):
                            act.wait_ge(g["x_step"].handle, g["x_step"].after(c - 3))
                        act.activation(both[:, s % 4], banks[s % 4][:], ACT.Copy).then_inc(g["a_step"].handle, 1)
                    pipelined(act, N_CHUNKS, [(0, indices)] + select_act(act, order_d, side) + [(5, copy)], A)

                @block.tensor
                def _(pe):
                    def add(c, s, r):
                        pe.wait_ge(got[s].handle, got[s].after(32 * (r + 1)))
                        if later(c, 4):
                            pe.wait_ge(g["a_step"].handle, g["a_step"].after(c - 3))
                        nc.tensor.matmul(banks[s % 4][:], ident[:], left[:, s], start=True, stop=False)
                        nc.tensor.matmul(banks[s % 4][:], ident[:], right[:, s], start=False, stop=True)\
                          .then_inc(g["summed"].handle, 1)
                    pipelined(pe, N_CHUNKS, select_pe(pe, True, side) + [(0, add)], A)

                @block.vector
                def _(dve):
                    def leaky_relu(c, s, r):
                        dve.wait_ge(g["a_step"].handle, g["a_step"].after(c + 1))
                        if later(c, 4):
                            wait_apart(dve, apart_dve, (g["weighed"].handle, g["weighed"].after(c - 3)))
                        dve.scalar_tensor_tensor(leaky[:, s % 4], both[:, s % 4], 0.2, both[:, s % 4], ALU.mult, ALU.max)\
                           .then_inc(g["x_step"].handle, 1)

                    def weigh(c, s, r):
                        wait_apart(dve, apart_dve, (g["x_step"].handle, g["x_step"].after(c + 1)))
                        if later(c, 4):
                            wait_apart(dve, apart_dve, (g["y_step"].handle, g["y_step"].after(c - 3)))
                        dve.tensor_tensor(prod[:, s % 4], leaky[:, s % 4], att_row[:], ALU.mult).then_inc(g["weighed"].handle, 1)

                    def head_sums(c, s, r):
                        wait_apart(dve, apart_dve, (g["weighed"].handle, g["weighed"].after(c + 1)))
                        dve.tensor_reduce(score[:, bass.ds(c, 1), :].rearrange("p o h -> p (o h)"),
                                          prod[:, s % 4].rearrange("p (h k) -> p h k", h=HEADS), AX.X, ALU.add)\
                           .then_inc(g["y_step"].handle, 1)
                    pipelined(dve, N_CHUNKS, select_dve(dve, order_d, side) + [(6, head_sums), (5, weigh), (4, leaky_relu)], A)
            for s in range(UNROLL):
                gather[s].passed(32 * N_CHUNKS // A)
                scatter[s].passed(32 * N_CHUNKS // A)
            for name in ("looked", "summed", "a_step", "x_step", "weighed", "y_step"):
                g[name].passed(N_CHUNKS)
            side_passed(True, (), None)

        def attention_maxima(score, top, weight):
            Q = 4
            J = N_CHUNKS // Q
            W = J * P
            LANES = P // Q
            with ExitStack() as local:
                turned = sb("turned", [P, 1 + W], f32, local)
                keys = sb("keys", [P, W + 2], i32, local)
                gap = sb("gap", [P, W], f32, local)
                start = sb("start", [P, 1], f32, local)
                spread = sb("spread", [P, J, Q, LANES], f32, local)
                block = local.enter_context(nc.Block())
                g = sig
                v0, t0, a0 = g["v_step"], g["t_step"], g["a_step"]
                B = J // UNROLL
                N_SCAN = 3 + 2 * (2 + 2 * Q)

                @block.sync
                def _(sp):
                    for q in range(Q):
                        sp.dma_start(keys[q * LANES:(q + 1) * LANES, :],
                                     bass.AP(dst_list.tensor, q * W, [[0, LANES], [1, W + 2]])).then_inc(once.handle, 16)

                @block.tensor
                def _(pe):
                    pe.wait_ge(v0.handle, v0.after(2))
                    for b in range(B):
                        if b >= 2:
                            pe.wait_ge(a0.handle, a0.after(b - 1))
                        for n in range(UNROLL):
                            j = b * UNROLL + n
                            last = nc.tensor.transpose(banks[b % 2][:, n * P:(n + 1) * P],
                                                       spread[:, j].rearrange("p q l -> p (q l)"), ident[:])
                        last.then_inc(t0.handle, 1)
                    pe.wait_ge(v0.handle, v0.after(N_SCAN))
                    for b in range(B):
                        pe.wait_ge(a0.handle, a0.after(max(B, B + b - 1)))
                        for n in range(UNROLL):
                            j = b * UNROLL + n
                            last = nc.tensor.transpose(banks[b % 2][:, n * P:(n + 1) * P],
                                                       turned[:, 1 + j * P:1 + (j + 1) * P], ident[:])
                        last.then_inc(t0.handle, 1)

                @block.scalar
                def _(act):
                    for b in range(B):
                        act.wait_ge(t0.handle, t0.after(b + 1))
                        act.activation(turned[:, 1 + b * UNROLL * P:1 + (b + 1) * UNROLL * P],
                                       banks[b % 2][:], ACT.Copy)\
                           .then_inc(a0.handle, 1)
                    for b in range(B):
                        act.wait_ge(t0.handle, t0.after(B + b + 1))
                        for n in range(UNROLL):
                            j = b * UNROLL + n
                            last = act.activation(top[:].rearrange("p (q j) h -> p j q h", q=Q)[:, j],
                                                  banks[b % 2][:, n * P:(n + 1) * P]
                                                  .rearrange("p (q l) -> p q l", q=Q)[:, :, 0:HEADS], ACT.Copy)
                        last.then_inc(a0.handle, 1)
                    act.wait_ge(v0.handle, v0.after(N_SCAN + 1))
                    act.activation(weight[:], weight[:], ACT.Exp).then_inc(a0.handle, 1)

                @block.vector
                def _(dve):
                    v = Signal(v0.handle)
                    v.base = v0.base
                    lanes = lambda q: slice(q * LANES, (q + 1) * LANES)
                    chain(dve, dve.memset(spread[:], 0.0), v)
                    chain(dve, dve.tensor_copy(spread[:, :, :, 0:HEADS],
                                               score[:].rearrange("p (q j) h -> p j q h", q=Q)), v)
                    dve.wait_ge(once.handle, once.after(16 * Q))
                    chain(dve, dve.memset(turned[:, 0:1], 0.0), v)
                    for back in (False, True):
                        other = keys[:, 2:W + 2] if back else keys[:, 0:W]
                        chain(dve, dve.tensor_tensor(gap[:], keys[:, 1:W + 1], other, ALU.is_equal), v)
                        chain(dve, dve.tensor_scalar(gap[:], gap[:], -1.0, -LOW, ALU.add, ALU.mult), v)
                        if not back:
                            dve.wait_ge(a0.handle, a0.after(B))
                        for n in range(Q):
                            q = Q - 1 - n if back else n
                            prior = q + 1 if back else q - 1
                            if n == 0:
                                chain(dve, dve.memset(start[lanes(q), :], LOW), v)
                            else:
                                end = turned[lanes(prior), 1:2] if back else turned[lanes(prior), W:W + 1]
                                chain(dve, dve.tensor_copy(start[lanes(q), :], end), v)
                            line = turned[lanes(q), 1:W + 1]
                            flags = gap[lanes(q), :]
                            if back:
                                line, flags = turned[lanes(q), W:0:-1], gap[lanes(q), ::-1]
                            chain(dve, dve.tensor_tensor_scan(line, flags, line, start[lanes(q), 0:1], ALU.add, ALU.max), v)
                    dve.wait_ge(a0.handle, a0.after(2 * B))
                    dve.tensor_tensor(weight[:], score[:], top[:], ALU.subtract).then_inc(v.handle, 1)
            once.passed(16 * Q)
            v0.passed(N_SCAN + 1)
            t0.passed(2 * B)
            a0.passed(2 * B + 1)

        def attention_sums(top, weight):
            A = 2 * UNROLL
            WIDE = D + HEADS
            with ExitStack() as local:
                raw = sb("raw", [P, A, D], f32, local)
                rows_in = sb("rows_in", [P, UNROLL, 2, WIDE], f16, local)
                scaled = sb("scaled", [P, UNROLL, WIDE], f32, local)
                sums = sb("sums", [P, A, WIDE + HEADS], f32, local)
                idx = sb("idx", [P, A], i32, local)
                block = local.enter_context(nc.Block())
                g = sig
                got = gather + scatter
                put = put_sems
                pair = lambda s: psum[:, (s % UNROLL) * 2 * BANK:(s % UNROLL) * 2 * BANK + WIDE]

                @block.sync
                def _(sp):
                    def sums_store(c, s, r):
                        wait_apart(sp, apart_sp, (g["sums_out"].handle, g["sums_out"].after(c + 1)))
                        sp.dma_start(AGG_A[bass.ds(c * P, P), :], sums[:, s]).then_inc(put[s].handle, 16)
                    pipelined(sp, N_CHUNKS, [(0, sums_store)], A)
                    for s in range(A):
                        wait_apart(sp, apart_sp, (put[s].handle, put[s].after(16 * N_CHUNKS // A)))

                @block.gpsimd
                def _(pool):
                    def gathers(c, s, r):
                        if later(c, A):
                            wait_apart(pool, apart_pool, (got[s].handle, got[s].after(16 * r)))
                            wait_apart(pool, apart_pool, (g["weighed"].handle, g["weighed"].after(c - A + 1)))
                        pool.tensor_copy(idx[:, s:s + 1], order_d["value"][:, bass.ds(c, 1)]).then_inc(g["looked"].handle, 1)
                        wait_apart(pool, apart_pool, (g["looked"].handle, g["looked"].after(c + 1)))
                        pool.indirect_dma_start(out=raw[:, s], out_offset=None, in_=XL,
                                                in_offset=bass.IndirectOffsetOnAxis(ap=idx[:, s:s + 1], axis=0),
                                                bounds_check=N_PAD - 1, oob_is_err=False).then_inc(got[s].handle, 16)
                    pipelined(pool, N_CHUNKS, [(0, gathers)], A)

                @block.tensor
                def _(pe):
                    def sum_up(c, s, r):
                        pe.wait_ge(g["w_lo"].handle, g["w_lo"].after(c + 1))
                        if later(c, UNROLL):
                            pe.wait_ge(g["sums_out"].handle, g["sums_out"].after(c - UNROLL + 1))
                        sel = SEL[:, bass.ds(c, 1), :].rearrange("p o m -> p (o m)")
                        for first, n in ((0, D), (D, HEADS)):
                            for half_ in range(2):
                                last = nc.tensor.matmul(pair(s)[:, first:first + n], sel,
                                                        rows_in[:, s % UNROLL, half_, first:first + n],
                                                        start=half_ == 0, stop=half_ == 1)
                        last.then_inc(g["summed"].handle, 1)
                    pipelined(pe, N_CHUNKS, [(0, sum_up)], A)

                @block.scalar
                def _(act):
                    def high(c, s, r):
                        act.wait_ge(g["weighed"].handle, g["weighed"].after(c + 1))
                        if later(c, UNROLL):
                            act.wait_ge(g["summed"].handle, g["summed"].after(c - UNROLL + 1))
                        act.activation(rows_in[:, s % UNROLL, 0], scaled[:, s % UNROLL], ACT.Copy).then_inc(g["w_hi"].handle, 1)

                    def evict(c, s, r):
                        act.wait_ge(g["summed"].handle, g["summed"].after(c + 1))
                        if later(c, A):
                            wait_apart(act, apart_act, (put[s].handle, put[s].after(16 * r)))
                        act.activation(sums[:, s, WIDE:], top[:, bass.ds(c, 1), :].rearrange("p o h -> p (o h)"), ACT.Copy)
                        act.activation(sums[:, s, 0:WIDE], pair(s), ACT.Copy).then_inc(g["sums_out"].handle, 1)
                    pipelined(act, N_CHUNKS, [(0, high), (2, evict)], A)

                @block.vector
                def _(dve):
                    def weigh(c, s, r):
                        wait_apart(dve, apart_dve, (got[s].handle, got[s].after(16 * (r + 1))))
                        if later(c, UNROLL):
                            wait_apart(dve, apart_dve, (g["w_lo"].handle, g["w_lo"].after(c - UNROLL + 1)))
                        w = weight[:, bass.ds(c, 1), :].rearrange("p o h -> p (o h)")
                        dve.tensor_tensor(scaled[:, s % UNROLL, 0:D].rearrange("p (h k) -> p h k", h=HEADS),
                                          raw[:, s].rearrange("p (h k) -> p h k", h=HEADS),
                                          w.unsqueeze(2).to_broadcast([P, HEADS, HEAD_DIM]), ALU.mult)
                        dve.tensor_copy(scaled[:, s % UNROLL, D:], w).then_inc(g["weighed"].handle, 1)

                    def low(c, s, r):
                        dve.wait_ge(g["w_hi"].handle, g["w_hi"].after(c + 1))
                        dve.tensor_tensor(rows_in[:, s % UNROLL, 1], scaled[:, s % UNROLL], rows_in[:, s % UNROLL, 0],
                                          ALU.subtract).then_inc(g["w_lo"].handle, 1)
                    pipelined(dve, N_CHUNKS, [(0, weigh), (2, low)], A)
            for s in range(UNROLL):
                for d_ in (gather, scatter):
                    d_[s].passed(16 * N_CHUNKS // A)
            for s in range(A):
                put[s].passed(16 * N_CHUNKS // A)
            for name in ("summed", "sums_out", "looked", "weighed", "w_hi", "w_lo"):
                g[name].passed(N_CHUNKS)

        def attention_output():
            WIDE = D + 2 * HEADS
            V = 2 * UNROLL
            with ExitStack() as local:
                sums = sb("sums_in", [P, UNROLL, WIDE], f32, local)
                left = sb("left_in", [P, UNROLL, D], f32, local)
                rest = sb("rest_in", [P, UNROLL, D], f32, local)
                near = sb("near", [P, UNROLL, D], f32, local)
                far = sb("far", [P, UNROLL, D], f32, local)
                neg = sb("neg", [P, 2, D], f32, local)
                ex = sb("ex", [P, UNROLL, D], f32, local)
                pos = sb("pos", [P, UNROLL, D], f32, local)
                elu = sb("elu", [P, 2, D], f32, local)
                res = sb("res", [P, UNROLL, D], f32, local)
                place = sb("place", [P, UNROLL], i32, local)
                m = sb("m", [P, V, HEADS], f32, local)
                dif = sb("dif", [P, V, 2, HEADS], f32, local)
                e = sb("e", [P, V, 2, HEADS], f32, local)
                den = sb("den", [P, V, HEADS], f32, local)
                coef = sb("coef", [P, V, 2, HEADS], f32, local)
                block = local.enter_context(nc.Block())
                g = sig
                wide = lambda a: a.unsqueeze(2).to_broadcast([P, HEADS, HEAD_DIM])
                heads = lambda a: a.rearrange("p (h k) -> p h k", h=HEADS)

                def tiles(eng, steps):
                    pipelined(eng, N_TILES,
                              [(lag, lambda t, w, r, step=step: step(t, w % UNROLL, 2 * r + w // UNROLL, w))
                               for lag, step in steps], V)

                @block.sync
                def _(sp):
                    def load_left(t, s, r, w):
                        if later(t, UNROLL):
                            wait_apart(sp, apart_sp, (g["p_step"].handle, g["p_step"].after(t - UNROLL + 1)))
                        sp.dma_start(left[:, s], XL[bass.ds(t * P, P), :]).then_inc(load[s].handle, 16)

                    def load_rest(t, s, r, w):
                        if later(t, UNROLL):
                            wait_apart(sp, apart_sp, (g["out_lo"].handle, g["out_lo"].after(t - UNROLL + 1)))
                        sp.dma_start(rest[:, s], XH[bass.ds(t * P, P), :]).then_inc(own_in[s].handle, 16)

                    def stores(t, s, r, w):
                        wait_apart(sp, apart_sp, (g["out_lo"].handle, g["out_lo"].after(t + 1)))
                        sp.dma_start(out[bass.ds(t * P, P), :], res[:, s]).then_inc(store[s].handle, 16)
                    tiles(sp, [(0, load_left), (4, load_rest), (8, stores)])
                    for s in range(UNROLL):
                        wait_apart(sp, apart_sp, (store[s].handle, store[s].after(16 * N_TILES // UNROLL)))

                @block.gpsimd
                def _(pool):
                    def places(t, s, r, w):
                        if later(t, UNROLL):
                            wait_apart(pool, apart_pool, (gather[s].handle, gather[s].after(16 * r)))
                        pool.tensor_copy(place[:, s:s + 1], order_d["last"][:, bass.ds(t, 1)]).then_inc(g["looked"].handle, 1)

                    def gathers(t, s, r, w):
                        if later(t, UNROLL):
                            wait_apart(pool, apart_pool, (g["combined"].handle, g["combined"].after(t - UNROLL + 1)))
                        wait_apart(pool, apart_pool, (g["looked"].handle, g["looked"].after(t + 1)))
                        pool.indirect_dma_start(out=sums[:, s], out_offset=None, in_=AGG_A,
                                                in_offset=bass.IndirectOffsetOnAxis(ap=place[:, s:s + 1], axis=0),
                                                bounds_check=E_PAD, oob_is_err=False).then_inc(gather[s].handle, 16)

                    def own_share(t, s, r, w):
                        wait_apart(pool, apart_pool, (load[s].handle, load[s].after(16 * (r + 1))))
                        wait_apart(pool, apart_pool, (g["norm"].handle, g["norm"].after(t + 1)))
                        if later(t, UNROLL):
                            wait_apart(pool, apart_pool, (g["product"].handle, g["product"].after(t - UNROLL + 1)))
                        pool.tensor_tensor(out=heads(near[:, s]), in0=heads(left[:, s]), in1=wide(coef[:, w, 1]),
                                           op=ALU.mult).then_inc(g["p_step"].handle, 1)
                    tiles(pool, [(0, places), (0, gathers), (4, own_share)])

                @block.tensor
                def _(pe):
                    def mix(t, s, r, w):
                        pe.wait_ge(g["combined"].handle, g["combined"].after(t + 1))
                        pe.wait_ge(g["p_step"].handle, g["p_step"].after(t + 1))
                        if later(t, UNROLL):
                            pe.wait_ge(g["out_hi"].handle, g["out_hi"].after(t - UNROLL + 1))
                        nc.tensor.matmul(banks[s][:], ones[0:1, :], bias_out[0:1, :], start=True, stop=False)
                        nc.tensor.matmul(banks[s][:], ident[:], far[:, s], start=False, stop=False)
                        nc.tensor.matmul(banks[s][:], ident[:], near[:, s], start=False, stop=True)\
                          .then_inc(g["product"].handle, 1)
                    tiles(pe, [(5, mix)])

                @block.scalar
                def _(act):
                    def exps(t, s, r, w):
                        act.wait_ge(g["squares"].handle, g["squares"].after(t + 1))
                        act.activation(e[:, w], dif[:, w], ACT.Exp).then_inc(g["a_step"].handle, 1)

                    def elu_parts(t, s, r, w):
                        q = g["w_hi"]
                        act.wait_ge(g["product"].handle, g["product"].after(t + 1))
                        if later(t, UNROLL):
                            act.wait_ge(g["out_sum"].handle, g["out_sum"].after(t - UNROLL + 1))
                        act.activation(neg[:, s % 2], banks[s][:], ACT.Relu, scale=-1.0).then_inc(q.handle, 1)
                        act.activation(pos[:, s], banks[s][:], ACT.Relu)
                        act.wait_ge(q.handle, q.after(t + 1))
                        act.activation(ex[:, s], neg[:, s % 2], ACT.Exp, scale=-1.0).then_inc(g["out_hi"].handle, 1)
                    tiles(act, [(2, exps), (5, elu_parts)])

                @block.vector
                def _(dve):
                    def own(t):
                        return own_scores[:, bass.ds(t, 1), :].rearrange("p o h -> p (o h)")

                    def maximum(t, s, r, w):
                        dve.wait_ge(gather[s].handle, gather[s].after(16 * (r + 1)))
                        dve.tensor_tensor(m[:, w], own(t), sums[:, s, D + HEADS:], ALU.max).then_inc(g["y_step"].handle, 1)

                    def differences(t, s, r, w):
                        wait_apart(dve, apart_dve, (g["y_step"].handle, g["y_step"].after(t + 1)))
                        dve.tensor_tensor(dif[:, w, 0], sums[:, s, D + HEADS:], m[:, w], ALU.subtract)
                        dve.tensor_tensor(dif[:, w, 1], own(t), m[:, w], ALU.subtract).then_inc(g["squares"].handle, 1)

                    def scaled_denominator(t, s, r, w):
                        dve.wait_ge(g["a_step"].handle, g["a_step"].after(t + 1))
                        dve.tensor_tensor(den[:, w], e[:, w, 0], sums[:, s, D:D + HEADS], ALU.mult)\
                           .then_inc(g["ranked"].handle, 1)

                    def denominator(t, s, r, w):
                        wait_apart(dve, apart_dve, (g["ranked"].handle, g["ranked"].after(t + 1)))
                        dve.tensor_tensor(den[:, w], den[:, w], e[:, w, 1], ALU.add).then_inc(g["found"].handle, 1)

                    def guarded(t, s, r, w):
                        wait_apart(dve, apart_dve, (g["found"].handle, g["found"].after(t + 1)))
                        dve.tensor_scalar(den[:, w], den[:, w], 1e-16, None, ALU.max).then_inc(g["based"].handle, 1)

                    def inverse(t, s, r, w):
                        wait_apart(dve, apart_dve, (g["based"].handle, g["based"].after(t + 1)))
                        dve.reciprocal(den[:, w], den[:, w]).then_inc(g["turned"].handle, 1)

                    def coefficients(t, s, r, w):
                        wait_apart(dve, apart_dve, (g["turned"].handle, g["turned"].after(t + 1)))
                        dve.tensor_tensor(coef[:, w, 0], e[:, w, 0], den[:, w], ALU.mult)
                        dve.tensor_tensor(coef[:, w, 1], e[:, w, 1], den[:, w], ALU.mult).then_inc(g["norm"].handle, 1)

                    def weigh(t, s, r, w):
                        wait_apart(dve, apart_dve, (g["norm"].handle, g["norm"].after(t + 1)))
                        if later(t, UNROLL):
                            dve.wait_ge(g["product"].handle, g["product"].after(t - UNROLL + 1))
                        dve.tensor_tensor(heads(far[:, s]), heads(sums[:, s, 0:D]), wide(coef[:, w, 0]), ALU.mult)\
                           .then_inc(g["combined"].handle, 1)

                    def elu_sum(t, s, r, w):
                        dve.wait_ge(g["out_hi"].handle, g["out_hi"].after(t + 1))
                        dve.scalar_tensor_tensor(elu[:, s % 2], ex[:, s], -1.0, pos[:, s], ALU.add, ALU.add)\
                           .then_inc(g["out_sum"].handle, 1)

                    def finish(t, s, r, w):
                        wait_apart(dve, apart_dve, (g["out_sum"].handle, g["out_sum"].after(t + 1)),
                                   (own_in[s].handle, own_in[s].after(16 * (r + 1))))
                        if later(t, UNROLL):
                            wait_apart(dve, apart_dve, (store[s].handle, store[s].after(16 * r)))
                        dve.tensor_tensor(res[:, s], elu[:, s % 2], rest[:, s], ALU.add).then_inc(g["out_lo"].handle, 1)
                    tiles(dve, [(3, scaled_denominator), (2, maximum), (6, elu_sum), (3, denominator), (2, differences),
                                (3, guarded), (6, finish), (3, inverse), (3, coefficients), (3, weigh)])

        def clear_rows():
            with ExitStack() as local:
                zero = sb("zero", [1, D + 2 * HEADS], f32, local)
                block = local.enter_context(nc.Block())
                v0 = sig["v_step"]

                @block.vector
                def _(dve):
                    dve.memset(zero[:, 0:D + HEADS], 0.0).then_inc(v0.handle, 1)
                    dve.memset(zero[:, D + HEADS:], LOW).then_inc(v0.handle, 1)

                @block.sync
                def _(sp):
                    wait_apart(sp, apart_sp, (v0.handle, v0.after(2)))
                    sp.dma_start(AGG[E_PAD:E_PAD + 1, :], zero[:, 0:D]).then_inc(once.handle, 16)
                    sp.dma_start(AGG_A[E_PAD:E_PAD + 1, :], zero[:]).then_inc(once.handle, 16)
                    wait_apart(sp, apart_sp, (once.handle, once.after(32)))
            v0.passed(2)
            once.passed(32)

        def listed(a):
            return [bass.AP(a.tensor, 1 + h * HALF * P, [[P, HALF], [1, P]]) for h in range(2)]
        pairs_by_source = [bass.AP(SORTED.tensor, 2 * h * HALF * P, [[2 * P, HALF], [1, 2 * P]]) for h in range(2)]

        def row(a):
            return a.rearrange("(o n) -> o n", o=1)

        constants()
        clear_rows()
        edge_columns(listed(src_list), listed(dst_list), order_s)
        edge_columns(listed(dst_list), listed(src_list), order_d)

        split_weights([(Ws_neigh[0], w_out, False)], [])
        for layer in range(3):
            own_weights = dict(jobs=[(Ws_self[layer], w_own, False)], rows_=[(bs[layer:layer + 1, :], bias_own)])
            if layer == 0:
                dense(x_in=x, ht=True, **own_weights)
            else:
                dense(own=U, order=order_d, norm=False, ht=True, **own_weights)
            aggregate(order_d, own=True, jobs=[(Ws_neigh[layer + 1], w_out, False)] if layer < 2 else [(W1, w_out, True)],
                      rows_=[(row(b1), bias_out)] if layer == 2 else [], select=layer == 0,
                      count=((order_d, True), (order_s, False)) if layer == 0 else (), sort=order_s if layer == 1 else None)
            join_chunks(AGG, D, order_d)
        dense(x_in=x, own=U, order=order_d, log_map=True, x_out=X1)
        aggregate(order_d, jobs=[(wn, w_out, False)])
        join_chunks(AGG, D, order_d)
        dense(x_in=X1, order=order_d, exp_map=True, x_out=X2, ht=True, jobs=[(wc, w_own, False)],
              rows_=[(row(b2), bias_own)])
        edge_columns(pairs_by_source, None, order_s)
        aggregate(order_s, own=True, select=True, jobs=[(W_l, w_out, False), (W_r, w_out2, False)],
                  rows_=[(row(att.rearrange("h k -> (h k)")), att_row), (row(b3), bias_out)])
        join_chunks(AGG, D, order_s)
        dense(x_in=X2, own=U, order=order_s, attention=True)
        score = sb("score", [P, N_CHUNKS, HEADS], f32)
        top = sb("top", [P, N_CHUNKS, HEADS], f32)
        weight = sb("weight", [P, N_CHUNKS, HEADS], f32)
        attention_scores(score)
        attention_maxima(score, top, weight)
        attention_sums(top, weight)
        join_chunks(AGG_A, D + HEADS, order_d)
        attention_output()


_INS = ["x", "src", "dst", "L0_gnn_Ws_self", "L0_gnn_Ws_neigh", "L0_gnn_bs", "L1_gnn_W", "L1_gnn_b", "L2_gnn_wc",
        "L2_gnn_wn", "L2_gnn_bias", "L3_gnn_W_l", "L3_gnn_W_r", "L3_gnn_att", "L3_gnn_bias"]


def kernel(**inputs):
    import numpy as np
    import concourse.bacc as bacc
    from concourse.bass_utils import run_bass_kernel_spmd

    nc = bacc.Bacc("TRN2", target_bir_lowering=False, num_devices=1)
    arrays, args = {}, []
    for name in _INS:
        a = np.ascontiguousarray(inputs[name])
        if name == "x":
            a = np.concatenate([a, np.zeros((N_PAD - N_NODES, D), a.dtype)])
        if name in ("src", "dst"):
            extra = np.minimum(N_NODES + np.arange(E_PAD - N_EDGES), N_PAD - 1).astype(a.dtype)
            edge = np.full((1,), -1, a.dtype)
            a = np.concatenate([edge, a, extra, edge])
        arrays[f"in_{name}"] = a
        args.append(nc.dram_tensor(f"in_{name}", a.shape, mybir.dt.from_np(a.dtype), kind="ExternalInput").ap())
    out = nc.dram_tensor("out_0", (N_PAD, D), mybir.dt.float32, kind="ExternalOutput").ap()

    def scratch(name, shape, dtype):
        return nc.dram_tensor(name, shape, dtype, kind="Internal").ap()

    gnn_program(nc, *args, out, scratch)
    r = run_bass_kernel_spmd(nc, [arrays], core_ids=[0])
    return r.results[0]["out_0"][:N_NODES]
```
